# Optimizing a Trainium2 kernel written in Bass

```python
import numpy as np
import jax
import jax.numpy as jnp

def _softmax(x, axis=-1):
    return jax.nn.softmax(x, axis=axis)

def _gelu(x):
    return jax.nn.gelu(x, approximate=True)

def _silu(x):
    return jax.nn.silu(x)

def _sigmoid(x):
    return jax.nn.sigmoid(x)

def _layernorm(x, axis=-1, eps=1e-05):
    m = jnp.mean(x, axis=axis, keepdims=True)
    v = jnp.var(x, axis=axis, keepdims=True)
    return (x - m) / jnp.sqrt(v + eps)

def _scatter_add(tgt, idx, src, axis=0):
    return tgt.at[idx].add(src)

def _segment_sum(src, seg, n):
    return jax.ops.segment_sum(src, seg, n)
kernel_name = 'mk_adaln_d1_jaxref_r8_f3269f'

def setup_inputs(seed: int=0):
    np.random.seed(seed)
    _w = jnp.asarray

    def _L0_attn_setup():
        import jax, jax.numpy as jnp
        import numpy as np
        MODEL_DIM = 128
        D_STATE = 16
        EXPAND = 2
        D_CONV = 4
        D_INNER = MODEL_DIM * EXPAND
        B, L = (4, 128)

        def _causal_depthwise_conv(x_bdl, conv_w, conv_b):
            kern = conv_w[:, None, :]
            out = jax.lax.conv_general_dilated(x_bdl, kern, window_strides=(1,), padding=[(D_CONV - 1, 0)], dimension_numbers=('NCH', 'OIH', 'NCH'), feature_group_count=D_INNER)
            return out + conv_b[None, :, None]
        key = jax.random.key(seed)
        ks = jax.random.split(key, 8)
        s_in = 1.0 / np.sqrt(MODEL_DIM)
        s_inner = 1.0 / np.sqrt(D_INNER)
        x = jax.random.normal(ks[0], (B, L, MODEL_DIM), dtype=jnp.float32)
        W_in = jax.random.normal(ks[1], (MODEL_DIM, 2 * D_INNER), dtype=jnp.float32) * s_in
        conv_w = jax.random.normal(ks[2], (D_INNER, D_CONV), dtype=jnp.float32) * (1.0 / np.sqrt(D_CONV))
        conv_b = jnp.zeros((D_INNER,), dtype=jnp.float32)
        W_x = jax.random.normal(ks[3], (D_INNER, 2 * D_STATE + 1), dtype=jnp.float32) * s_inner
        dt_w = jax.random.normal(ks[4], (D_INNER,), dtype=jnp.float32)
        dt_b = jax.random.normal(ks[5], (D_INNER,), dtype=jnp.float32) * 0.1
        A_log = jnp.broadcast_to(jnp.log(jnp.arange(1, D_STATE + 1, dtype=jnp.float32)), (D_INNER, D_STATE))
        D = jnp.ones((D_INNER,), dtype=jnp.float32)
        W_out = jax.random.normal(ks[6], (D_INNER, MODEL_DIM), dtype=jnp.float32) * s_inner
        return {'x': x, 'W_in': W_in, 'conv_w': conv_w, 'conv_b': conv_b, 'W_x': W_x, 'dt_w': dt_w, 'dt_b': dt_b, 'A_log': A_log, 'D': D, 'W_out': W_out}
    _L0_attn_in = _L0_attn_setup()

    def _L0_ffn_setup():
        import jax, jax.numpy as jnp
        import numpy as np
        B, S, D_IN, D_OUT, E, GATE_K, TOP_K = (4, 1024, 128, 128, 8, 64, 2)

        def _gate(x, Vg):
            T = x.shape[0]
            xe = jnp.einsum('ti,eir->ter', x, Vg)
            proj = jnp.einsum('ter,eir->tei', xe, Vg)
            residuals = jnp.linalg.norm(x[:, None, :] - proj, axis=-1)
            rw = jax.nn.softmax(-residuals, axis=1)
            thr = 1.0 / E
            mask = rw > thr
            rows = jnp.arange(T)[:, None]
            top1_idx = jnp.argmax(rw, axis=1, keepdims=True)
            top1_mask = jnp.zeros_like(mask).at[rows, top1_idx].set(True)
            mask = jnp.where(jnp.any(mask), mask, top1_mask)
            if TOP_K < E:
                _, topi = jax.lax.top_k(rw, TOP_K)
                topk_mask = jnp.zeros_like(mask).at[rows, topi].set(True)
                mask = mask & topk_mask
            fw = rw * mask.astype(rw.dtype)
            sw = fw.sum(axis=1, keepdims=True)
            sw = jnp.where(sw == 0, jnp.ones_like(sw), sw)
            return fw / sw
        key = jax.random.key(seed)
        ks = jax.random.split(key, 6)
        return {'hidden_states': jax.random.normal(ks[0], (B, S, D_IN), dtype=jnp.float32), 'Wp': jax.random.normal(ks[1], (D_OUT, D_IN), dtype=jnp.float32) * 0.02, 'bp': jax.random.normal(ks[2], (D_OUT,), dtype=jnp.float32) * 0.02, 'We': jax.random.normal(ks[3], (E, D_OUT, D_IN), dtype=jnp.float32) * 0.02, 'be': jax.random.normal(ks[4], (E, D_OUT), dtype=jnp.float32) * 0.02, 'Vg': jax.random.normal(ks[5], (E, D_IN, GATE_K), dtype=jnp.float32) * 0.05}
    _L0_ffn_in = _L0_ffn_setup()
    _L0_c = _w((lambda *s: np.random.randn(*s).astype(np.float32) * 0.05)(4, 128))
    _L0_wmod = _w((lambda *s: np.random.randn(*s).astype(np.float32) * 0.05)(128, 6 * 128) * 128 ** (-0.5))
    _d = {'L0_attn_x': _L0_attn_in['x'], 'L0_attn_W_in': _L0_attn_in['W_in'], 'L0_attn_conv_w': _L0_attn_in['conv_w'], 'L0_attn_conv_b': _L0_attn_in['conv_b'], 'L0_attn_W_x': _L0_attn_in['W_x'], 'L0_attn_dt_w': _L0_attn_in['dt_w'], 'L0_attn_dt_b': _L0_attn_in['dt_b'], 'L0_attn_A_log': _L0_attn_in['A_log'], 'L0_attn_D': _L0_attn_in['D'], 'L0_attn_W_out': _L0_attn_in['W_out'], 'L0_ffn_Wp': _L0_ffn_in['Wp'], 'L0_ffn_bp': _L0_ffn_in['bp'], 'L0_ffn_We': _L0_ffn_in['We'], 'L0_ffn_be': _L0_ffn_in['be'], 'L0_ffn_Vg': _L0_ffn_in['Vg'], 'L0_c': _L0_c, 'L0_wmod': _L0_wmod}
    _x0 = _d['L0_attn_x']
    _d['L0_attn_x'] = jax.random.normal(jax.random.fold_in(jax.random.key(seed), 1), (4, 512, 128), dtype=_x0.dtype)
    del _x0
    return _d

def reference(L0_attn_x, L0_attn_W_in, L0_attn_conv_w, L0_attn_conv_b, L0_attn_W_x, L0_attn_dt_w, L0_attn_dt_b, L0_attn_A_log, L0_attn_D, L0_attn_W_out, L0_ffn_Wp, L0_ffn_bp, L0_ffn_We, L0_ffn_be, L0_ffn_Vg, L0_c, L0_wmod):

    def _L0_attn_ref(x, W_in, conv_w, conv_b, W_x, dt_w, dt_b, A_log, D, W_out):
        import jax, jax.numpy as jnp
        import numpy as np
        MODEL_DIM = 128
        D_STATE = 16
        EXPAND = 2
        D_CONV = 4
        D_INNER = MODEL_DIM * EXPAND
        B, L = (4, 128)

        def _causal_depthwise_conv(x_bdl, conv_w, conv_b):
            kern = conv_w[:, None, :]
            out = jax.lax.conv_general_dilated(x_bdl, kern, window_strides=(1,), padding=[(D_CONV - 1, 0)], dimension_numbers=('NCH', 'OIH', 'NCH'), feature_group_count=D_INNER)
            return out + conv_b[None, :, None]
        xz = x @ W_in
        x_main, z = jnp.split(xz, 2, axis=-1)
        xc = _causal_depthwise_conv(jnp.swapaxes(x_main, 1, 2), conv_w, conv_b)
        x_conv = jax.nn.silu(jnp.swapaxes(xc, 1, 2))
        ssm = x_conv @ W_x
        delta_raw = ssm[..., 0:1]
        B_in = ssm[..., 1:1 + D_STATE]
        C_in = ssm[..., 1 + D_STATE:]
        delta = jax.nn.softplus(delta_raw * dt_w + dt_b)
        A = -jnp.exp(A_log)
        dA = jnp.exp(delta[..., None] * A)
        dBx = (delta * x_conv)[..., None] * B_in[:, :, None, :]

        def step(h, inp):
            dA_t, dBx_t, C_t = inp
            h = dA_t * h + dBx_t
            y_t = jnp.einsum('bdn,bn->bd', h, C_t)
            return (h, y_t)
        h0 = jnp.zeros((x.shape[0], D_INNER, D_STATE), dtype=x.dtype)
        xs = (jnp.swapaxes(dA, 0, 1), jnp.swapaxes(dBx, 0, 1), jnp.swapaxes(C_in, 0, 1))
        _, ys = jax.lax.scan(step, h0, xs)
        y = jnp.swapaxes(ys, 0, 1)
        y = y + D * x_conv
        y = y * jax.nn.silu(z)
        return y @ W_out

    def _L0_ffn_ref(hidden_states, Wp, bp, We, be, Vg):
        import jax, jax.numpy as jnp
        import numpy as np
        B, S, D_IN, D_OUT, E, GATE_K, TOP_K = (4, 1024, 128, 128, 8, 64, 2)

        def _gate(x, Vg):
            T = x.shape[0]
            xe = jnp.einsum('ti,eir->ter', x, Vg)
            proj = jnp.einsum('ter,eir->tei', xe, Vg)
            residuals = jnp.linalg.norm(x[:, None, :] - proj, axis=-1)
            rw = jax.nn.softmax(-residuals, axis=1)
            thr = 1.0 / E
            mask = rw > thr
            rows = jnp.arange(T)[:, None]
            top1_idx = jnp.argmax(rw, axis=1, keepdims=True)
            top1_mask = jnp.zeros_like(mask).at[rows, top1_idx].set(True)
            mask = jnp.where(jnp.any(mask), mask, top1_mask)
            if TOP_K < E:
                _, topi = jax.lax.top_k(rw, TOP_K)
                topk_mask = jnp.zeros_like(mask).at[rows, topi].set(True)
                mask = mask & topk_mask
            fw = rw * mask.astype(rw.dtype)
            sw = fw.sum(axis=1, keepdims=True)
            sw = jnp.where(sw == 0, jnp.ones_like(sw), sw)
            return fw / sw
        in_shape = hidden_states.shape
        pretrained_out = jnp.einsum('bsi,oi->bso', hidden_states, Wp) + bp
        x = hidden_states.reshape(-1, in_shape[-1])
        w = _gate(x, Vg)
        expert_out = jnp.einsum('ti,eoi->teo', x, We) + be[None]
        final = jnp.einsum('te,teo->to', w, expert_out)
        final = final.reshape(*in_shape[:-1], We.shape[1])
        return pretrained_out + final
    x = L0_attn_x
    mod = (_silu(L0_c) @ L0_wmod).reshape(L0_c.shape[0], 6, 1, -1)
    sa, ca, ga, sb, cb, gb = (mod[:, 0], mod[:, 1], mod[:, 2], mod[:, 3], mod[:, 4], mod[:, 5])
    ga = (2 * (ga >= 0) - 1) * jnp.maximum(jnp.abs(ga), 0.25)
    gb = (2 * (gb >= 0) - 1) * jnp.maximum(jnp.abs(gb), 0.25)
    h = _layernorm(x, axis=-1) * (1 + ca) + sa
    x = x + ga * _L0_attn_ref(h, L0_attn_W_in, L0_attn_conv_w, L0_attn_conv_b, L0_attn_W_x, L0_attn_dt_w, L0_attn_dt_b, L0_attn_A_log, L0_attn_D, L0_attn_W_out)
    h = _layernorm(x, axis=-1) * (1 + cb) + sb
    x = x + gb * _L0_ffn_ref(h, L0_ffn_Wp, L0_ffn_bp, L0_ffn_We, L0_ffn_be, L0_ffn_Vg)
    return x

_drawn_inputs = setup_inputs


def setup_inputs(seed=0):
    import zlib

    import numpy as np

    out = dict(_drawn_inputs(seed))
    spreads = {'L0_attn_conv_b': (0.0, 0.358), 'L0_attn_D': (1.0, 0.6)}
    factors = {'L0_attn_dt_b': 6.884, 'L0_attn_A_log': 2.917, 'L0_ffn_bp': 8.0, 'L0_ffn_be': 8.0}
    for name, (base, spread) in spreads.items():
        noise = np.random.default_rng([zlib.crc32(name.encode()), seed]).standard_normal(out[name].shape)
        drawn = base * np.exp(spread * noise) if base else spread * noise
        out[name] = jnp.asarray(drawn.astype(out[name].dtype))
    for name, factor in factors.items():
        out[name] = (out[name] * factor).astype(out[name].dtype)
    return out
```

```python
from contextlib import ExitStack

import numpy as np

import concourse.bass as bass
from concourse import mybir

ALU = mybir.AluOpType
ACT = mybir.ActivationFunctionType
AX = mybir.AxisListType.X
F32 = mybir.dt.float32
BF16 = mybir.dt.bfloat16

P = 128
NB = 4
T = 512
NT = T // P
DI = 256
NH = DI // P
NS = 16
KC = 4
NE = 8
RV = 64
NP3 = 3
NPART = NS * NP3 + NP3
C_AT = 64
EPS = 1e-5

SMALL = {"selE": NE, "conv_b": NH, "dt_w": NH, "dt_b": NH, "D": NH, "A_log": NH * NS, "conv_w": NH * KC, "low": 8, "sel": NS + 1, "tri": NE * NE}

EARLY = ["vec_ln1", "act_rstd1", "vec_xn1", "pe_xT", "act_hT"]
HEAD = EARLY + ["pe_x0", "pe_x1", "act_x0", "act_x1", "vec_c0", "act_t0", "vec_x0", "vec_c1", "act_t1", "vec_x1",
                "pe_ssm", "act_hi", "vec_u", "act_mid", "sp_c", "vec_parts", "pe_delta", "act_soft", "vec_soft",
                "sum_delta"]
LEAD = {"vec_ln1": -6, "act_rstd1": -5, "vec_xn1": -4, "pe_xT": -2, "act_hT": -2,
        "pe_x0": 0, "act_x0": 0, "vec_c0": 0.5, "pe_x1": 0.6, "act_x1": 0.6, "act_t0": 1, "vec_c1": 1, "pe_z0": 1,
        "vec_x0": 2, "act_t1": 2, "act_z0": 2, "vec_z0": 2, "vec_x1": 2, "pe_z1": 3, "act_z1": 3, "vec_z1": 3,
        "pe_ssm": 4, "act_hi": 4, "sp_c": 4, "vec_u": 5, "act_mid": 6, "vec_parts": 7, "pe_delta": 9, "act_soft": 9,
        "vec_soft": 10, "sum_delta": 11}
LAG = {"vec_y": 1, "pool_g": 2, "pe_wout": 5.4, "vec_x2": 5.6, "act_rstd2": 6.6, "vec_xn2": 7.4, "pe_xT2": 9, "act_h2T": 9,
       "pe_r0": 10, "act_r0": 10, "pe_r1": 11, "act_r1": 11, "pe_r2": 12, "act_r2": 12, "pe_r3": 13, "act_r3": 13,
       "vec_clamp": 14, "act_sqrt": 15, "vec_gate1": 16, "act_gexp": 17, "vec_gate2": 18, "pe_wT": 20, "act_wT": 20,
       "pe_o": 21}
for _e in range(NE):
    LAG |= {f"pe_b{_e}": 21 + _e, f"vec_h{_e}": 21 + _e}
    if _e >= 2:
        LAG[f"pe_a{_e - 2}"] = 21 + _e
LAG |= {f"pe_a{NE - 2}": 29, f"pe_a{NE - 1}": 30, "vec_out": 31, "pool_out": 31, "sp_out": 31}
FIT = [0.95, 0.75, 0.48]
SETUP = {"pe_z0": 0, "pe_z1": 0, "act_z0": 0, "vec_z0": 0, "act_z1": 0, "vec_z1": 0, "pe_gate0": 4, "pe_gate1": 4, "vec_gates": 5, "pool_wog": 6, "pe_V0": 8, "pe_V1": 8, "vec_V": 9}


def plan():
    steps = [[] for _ in range(NB * NS)]
    for name, n in SETUP.items():
        steps[n].append((name, 0))
    for q in range(NB - 1):
        fit = FIT[q]
        for name, n in LAG.items():
            steps[NS * (q + 1) + int(n * fit)].append((name, q))
    for q in range(1, NB):
        for name, n in LEAD.items():
            steps[max(NS * (q - 1) + int(n), 0)].append((name, q))
    order = [("modulate", 0)] + [(name, 0) for name in HEAD] + [("first", 0)]
    for s, pieces in enumerate(steps):
        order += [("scan", s), *pieces]
    return order + [("last", 0)] + [(name, NB - 1) for name in LAG]


C_AHEAD = 4
AHEAD = 2
NG = 3
W9_AT = 32


def bank_plan(order, shared_banks):
    uses, turn = {}, []
    for name, q in order:
        if name in shared_banks:
            count, sem, per, first = shared_banks[name]
            for i in range(count):
                k = len(turn)
                before = turn[k - NG] if k >= NG else None
                uses.setdefault((name, q), []).append((k % NG, before))
                turn.append((sem, per * q + first + i))
    return uses


def adaln_mamba_experts(nc, x, W_in, smalls, W_x, W_out, We_Wp, be_bp, VgT, cT, wmod, eye, C_dram, out):
    order = plan()
    with ExitStack() as ctx:
        def sb(name, shape, dt=F32):
            return ctx.enter_context(nc.sbuf_tensor(name, shape, dt))

        def ps(name, shape):
            return ctx.enter_context(nc.psum_tensor(name, shape, F32))

        ND, NX, NHB, NPB, NC, NW = 4, 3, 3, 3, 5, 3
        def sem(name):
            return ctx.enter_context(nc.semaphore(name))

        x_in = [sem(f"x{b}_in") for b in range(NB)]
        C_in = [sem(f"C{i}_in") for i in range(NC)]
        bn_ready, stats_ready, lnv_ready, rstd_ready, xn_ready = (
            [sem(f"{name}{i}") for i in range(2)] for name in ("bn_ready", "stats_ready", "lnv_ready", "rstd_ready", "xn_ready"))
        (c_in, wm_in, ident_in, small_in, win_in, wx_in, wo_in, v_in, w9_in, b9_in) = map(sem, (
            "c_in", "wm_in", "ident_in", "small_in", "win_in", "wx_in", "wo_in", "v_in", "w9_in",
            "b9_in"))
        (w41_clear, w41_one, reset_ready, sel_ready, Woh_ready, convbh_ready, taps_ready, Ae_ready,
         A_ready, V_done, M_ready) = map(sem, (
            "w41_clear", "w41_one", "reset_ready", "sel_ready", "Woh_ready", "convbh_ready",
            "taps_ready", "Ae_ready", "A_ready", "V_done", "M_ready"))
        (cth_ready, ch_ready, csig_ready, cs_ready, cb_ready, mod_done, mod_ready, gate_done,
         gates_read, gsgn_twice, gsgn_ready, gabs_ready, gates_ready, Wog_ready) = map(sem, (
            "cth_ready", "ch_ready", "csig_ready", "cs_ready", "cb_ready", "mod_done", "mod_ready",
            "gate_done", "gates_read", "gsgn_twice", "gsgn_ready", "gabs_ready", "gates_ready",
            "Wog_ready"))
        (xT_done, hT_ready, x_done, z_done, xin_ready, tap_done, conv_done, xth_ready, xconv_ready,
         zth_ready, zgate_ready) = map(sem, (
            "xT_done", "hT_ready", "x_done", "z_done", "xin_ready", "tap_done", "conv_done",
            "xth_ready", "xconv_ready", "zth_ready", "zgate_ready"))
        (ssm_done, C_rows_ready, C_stored, hi_ready, rest_ready, mid_ready, parts_ready, delta_done,
         dabs_ready, softin_half, softin_ready, dexp_ready, dw1_ready, dcor_ready, dlog_ready,
         dsum_ready, delta_ready, dx_ready) = map(sem, (
            "ssm_done", "C_rows_ready", "C_stored", "hi_ready", "rest_ready", "mid_ready",
            "parts_ready", "delta_done", "dabs_ready", "softin_half", "softin_ready", "dexp_ready",
            "dw1_ready", "dcor_ready", "dlog_ready", "dsum_ready", "delta_ready", "dx_ready"))
        (Bps_ready, dA_half, dA_ready, dBx_ready, scan_done, prod_ready, nsum_done) = map(sem, (
            "Bps_ready", "dA_half", "dA_ready", "dBx_ready", "scan_done", "prod_ready",
            "nsum_done"))
        (y_ready, yg_ready, wout_done, x2_ready, xT2_done, h2T_ready) = map(sem, (
            "y_ready", "yg_ready", "wout_done", "x2_ready", "xT2_done", "h2T_ready"))
        (r_done, sq_some, sq_done, clamp_ready, lr_ready, res_ready, rmin_ready, gd_ready, ge_ready,
         lt_ready, eq_ready, eql_ready, cnt_ready, rank_ready, gs_ready, gr_ready, rw_ready, msk_ready,
         keep_ready, fw_ready, sw_ready, swz_ready, rsw_ready, w_ready, w_hi_ready, w_part0,
         w_rest_ready, w_mid_ready, w_part1, w_parts_ready, wT_done, wTp_ready, wT_ready) = map(sem, (
            "r_done", "sq_some", "sq_done", "clamp_ready", "lr_ready", "res_ready", "rmin_ready",
            "gd_ready", "ge_ready", "lt_ready", "eq_ready", "eql_ready", "cnt_ready", "rank_ready",
            "gs_ready", "gr_ready", "rw_ready", "msk_ready", "keep_ready", "fw_ready", "sw_ready",
            "swz_ready", "rsw_ready", "w_ready", "w_hi_ready", "w_part0", "w_rest_ready",
            "w_mid_ready", "w_part1", "w_parts_ready", "wT_done", "wTp_ready", "wT_ready"))
        (o_start, b_done, wh_ready, a_done, acc_ready, out_ready, stored) = map(sem, (
            "o_start", "b_done", "wh_ready", "a_done", "acc_ready", "out_ready", "stored"))
        normT_done = [xT_done, xT2_done]

        shared_banks = {
            "pe_xT": (1, hT_ready, 1, 1), "pe_x0": (1, conv_done, 2, 1), "pe_x1": (1, conv_done, 2, 2),
            "pe_z0": (1, zgate_ready, 2, 1), "pe_z1": (1, zgate_ready, 2, 2), "pe_ssm": (1, rest_ready, 1, 1),
            "pe_delta": (1, softin_ready, 1, 1), "pe_wout": (1, x2_ready, 1, 1), "pe_xT2": (1, h2T_ready, 1, 1),
            "pe_wT": (1, wT_ready, 1, 1), **{f"pe_b{e}": (1, wh_ready, NE, e + 1) for e in range(NE)},
            "pe_gate0": (1, gates_read, 2, 1), "pe_gate1": (1, gates_read, 2, 2),
            "pe_V0": (1, M_ready, 2, 1), "pe_V1": (1, M_ready, 2, 2),
            **{f"pe_r{j}": (2, sq_done, 2 * NT, 2 * j + 1) for j in range(NT)},
        }
        banks = bank_plan(order, shared_banks)

        Win = sb("Win", [P, 2 * DI])
        small = sb("small", [P, sum(SMALL.values())])
        part_of, at = {}, 0
        for name, width in SMALL.items():
            part_of[name] = small[:, at:at + width]
            at += width
        convb, dtw, dtb, Dsk = (part_of[k] for k in ("conv_b", "dt_w", "dt_b", "D"))
        Al = part_of["A_log"].rearrange("p (h n) -> p h n", h=NH)
        low, selc = part_of["low"], part_of["sel"]
        tri = part_of["tri"].rearrange("p (e f) -> p e f", e=NE)
        conv_w = part_of["conv_w"].rearrange("p (h k) -> p h k", h=NH)
        convbh = sb("convbh", [P, NH])
        taps = sb("taps", [P, NH, KC])
        Wx = sb("Wx", [P, NH, C_AT + NS])
        Ae = sb("Ae", [P, NH, NS])
        A = sb("A", [P, NH, NS])
        Wo = sb("Wo", [P, NH, P])
        Wog = sb("Wog", [P, NB, NH, P])
        W9 = sb("W9", [P, (NE + 1) * P])
        b9 = sb("b9", [W9_AT + NE + 1, P])
        V = sb("V", [RV, NE, P])
        M = sb("M", [P, NE, P])
        c_sb = sb("c_sb", [P, NB])
        c_th = sb("c_th", [P, NB])
        c_h = sb("c_h", [P, NB])
        c_s = sb("c_s", [P, NB])
        c_b = sb("c_b", [P, NB, P])
        wm = sb("wm", [P, 6, P])
        mod = sb("mod", [P, 4, NB])
        mod1 = sb("mod1", [P, 4, NB])
        gate = sb("gate", [P, NB, 2, P])
        ident = sb("ident", [P, P])
        sel = sb("sel", [P, NS + 1], BF16)
        selE = sb("selE", [P, NE], BF16)
        x_sb = sb("x_sb", [P, NB, NT, P])
        stats = sb("stats", [P, 2, NT, 6])
        mv = sb("mv", [P, 2, NT, 2])
        lnv = sb("lnv", [P, 2, NT])
        rstd = sb("rstd", [P, 2, NT])
        xn = sb("xn", [P, 2, NT, P])
        hT = sb("hT", [P, T])
        h2T = sb("h2T", [P, NB, T])
        xch = sb("xch", [P, NH, T])
        th = sb("th", [P, NH, T])
        xconv = sb("xconv", [P, 2, NH, T])
        zz = sb("zz", [P, 2, NH, T])
        hi = sb("hi", [P, T], BF16)
        rest = sb("rest", [P, T])
        mid = sb("mid", [P, T], BF16)
        parts = sb("parts", [P, 2, T], BF16)
        dexp = sb("dexp", [P, NH, T])
        drel = sb("drel", [P, NH, T])
        dlog = sb("dlog", [P, NH, T])
        dw1 = sb("dw1", [P, NH, T])
        delta = sb("delta", [P, 2, NH, T])
        dx = sb("dx", [P, 2, NH, T])
        dA = sb("dA", [P, ND, NH, T])
        dBx = sb("dBx", [P, NX, NH, T])
        hs = sb("hs", [P, NHB, NH, T])
        prod = sb("prod", [P, NPB, NH, T])
        C_rows = sb("C_rows", [C_AT + NS, T])
        C_sb = sb("C_sb", [P, NC, T])
        y2 = sb("y2", [P, NH, T])
        sqj = sb("sqj", [P, 2, 4, P], BF16)
        r2 = sb("r2", [P, NB, NT, NE])
        r2c = sb("r2c", [P, NT, NE])
        lr = sb("lr", [P, NT, NE])
        res = sb("res", [P, NT, NE])
        rmin = sb("rmin", [P, NT])
        gd = sb("gd", [P, NT, NE])
        ge = sb("ge", [P, NT, NE])
        gs = sb("gs", [P, NT])
        gr = sb("gr", [P, NT])
        rw = sb("rw", [P, NT, NE])
        msk = sb("msk", [P, NT, NE])
        lt = sb("lt", [P, NT, NE, NE])
        eq = sb("eq", [P, NT, NE, NE])
        rank = sb("rank", [P, NT, NE])
        keep = sb("keep", [P, NT, NE])
        fw = sb("fw", [P, NT, NE])
        sw = sb("sw", [P, NT])
        swz = sb("swz", [P, NT])
        rsw = sb("rsw", [P, NT])
        w_hi = sb("w_hi", [P, NT, NE], BF16)
        w_rest = sb("w_rest", [P, NT, NE])
        w_mid = sb("w_mid", [P, NT, NE], BF16)
        w41 = sb("w41", [P, NT, W9_AT + NE + 1])
        wTp = sb("wTp", [NP3 * NE, T], BF16)
        wT9 = sb("wT9", [W9_AT + NE + 1, T])
        wh = sb("wh", [P, NW, T])
        graw = sb("graw", [P, 4 * P])
        gsgn = sb("gsgn", [P, 4 * P])
        acc = sb("acc", [P, NT, P])

        Bps = [ps(f"Bps{i}", [P, T]) for i in range(2)]
        Yps = ps("Yps", [P, NH, T])
        Ops = ps("Ops", [P, T])
        G = [ps(f"G{i}", [P, T]) for i in range(NG)]
        block = ctx.enter_context(nc.Block())

        last_s = NB * NS - 1

        loads = [
            (x_sb[:, 0], x[0].rearrange("(j p) i -> p j i", p=P), x_in[0]), (c_sb[:, :], cT, c_in),
            (wm[:, :, :], wmod.rearrange("k (m n) -> k m n", m=6), wm_in), (ident[:, :], eye, ident_in),
            (small[:, :], smalls, small_in), (Win[:, :], W_in, win_in), (Wx[:, :, :], W_x, wx_in),
            (x_sb[:, 1], x[1].rearrange("(j p) i -> p j i", p=P), x_in[1]),
            (Wo[:, :, :], W_out, wo_in), (V[:, :, :], VgT, v_in),
            (W9[:, :], We_Wp, w9_in), (b9[W9_AT:, :], be_bp, b9_in),
            (x_sb[:, 2], x[2].rearrange("(j p) i -> p j i", p=P), x_in[2]),
            (x_sb[:, 3], x[3].rearrange("(j p) i -> p j i", p=P), x_in[3]),
        ]
        @block.sync
        def _(sp):
            for dst, src, landed in loads:
                sp.dma_start(dst, src).then_inc(landed, 16)
            def load_C(s):
                sp.wait_ge(C_stored, 16 * (s // NS + 1))
                if s >= NC:
                    sp.wait_ge(prod_ready, s - NC + 1)
                sp.dma_start(C_sb[:, s % NC], C_dram[s // NS, s % NS].partition_broadcast(P)
                             ).then_inc(C_in[s % NC], 16)

            for name, q in order:
                if name == "sp_c":
                    sp.wait_ge(C_rows_ready, q + 1)
                    sp.dma_start(C_dram[q], C_rows[C_AT:, :]).then_inc(C_stored, 16)
                elif name == "first":
                    for s in range(C_AHEAD):
                        load_C(s)
                elif name == "scan":
                    if q + C_AHEAD <= last_s:
                        load_C(q + C_AHEAD)
                elif name == "sp_out":
                    sp.wait_ge(out_ready, q + 1)
                    sp.dma_start(out[q].rearrange("(j p) i -> p j i", p=P), x_sb[:, q]).then_inc(stored, 16)
            sp.wait_ge(stored, 16 * NB)

        def sum_delta(eng, q):
            eng.wait_ge(dcor_ready, q + 1)
            eng.wait_ge(dlog_ready, q + 1)
            eng.tensor_tensor(dlog[:, :, :], dlog[:, :, :], dw1[:, :, :], ALU.subtract).then_inc(dsum_ready, 1)
            eng.wait_ge(dsum_ready, q + 1)
            if q >= 2:
                eng.wait_ge(dA_ready, NS * (q - 1))
            eng.tensor_tensor(delta[:, q % 2], dlog[:, :, :], drel[:, :, :], ALU.add).then_inc(delta_ready, 1)
            eng.wait_ge(delta_ready, q + 1)
            eng.wait_ge(xconv_ready, 2 * (q + 1))
            if q >= 2:
                eng.wait_ge(dBx_ready, NS * (q - 1))
            eng.tensor_tensor(dx[:, q % 2], delta[:, q % 2], xconv[:, q % 2], ALU.mult).then_inc(dx_ready, 1)

        @block.gpsimd
        def _(pool):
            pool.memset(w41[:, :, :], 0.0).then_inc(w41_clear, 1)
            pool.wait_ge(w41_clear, 1)
            pool.memset(w41[:, :, W9_AT + NE:], 1.0).then_inc(w41_one, 1)
            for i in range(ND):
                pool.memset(dA[:, i, :, 0:1], 0.0).then_inc(reset_ready, 1)
            pool.wait_ge(small_in, 16)
            pool.tensor_copy(sel[:, :], selc).then_inc(sel_ready, 1)
            pool.tensor_copy(selE[:, :], part_of["selE"]).then_inc(sel_ready, 1)
            pool.wait_ge(wo_in, 16)
            pool.tensor_scalar(Wo[:, :, :], Wo[:, :, :], 0.5, 1.0, ALU.mult, ALU.mult).then_inc(Woh_ready, 1)

            for name, q in order:
                if name == "scan":
                    s = q
                    pool.wait_ge(scan_done, s + 1)
                    pool.wait_ge(C_in[s % NC], 16 * (s // NC + 1))
                    if s >= NPB:
                        pool.wait_ge(nsum_done, s - NPB + 1)
                    pool.tensor_tensor(prod[:, s % NPB], hs[:, s % NHB],
                                       C_sb[:, s % NC].unsqueeze(1).to_broadcast([P, NH, T]),
                                       ALU.mult).then_inc(prod_ready, 1)
                elif name == "modulate":
                    pool.wait_ge(cs_ready, 1)
                    pool.tensor_copy(c_b[:, :, :], c_s[:, :].unsqueeze(2).to_broadcast([P, NB, P])
                                     ).then_inc(cb_ready, 1)
                elif name == "pool_wog":
                    pool.wait_ge(gates_ready, 2)
                    pool.wait_ge(Woh_ready, 1)
                    for b in range(NB):
                        pool.tensor_tensor(Wog[:, b], Wo[:, :, :],
                                           gate[:, b, 0].unsqueeze(1).to_broadcast([P, NH, P]),
                                           ALU.mult).then_inc(Wog_ready, 1)
                elif name == "sum_delta":
                    if q > 0:
                        sum_delta(pool, q)
                elif name == "pool_g":
                    pool.wait_ge(y_ready, 2 * (q + 1))
                    pool.wait_ge(zgate_ready, 2 * (q + 1))
                    if q > 0:
                        pool.wait_ge(wout_done, q)
                    pool.tensor_tensor(y2[:, :, :], y2[:, :, :], zz[:, q % 2], ALU.mult).then_inc(yg_ready, 1)
                elif name == "pool_out":
                    pool.wait_ge(acc_ready, q + 1)
                    pool.tensor_tensor(x_sb[:, q], acc[:, :, :], x_sb[:, q], ALU.add).then_inc(out_ready, 1)

        @block.scalar
        def _(act):
            act.preload_act_table_set("natural_log_exp_and_others")
            act.wait_ge(c_in, 16)
            act.activation(c_th[:, :], c_sb[:, :], ACT.Exp, scale=-1.0).then_inc(cth_ready, 1)
            act.wait_ge(small_in, 16)
            act.activation(convbh[:, :], convb[:, :], ACT.Copy, scale=0.5).then_inc(convbh_ready, 1)
            act.activation(Ae[:, :, :], Al[:, :, :], ACT.Exp).then_inc(Ae_ready, 1)

            def exps(s):
                q, n = divmod(s, NS)
                act.wait_ge(delta_ready, q + 1)
                act.wait_ge(A_ready, 1)
                act.wait_ge(reset_ready, ND)
                if s >= ND:
                    act.wait_ge(scan_done, s - ND + 1)
                for h in range(NH):
                    act.activation(dA[:, s % ND, h, 1:T], delta[:, q % 2, h, 1:T], ACT.Exp,
                                   scale=A[:, h, n:n + 1]).then_inc(dA_half if h == 0 else dA_ready, 1)

            def rstd_of(which, q):
                act.wait_ge(stats_ready[which], NT * (q + 1))
                if q > 0:
                    act.wait_ge(rstd_ready[which], q)
                act.activation(lnv[:, which], mv[:, which, :, 1], ACT.Ln, bias=low[:, 2:3]).then_inc(lnv_ready[which], 1)
                act.wait_ge(lnv_ready[which], q + 1)
                if q > 0:
                    act.wait_ge(xn_ready[which], NT * q)
                act.activation(rstd[:, which], lnv[:, which], ACT.Exp, scale=-0.5).then_inc(rstd_ready[which], 1)

            for name, q in order:
                g = banks.get(("pe_" + name[4:], q)) if name.startswith("act_") else None
                if name == "first":
                    for s in range(AHEAD):
                        exps(s)
                elif name == "scan":
                    if q + AHEAD <= last_s:
                        exps(q + AHEAD)
                elif name == "modulate":
                    act.wait_ge(mod_done, 1)
                    act.copy(mod[:, :, :], Yps[:, 0, 0:16].rearrange("p (k b) -> p k b", k=4)).then_inc(mod_ready, 1)
                    act.activation(mod1[:, :, :], Yps[:, 0, 0:16].rearrange("p (k b) -> p k b", k=4), ACT.Identity,
                                   bias=1.0).then_inc(mod_ready, 1)
                elif name == "act_rstd1":
                    rstd_of(0, q)
                elif name == "act_rstd2":
                    rstd_of(1, q)
                elif name == "act_hT":
                    g = banks[("pe_xT", q)]
                    act.wait_ge(xT_done, q + 1)
                    act.wait_ge(mod_ready, 2)
                    if q > 0:
                        act.wait_ge(x_done, 2 * q)
                        act.wait_ge(z_done, 2 * q)
                    act.activation(hT[:, :], G[g[0][0]][:, :], ACT.Identity, scale=mod1[:, 1, q:q + 1],
                                   bias=mod[:, 0, q:q + 1]).then_inc(hT_ready, 1)
                elif name == "act_h2T":
                    g = banks[("pe_xT2", q)]
                    act.wait_ge(xT2_done, q + 1)
                    act.activation(h2T[:, q], G[g[0][0]][:, :], ACT.Identity, scale=mod1[:, 3, q:q + 1],
                                   bias=mod[:, 2, q:q + 1]).then_inc(h2T_ready, 1)
                elif name in ("act_x0", "act_x1"):
                    h = int(name[-1])
                    k = 2 * q + h
                    act.wait_ge(x_done, k + 1)
                    act.wait_ge(taps_ready, 1)
                    act.wait_ge(convbh_ready, 1)
                    if k >= 2:
                        act.wait_ge(xconv_ready, k - 1)
                    act.activation(xch[:, h], G[g[0][0]][:, :], ACT.Identity, scale=taps[:, h, KC - 1:KC],
                                   bias=convbh[:, h:h + 1]).then_inc(xin_ready, 1)
                elif name in ("act_t0", "act_t1"):
                    h = int(name[-1])
                    k = 2 * q + h
                    act.wait_ge(conv_done, k + 1)
                    if k >= 2:
                        act.wait_ge(zgate_ready, k - 1)
                    act.activation(th[:, h], xch[:, h], ACT.Tanh).then_inc(xth_ready, 1)
                    if q == 0 and h == NH - 1:
                        act.preload_act_table_set("natural_log_exp_and_others")
                elif name in ("act_z0", "act_z1"):
                    h = int(name[-1])
                    k = 2 * q + h
                    act.wait_ge(z_done, k + 1)
                    act.wait_ge(xconv_ready, k + 1)
                    act.activation(th[:, h], G[g[0][0]][:, :], ACT.Tanh, scale=0.5).then_inc(zth_ready, 1)
                    if h == NH - 1:
                        act.preload_act_table_set("natural_log_exp_and_others")
                elif name == "act_hi":
                    g = banks[("pe_ssm", q)]
                    act.wait_ge(ssm_done, q + 1)
                    if q > 0:
                        act.wait_ge(rest_ready, q)
                        act.wait_ge(C_stored, 16 * q)
                    act.copy(C_rows[C_AT:, :], G[g[0][0]][C_AT:C_AT + NS, :]).then_inc(C_rows_ready, 1)
                    act.copy(hi[0:NPART, :], G[g[0][0]][0:NPART, :]).then_inc(hi_ready, 1)
                elif name == "act_mid":
                    act.wait_ge(rest_ready, q + 1)
                    if q > 0:
                        act.wait_ge(parts_ready, q)
                    act.copy(mid[0:NPART, :], rest[0:NPART, :]).then_inc(mid_ready, 1)
                elif name == "act_soft":
                    g = G[banks[("pe_delta", q)][0][0]]
                    act.wait_ge(delta_done, q + 1)
                    if q > 0:
                        act.wait_ge(dcor_ready, q)
                    for h in range(NH):
                        act.activation(dexp[:, h], g[:, :], ACT.Abs, scale=dtw[:, h:h + 1],
                                       bias=dtb[:, h:h + 1]).then_inc(dabs_ready, 1)
                    if q > 0:
                        act.wait_ge(delta_ready, q)
                    for h in range(NH):
                        act.activation(drel[:, h], g[:, :], ACT.Relu, scale=dtw[:, h:h + 1], bias=dtb[:, h:h + 1]
                                       ).then_inc(softin_half if h == 0 else softin_ready, 1)
                    act.wait_ge(dabs_ready, 2 * (q + 1))
                    act.activation(dexp[:, :, :], dexp[:, :, :], ACT.Exp, scale=-1.0).then_inc(dexp_ready, 1)
                    act.wait_ge(dexp_ready, q + 1)
                    if q > 0:
                        act.wait_ge(delta_ready, q)
                    act.activation(dlog[:, :, :], dexp[:, :, :], ACT.Ln, bias=1.0).then_inc(dlog_ready, 1)
                elif name[:5] == "act_r":
                    j = int(name[-1])
                    for i in range(2):
                        k = 2 * (NT * q + j) + i
                        act.wait_ge(r_done, k + 1)
                        if k >= 2:
                            act.wait_ge(sq_done, k - 1)
                        for e in range(4):
                            act.activation(sqj[:, i, e], G[g[i][0]][:, e * P:(e + 1) * P], ACT.Square,
                                           accum_out=r2[:, q, j, 4 * i + e:4 * i + e + 1]
                                           ).then_inc(sq_some if e < 3 else sq_done, 1)
                elif name == "act_sqrt":
                    act.wait_ge(clamp_ready, q + 1)
                    if q > 0:
                        act.wait_ge(res_ready, q)
                    act.activation(lr[:, :, :], r2c[:, :, :], ACT.Ln).then_inc(lr_ready, 1)
                    act.wait_ge(lr_ready, q + 1)
                    if q > 0:
                        act.wait_ge(gd_ready, q)
                    act.activation(res[:, :, :], lr[:, :, :], ACT.Exp, scale=0.5).then_inc(res_ready, 1)
                elif name == "act_gexp":
                    act.wait_ge(gd_ready, q + 1)
                    if q > 0:
                        act.wait_ge(rw_ready, q)
                    act.activation(ge[:, :, :], gd[:, :, :], ACT.Exp).then_inc(ge_ready, 1)
                elif name == "act_wT":
                    g = G[g[0][0]]
                    act.wait_ge(wT_done, q + 1)
                    if q > 0:
                        act.wait_ge(b_done, NE * q)
                        act.wait_ge(o_start, q)
                    act.copy(wTp[:, :], g[0:NP3 * NE, :]).then_inc(wTp_ready, 1)
                    act.copy(wT9[W9_AT:, :], g[W9_AT:W9_AT + NE + 1, :]).then_inc(wT_ready, 1)

        @block.vector
        def _(vec):
            vec.wait_ge(c_in, 16)
            vec.wait_ge(cth_ready, 1)
            vec.tensor_scalar(c_h[:, :], c_th[:, :], 1.0, None, ALU.add).then_inc(ch_ready, 1)
            vec.wait_ge(ch_ready, 1)
            vec.reciprocal(c_th[:, :], c_h[:, :]).then_inc(csig_ready, 1)
            vec.wait_ge(csig_ready, 1)
            vec.tensor_tensor(c_s[:, :], c_th[:, :], c_sb[:, :], ALU.mult).then_inc(cs_ready, 1)
            vec.wait_ge(small_in, 16)
            vec.tensor_scalar(taps[:, :, :], conv_w, 0.5, None, ALU.mult).then_inc(taps_ready, 1)
            vec.wait_ge(Ae_ready, 1)
            vec.tensor_scalar(A[:, :, :], Ae[:, :, :], -1.0, None, ALU.mult).then_inc(A_ready, 1)

            def dbx(s):
                q = s // NS
                vec.wait_ge(Bps_ready, s + 1)
                vec.wait_ge(dx_ready, q + 1)
                if s >= NX:
                    vec.wait_ge(scan_done, s - NX + 1)
                vec.tensor_tensor(dBx[:, s % NX], dx[:, q % 2], Bps[s % 2][:, :].unsqueeze(1).to_broadcast([P, NH, T]),
                                  ALU.mult).then_inc(dBx_ready, 1)

            def stats_of(which, q, src):
                if q > 0:
                    vec.wait_ge(bn_ready[which], NT * q)
                    vec.wait_ge(stats_ready[which], NT * q)
                for j in range(NT):
                    vec.bn_stats(stats[:, which, j], src[:, q, j]).then_inc(bn_ready[which], 1)
                if q > 0:
                    vec.wait_ge(rstd_ready[which], q)
                    vec.wait_ge(xn_ready[which], NT * q)
                for j in range(NT):
                    vec.wait_ge(bn_ready[which], NT * q + j + 1)
                    vec.bn_aggr(mv[:, which, j], stats[:, which, j]).then_inc(stats_ready[which], 1)

            def norm_of(which, q, src):
                vec.wait_ge(rstd_ready[which], q + 1)
                vec.wait_ge(stats_ready[which], NT * (q + 1))
                if q > 0:
                    vec.wait_ge(normT_done[which], q)
                for j in range(NT):
                    vec.tensor_scalar(xn[:, which, j], src[:, q, j], mv[:, which, j, 0:1], rstd[:, which, j:j + 1],
                                      ALU.subtract, ALU.mult).then_inc(xn_ready[which], 1)

            for name, q in order:
                if name == "first":
                    for s in range(AHEAD):
                        dbx(s)
                elif name == "scan":
                    s = q
                    if s + AHEAD <= last_s:
                        dbx(s + AHEAD)
                    vec.wait_ge(dA_ready, s + 1)
                    vec.wait_ge(dBx_ready, s + 1)
                    if s >= NHB:
                        vec.wait_ge(prod_ready, s - NHB + 1)
                    vec.tensor_tensor_scan(hs[:, s % NHB].rearrange("p h t -> p (h t)"),
                                           dA[:, s % ND].rearrange("p h t -> p (h t)"),
                                           dBx[:, s % NX].rearrange("p h t -> p (h t)"), 0.0,
                                           ALU.mult, ALU.add).then_inc(scan_done, 1)
                elif name == "vec_ln1":
                    vec.wait_ge(x_in[q], 16)
                    stats_of(0, q, x_sb)
                elif name == "vec_xn1":
                    norm_of(0, q, x_sb)
                elif name == "vec_xn2":
                    norm_of(1, q, x_sb)
                elif name in ("vec_c0", "vec_c1"):
                    h = int(name[-1])
                    k = 2 * q + h
                    g = G[banks[("pe_x%d" % h, q)][0][0]]
                    vec.wait_ge(xin_ready, k + 1)
                    for i in range(1, KC):
                        if k > 0 or i > 1:
                            vec.wait_ge(tap_done, 2 * k + i - 1)
                        vec.scalar_tensor_tensor(xch[:, h, i:], g[:, :T - i], taps[:, h, KC - 1 - i:KC - i],
                                                 xch[:, h, i:], ALU.mult, ALU.add
                                                 ).then_inc(tap_done if i < KC - 1 else conv_done, 1)
                elif name in ("vec_x0", "vec_x1"):
                    h = int(name[-1])
                    k = 2 * q + h
                    vec.wait_ge(xth_ready, k + 1)
                    if q >= 2:
                        vec.wait_ge(y_ready, 2 * (q - 1))
                        vec.wait_ge(dx_ready, q - 1)
                    vec.scalar_tensor_tensor(xconv[:, q % 2, h], th[:, h], 1.0, xch[:, h], ALU.add,
                                             ALU.mult).then_inc(xconv_ready, 1)
                elif name in ("vec_z0", "vec_z1"):
                    h = int(name[-1])
                    k = 2 * q + h
                    g = banks[("pe_" + name[4:], q)]
                    vec.wait_ge(zth_ready, k + 1)
                    if q >= 2:
                        vec.wait_ge(yg_ready, q - 1)
                    vec.scalar_tensor_tensor(zz[:, q % 2, h], th[:, h], 1.0, G[g[0][0]][:, :], ALU.add,
                                             ALU.mult).then_inc(zgate_ready, 1)
                elif name == "vec_u":
                    g = banks[("pe_ssm", q)]
                    vec.wait_ge(hi_ready, q + 1)
                    if q > 0:
                        vec.wait_ge(mid_ready, q)
                        vec.wait_ge(parts_ready, q)
                    vec.scalar_tensor_tensor(rest[0:NPART, :], hi[0:NPART, :], low[0:NPART, 0:1],
                                             G[g[0][0]][0:NPART, :], ALU.mult, ALU.add).then_inc(rest_ready, 1)
                elif name == "vec_parts":
                    vec.wait_ge(mid_ready, q + 1)
                    if q >= 2:
                        vec.wait_ge(Bps_ready, NS * (q - 1))
                        vec.wait_ge(delta_done, q - 1)
                    vec.scalar_tensor_tensor(parts[0:NPART, q % 2], mid[0:NPART, :], low[0:NPART, 1:2],
                                             rest[0:NPART, :], ALU.mult, ALU.add).then_inc(parts_ready, 1)
                elif name == "vec_soft":
                    vec.wait_ge(dexp_ready, q + 1)
                    if q > 0:
                        vec.wait_ge(dsum_ready, q)
                    vec.tensor_scalar(dw1[:, :, :], dexp[:, :, :], 1.0, None, ALU.add).then_inc(dw1_ready, 1)
                    vec.wait_ge(dw1_ready, q + 1)
                    vec.scalar_tensor_tensor(dw1[:, :, :].rearrange("p h t -> p (h t)"),
                                             dw1[:, :, :].rearrange("p h t -> p (h t)"), -1.0,
                                             dexp[:, :, :].rearrange("p h t -> p (h t)"), ALU.add, ALU.subtract
                                             ).then_inc(dcor_ready, 1)
                elif name == "sum_delta":
                    if q == 0:
                        sum_delta(vec, q)
                elif name == "vec_gates":
                    for i in range(2):
                        b = banks[(f"pe_gate{i}", 0)][0][0]
                        vec.wait_ge(gate_done, i + 1)
                        if i > 0:
                            vec.wait_ge(gates_ready, i)
                        vec.tensor_copy(graw[:, :], G[b][:, :]).then_inc(gates_read, 1)
                        vec.wait_ge(gates_read, i + 1)
                        vec.tensor_scalar(gsgn[:, :], graw[:, :], 0.0, 2.0, ALU.is_ge, ALU.mult).then_inc(gsgn_twice, 1)
                        vec.wait_ge(gsgn_twice, i + 1)
                        vec.tensor_scalar(gsgn[:, :], gsgn[:, :], -1.0, None, ALU.add).then_inc(gsgn_ready, 1)
                        vec.wait_ge(gsgn_ready, i + 1)
                        vec.tensor_tensor(graw[:, :], gsgn[:, :], graw[:, :], ALU.mult).then_inc(gabs_ready, 1)
                        vec.wait_ge(gabs_ready, i + 1)
                        vec.scalar_tensor_tensor(gate[:, 2 * i:2 * i + 2].rearrange("p b k o -> p (b k o)"), graw[:, :], 0.25,
                                                 gsgn[:, :], ALU.max, ALU.mult).then_inc(gates_ready, 1)
                elif name == "vec_V":
                    for i in range(2):
                        b = banks[(f"pe_V{i}", 0)][0][0]
                        vec.wait_ge(V_done, i + 1)
                        vec.tensor_tensor(M[:, 4 * i:4 * i + 4], ident[:, :].unsqueeze(1).to_broadcast([P, 4, P]),
                                          G[b][:, :].rearrange("p (e i) -> p e i", e=4), ALU.subtract
                                          ).then_inc(M_ready, 1)
                elif name == "vec_y":
                    vec.wait_ge(nsum_done, NS * (q + 1))
                    if q > 0:
                        vec.wait_ge(wout_done, q)
                    for h in range(NH):
                        vec.scalar_tensor_tensor(y2[:, h], xconv[:, q % 2, h], Dsk[:, h:h + 1], Yps[:, h], ALU.mult,
                                                 ALU.add).then_inc(y_ready, 1)
                elif name == "vec_x2":
                    g = banks[("pe_wout", q)]
                    vec.wait_ge(wout_done, q + 1)
                    vec.tensor_tensor(x_sb[:, q], G[g[0][0]][:, :].rearrange("p (j o) -> p j o", j=NT), x_sb[:, q],
                                      ALU.add).then_inc(x2_ready, 1)
                    vec.wait_ge(x2_ready, q + 1)
                    stats_of(1, q, x_sb)
                elif name == "vec_clamp":
                    vec.wait_ge(sq_done, 2 * NT * (q + 1))
                    if q > 0:
                        vec.wait_ge(lr_ready, q)
                    vec.tensor_scalar(r2c[:, :, :], r2[:, q], 1e-18, None, ALU.max).then_inc(clamp_ready, 1)
                elif name == "vec_gate1":
                    vec.wait_ge(res_ready, q + 1)
                    if q > 0:
                        vec.wait_ge(gd_ready, q)
                    vec.tensor_reduce(rmin[:, :], res[:, :, :], AX, ALU.min).then_inc(rmin_ready, 1)
                    vec.wait_ge(rmin_ready, q + 1)
                    if q > 0:
                        vec.wait_ge(ge_ready, q)
                    vec.tensor_tensor(gd[:, :, :], rmin[:, :].unsqueeze(2).to_broadcast([P, NT, NE]), res[:, :, :],
                                      ALU.subtract).then_inc(gd_ready, 1)
                    ve = r2[:, q].unsqueeze(3).to_broadcast([P, NT, NE, NE])
                    vf = r2[:, q].unsqueeze(2).to_broadcast([P, NT, NE, NE])
                    if q > 0:
                        vec.wait_ge(rank_ready, q)
                        vec.wait_ge(cnt_ready, q)
                    vec.tensor_tensor(lt[:, :, :, :], vf, ve, ALU.is_lt).then_inc(lt_ready, 1)
                    vec.tensor_tensor(eq[:, :, :, :], vf, ve, ALU.is_equal).then_inc(eq_ready, 1)
                    vec.wait_ge(eq_ready, q + 1)
                    vec.tensor_tensor(eq[:, :, :, :].rearrange("p j e f -> p j (e f)"),
                                      eq[:, :, :, :].rearrange("p j e f -> p j (e f)"),
                                      tri[:, :, :].rearrange("p e f -> p (e f)").unsqueeze(1).to_broadcast([P, NT, NE * NE]),
                                      ALU.mult).then_inc(eql_ready, 1)
                    vec.wait_ge(eql_ready, q + 1)
                    if q > 0:
                        vec.wait_ge(rank_ready, q)
                    vec.tensor_tensor(lt[:, :, :, :], lt[:, :, :, :], eq[:, :, :, :], ALU.add).then_inc(cnt_ready, 1)
                    vec.wait_ge(cnt_ready, q + 1)
                    if q > 0:
                        vec.wait_ge(keep_ready, q)
                    vec.tensor_reduce(rank[:, :, :], lt[:, :, :, :], AX, ALU.add).then_inc(rank_ready, 1)
                elif name == "vec_gate2":
                    vec.wait_ge(ge_ready, q + 1)
                    if q > 0:
                        vec.wait_ge(w_ready, q)
                    vec.tensor_reduce(gs[:, :], ge[:, :, :], AX, ALU.add).then_inc(gs_ready, 1)
                    vec.wait_ge(gs_ready, q + 1)
                    vec.reciprocal(gr[:, :], gs[:, :]).then_inc(gr_ready, 1)
                    vec.wait_ge(gr_ready, q + 1)
                    vec.tensor_tensor(rw[:, :, :], ge[:, :, :], gr[:, :].unsqueeze(2).to_broadcast([P, NT, NE]),
                                      ALU.mult).then_inc(rw_ready, 1)
                    vec.wait_ge(rw_ready, q + 1)
                    vec.tensor_scalar(msk[:, :, :], rw[:, :, :], 1.0 / NE, None, ALU.is_gt).then_inc(msk_ready, 1)
                    vec.wait_ge(msk_ready, q + 1)
                    vec.wait_ge(rank_ready, q + 1)
                    vec.scalar_tensor_tensor(keep[:, :, :], rank[:, :, :], 2.0, msk[:, :, :], ALU.is_lt,
                                             ALU.mult).then_inc(keep_ready, 1)
                    vec.wait_ge(keep_ready, q + 1)
                    vec.tensor_tensor(fw[:, :, :], rw[:, :, :], keep[:, :, :], ALU.mult).then_inc(fw_ready, 1)
                    vec.wait_ge(fw_ready, q + 1)
                    vec.tensor_reduce(sw[:, :], fw[:, :, :], AX, ALU.add).then_inc(sw_ready, 1)
                    vec.wait_ge(sw_ready, q + 1)
                    vec.scalar_tensor_tensor(swz[:, :], sw[:, :], 0.0, sw[:, :], ALU.is_equal, ALU.add).then_inc(swz_ready, 1)
                    vec.wait_ge(swz_ready, q + 1)
                    vec.reciprocal(rsw[:, :], swz[:, :]).then_inc(rsw_ready, 1)
                    vec.wait_ge(rsw_ready, q + 1)
                    vec.wait_ge(w41_one, 1)
                    if q > 0:
                        vec.wait_ge(wT_done, q)
                    w = w41[:, :, W9_AT:W9_AT + NE]
                    vec.tensor_tensor(w, fw[:, :, :], rsw[:, :].unsqueeze(2).to_broadcast([P, NT, NE]),
                                      ALU.mult).then_inc(w_ready, 1)
                    vec.wait_ge(w_ready, q + 1)
                    vec.tensor_copy(w_hi[:, :, :], w).then_inc(w_hi_ready, 1)
                    vec.wait_ge(w_hi_ready, q + 1)
                    vec.tensor_copy(w41[:, :, 0:NE], w_hi[:, :, :]).then_inc(w_part0, 1)
                    vec.tensor_tensor(w_rest[:, :, :], w, w_hi[:, :, :], ALU.subtract).then_inc(w_rest_ready, 1)
                    vec.wait_ge(w_rest_ready, q + 1)
                    vec.tensor_copy(w_mid[:, :, :], w_rest[:, :, :]).then_inc(w_mid_ready, 1)
                    vec.wait_ge(w_mid_ready, q + 1)
                    vec.tensor_copy(w41[:, :, NE:2 * NE], w_mid[:, :, :]).then_inc(w_part1, 1)
                    vec.tensor_tensor(w41[:, :, 2 * NE:3 * NE], w_rest[:, :, :], w_mid[:, :, :], ALU.subtract
                                      ).then_inc(w_parts_ready, 1)
                elif name[:5] == "vec_h":
                    e = int(name[-1])
                    k = NE * q + e
                    bank = banks[(f"pe_b{e}", q)][0][0]
                    vec.wait_ge(b_done, k + 1)
                    if k >= NW:
                        vec.wait_ge(a_done, k - NW + 1)
                    vec.tensor_tensor(wh[:, (NE * q + e) % NW], h2T[:, q], G[bank][:, :], ALU.mult).then_inc(wh_ready, 1)
                elif name == "vec_out":
                    vec.wait_ge(a_done, NE * (q + 1))
                    if q > 0:
                        vec.wait_ge(out_ready, q)
                    vec.tensor_tensor(acc[:, :, :], Ops[:, :].rearrange("p (j o) -> p j o", j=NT),
                                      gate[:, q, 1].unsqueeze(1).to_broadcast([P, NT, P]), ALU.mult
                                      ).then_inc(acc_ready, 1)

        @block.tensor
        def _(pe):
            def shared(name, q, i=0):
                bank, before = banks[(name, q)][i]
                if before is not None:
                    pe.wait_ge(*before)
                return G[bank]

            def bcast_B(s):
                q, n = divmod(s, NS)
                pe.wait_ge(parts_ready, q + 1)
                pe.wait_ge(sel_ready, 2)
                if s >= 2:
                    pe.wait_ge(dBx_ready, s - 1)
                pe.matmul(Bps[s % 2][:, :], sel[0:NPART, n:n + 1].to_broadcast([NPART, P]), parts[0:NPART, q % 2], start=True, stop=True
                          ).then_inc(Bps_ready, 1)

            def nsum(s):
                q, n = divmod(s, NS)
                pe.wait_ge(prod_ready, s + 1)
                if n == 0:
                    pe.wait_ge(mod_ready, 2)
                    if q > 0:
                        pe.wait_ge(y_ready, 2 * q)
                for h in range(NH):
                    mm = pe.matmul(Yps[:, h], ident[:, :], prod[:, s % NPB, h], start=(n == 0), stop=(n == NS - 1))
                mm.then_inc(nsum_done, 1)

            pe.wait_ge(wm_in, 16)
            pe.wait_ge(cs_ready, 1)
            for i, k in enumerate((0, 1, 3, 4)):
                mm = pe.matmul(Yps[:, 0, NB * i:NB * i + NB], wm[:, k], c_s[:, :], start=True, stop=True)
            mm.then_inc(mod_done, 1)
            pe.wait_ge(ident_in, 16)

            for name, q in order:
                if name == "first":
                    for s in range(AHEAD):
                        bcast_B(s)
                elif name == "scan":
                    if q + AHEAD <= last_s:
                        bcast_B(q + AHEAD)
                    if q >= 2:
                        nsum(q - 2)
                elif name == "last":
                    nsum(last_s - 1)
                    nsum(last_s)
                elif name == "pe_xT":
                    g = shared(name, q)
                    pe.wait_ge(xn_ready[0], NT * (q + 1))
                    for j in range(NT):
                        mm = pe.transpose(g[:, j * P:(j + 1) * P], xn[:, 0, j], ident[:, :])
                    mm.then_inc(xT_done, 1)
                elif name == "pe_xT2":
                    g = shared(name, q)
                    pe.wait_ge(xn_ready[1], NT * (q + 1))
                    for j in range(NT):
                        mm = pe.transpose(g[:, j * P:(j + 1) * P], xn[:, 1, j], ident[:, :])
                    mm.then_inc(xT2_done, 1)
                elif name in ("pe_x0", "pe_x1"):
                    h = int(name[-1])
                    g = shared(name, q)
                    pe.wait_ge(hT_ready, q + 1)
                    pe.wait_ge(win_in, 16)
                    pe.matmul(g[:, :], Win[:, h * P:(h + 1) * P], hT[:, :], start=True, stop=True).then_inc(x_done, 1)
                elif name in ("pe_z0", "pe_z1"):
                    h = int(name[-1])
                    g = shared(name, q)
                    pe.matmul(g[:, :], Win[:, DI + h * P:DI + (h + 1) * P], hT[:, :], start=True, stop=True
                              ).then_inc(z_done, 1)
                elif name == "pe_ssm":
                    g = shared(name, q)
                    pe.wait_ge(wx_in, 16)
                    pe.wait_ge(xconv_ready, 2 * (q + 1))
                    for h in range(NH):
                        mm = pe.matmul(g[0:C_AT + NS, :], Wx[:, h], xconv[:, q % 2, h], start=(h == 0), stop=(h == NH - 1))
                    mm.then_inc(ssm_done, 1)
                elif name == "pe_delta":
                    g = shared(name, q)
                    pe.wait_ge(parts_ready, q + 1)
                    pe.wait_ge(sel_ready, 2)
                    pe.matmul(g[:, :], sel[0:NPART, NS:NS + 1].to_broadcast([NPART, P]), parts[0:NPART, q % 2], start=True, stop=True
                              ).then_inc(delta_done, 1)
                elif name in ("pe_gate0", "pe_gate1"):
                    i = int(name[-1])
                    g = shared(name, q)
                    pe.wait_ge(cb_ready, 1)
                    for b in range(2):
                        for k in range(2):
                            at = (2 * b + k) * P
                            mm = pe.matmul(g[:, at:at + P], c_b[:, 2 * i + b], wm[:, 2 + 3 * k], start=True, stop=True)
                    mm.then_inc(gate_done, 1)
                elif name in ("pe_V0", "pe_V1"):
                    i = int(name[-1])
                    g = shared(name, q)
                    pe.wait_ge(v_in, 16)
                    for e in range(4):
                        mm = pe.matmul(g[:, e * P:(e + 1) * P], V[:, 4 * i + e], V[:, 4 * i + e], start=True, stop=True)
                    mm.then_inc(V_done, 1)
                elif name == "pe_wout":
                    g = shared(name, q)
                    pe.wait_ge(yg_ready, q + 1)
                    pe.wait_ge(Wog_ready, NB)
                    for j in range(NT):
                        for h in range(NH):
                            mm = pe.matmul(g[:, j * P:(j + 1) * P], y2[:, h, j * P:(j + 1) * P], Wog[:, q, h],
                                           start=(h == 0), stop=(h == NH - 1))
                    mm.then_inc(wout_done, 1)
                elif name[:4] == "pe_r":
                    j = int(name[-1])
                    for i in range(2):
                        g = shared(name, q, i)
                        if j == 0:
                            pe.wait_ge(h2T_ready, q + 1)
                            pe.wait_ge(M_ready, 2)
                        pe.matmul(g[:, :], h2T[:, q, j * P:(j + 1) * P], M[:, 4 * i:4 * i + 4].rearrange("p e i -> p (e i)"),
                                  start=True, stop=True).then_inc(r_done, 1)
                elif name == "pe_wT":
                    g = shared(name, q)
                    pe.wait_ge(w_parts_ready, q + 1)
                    pe.wait_ge(w_part0, q + 1)
                    pe.wait_ge(w_part1, q + 1)
                    for j in range(NT):
                        mm = pe.transpose(g[0:W9_AT + NE + 1, j * P:(j + 1) * P], w41[:, j], ident[:, :])
                    mm.then_inc(wT_done, 1)
                elif name == "pe_o":
                    pe.wait_ge(w9_in, 16)
                    pe.wait_ge(b9_in, 16)
                    pe.wait_ge(wT_ready, q + 1)
                    pe.wait_ge(h2T_ready, q + 1)
                    if q > 0:
                        pe.wait_ge(acc_ready, q)
                    for j in range(NT):
                        pe.matmul(Ops[:, j * P:(j + 1) * P], h2T[:, q, j * P:(j + 1) * P], W9[:, NE * P:],
                                  start=(j == 0), stop=False, skip_group_check=True)
                        mm = pe.matmul(Ops[:, j * P:(j + 1) * P], wT9[W9_AT:, j * P:(j + 1) * P], b9[W9_AT:, :],
                                       start=False, stop=False, skip_group_check=True)
                    mm.then_inc(o_start, 1)
                elif name[:4] == "pe_b":
                    e = int(name[-1])
                    g = shared(name, q)
                    pe.wait_ge(wTp_ready, q + 1)
                    pe.matmul(g[:, :], selE[0:NP3 * NE, e:e + 1].to_broadcast([NP3 * NE, P]), wTp[:, :], start=True,
                              stop=True).then_inc(b_done, 1)
                elif name[:4] == "pe_a":
                    e = int(name[-1])
                    pe.wait_ge(wh_ready, NE * q + e + 1)
                    for j in range(NT):
                        mm = pe.matmul(Ops[:, j * P:(j + 1) * P], wh[:, (NE * q + e) % NW, j * P:(j + 1) * P], W9[:, e * P:(e + 1) * P],
                                       start=False, stop=(e == NE - 1), skip_group_check=True)
                    mm.then_inc(a_done, 1)


def kernel(L0_attn_x, L0_attn_W_in, L0_attn_conv_w, L0_attn_conv_b, L0_attn_W_x, L0_attn_dt_w, L0_attn_dt_b,
           L0_attn_A_log, L0_attn_D, L0_attn_W_out, L0_ffn_Wp, L0_ffn_bp, L0_ffn_We, L0_ffn_be, L0_ffn_Vg, L0_c, L0_wmod):
    import concourse.bacc as _bacc
    from concourse.bass_utils import run_bass_kernel_spmd as _run

    def halves(a):
        return a.reshape(NH, P).T

    part = np.full(P, -1)
    which = np.full(P, -1)
    for i in range(NP3):
        part[NS * i:NS * (i + 1)], which[NS * i:NS * (i + 1)] = i, np.arange(NS)
        part[NS * NP3 + i], which[NS * NP3 + i] = i, NS
    sel = np.zeros((P, NS + 1), np.float32)
    for p in range(NPART):
        sel[p, which[p]] = 1.0
    selE = np.zeros((P, NE), np.float32)
    for p in range(NP3 * NE):
        selE[p, p % NE] = 1.0
    low = np.zeros((P, 8), np.float32)
    low[:, 0] = -(part >= 1).astype(np.float32)
    low[:, 1] = -(part >= 2).astype(np.float32)
    low[:, 2] = EPS
    tri = np.broadcast_to(np.tril(np.ones((NE, NE), np.float32), -1), (P, NE, NE))
    small = {
        "conv_b": halves(np.asarray(L0_attn_conv_b)), "dt_w": halves(np.asarray(L0_attn_dt_w)),
        "dt_b": halves(np.asarray(L0_attn_dt_b)), "D": halves(np.asarray(L0_attn_D)),
        "A_log": np.asarray(L0_attn_A_log).reshape(NH, P, NS).transpose(1, 0, 2).reshape(P, NH * NS),
        "conv_w": np.asarray(L0_attn_conv_w).reshape(NH, P, KC).transpose(1, 0, 2).reshape(P, NH * KC),
        "selE": selE, "low": low, "sel": sel, "tri": tri.reshape(P, NE * NE),
    }
    W_x = np.asarray(L0_attn_W_x).reshape(NH, P, 2 * NS + 1).transpose(1, 0, 2)
    W_o = np.asarray(L0_attn_W_out).reshape(NH, P, P).transpose(1, 0, 2)
    W9 = np.concatenate([np.asarray(L0_ffn_We), np.asarray(L0_ffn_Wp)[None]]).transpose(2, 0, 1).reshape(P, (NE + 1) * P)
    b9 = np.concatenate([np.asarray(L0_ffn_be), np.asarray(L0_ffn_bp)[None]])
    arrays = {
        "x": L0_attn_x, "W_in": L0_attn_W_in, 
        "small": np.concatenate([small[k] for k in SMALL], axis=1),
        "W_x": np.concatenate([W_x[:, :, 1:1 + NS]] * NP3 + [W_x[:, :, :1]] * NP3
                              + [np.zeros((P, NH, C_AT - NPART), np.float32), W_x[:, :, 1 + NS:]], axis=2),
        "W_out": W_o,
        "W9": W9, "b9": b9, "VgT": np.asarray(L0_ffn_Vg).transpose(2, 0, 1),
        "cT": np.asarray(L0_c).T, "wmod": L0_wmod, "ident": np.eye(P, dtype=np.float32),
    }
    nc = _bacc.Bacc("TRN2", target_bir_lowering=False, num_devices=1)
    ins, args = {}, []
    for name, a in arrays.items():
        a = np.ascontiguousarray(a)
        ins["in_" + name] = a
        args.append(nc.dram_tensor("in_" + name, a.shape, mybir.dt.from_np(a.dtype), kind="ExternalInput").ap())
    out = nc.dram_tensor("out", (NB, T, P), F32, kind="ExternalOutput").ap()
    C_dram = nc.dram_tensor("C_dram", (NB, NS, T), F32, kind="Internal").ap()
    adaln_mamba_experts(nc, *args, C_dram, out)
    return _run(nc, [ins], core_ids=[0]).results[0]["out"]
```

```python
from contextlib import ExitStack

import numpy as np

import concourse.bass as bass
from concourse import mybir

ALU = mybir.AluOpType
ACT = mybir.ActivationFunctionType
AX = mybir.AxisListType.X
F32 = mybir.dt.float32
BF16 = mybir.dt.bfloat16

P = 128
NB = 4
T = 512
NT = T // P
DI = 256
NH = DI // P
NS = 16
KC = 4
NE = 8
RV = 64
NP3 = 3
NPART = NS * NP3 + NP3
C_AT = 64
EPS = 1e-5

SMALL = {"selE": NE, "conv_b": NH, "dt_w": NH, "dt_b": NH, "D": NH, "A_log": NH * NS, "conv_w": NH * KC, "low": 8, "sel": NS + 1, "tri": NE * NE}

HEAD = [
    ("vec_ln1", 0), ("act_rstd1", 0), ("vec_shift1", 0), ("act_xn1", 0), ("pe_xT", 0), ("act_hT", 0),
    ("vec_ln1", 1), ("pe_x0", 0), ("pe_x1", 0), ("pe_z0", 0), ("act_rstd1", 1), ("vec_shift1", 1),
    ("act_x0", 0), ("act_x1", 0), ("vec_c0", 0), ("pe_z1", 0), ("vec_c1", 0), ("act_t0", 0), ("vec_x0", 0),
    ("act_t1", 0), ("vec_x1", 0), ("pe_ssm", 0), ("act_z0", 0), ("vec_z0", 0), ("act_z1", 0),
    ("vec_z1", 0), ("act_hi", 0), ("act_C", 0), ("act_xn1", 1), ("pe_xT", 1), ("vec_u", 0), ("act_mid", 0),
    ("sp_c", 0), ("vec_parts", 0), ("act_hT", 1), ("pe_delta", 0), ("act_soft0", 0), ("act_soft1", 0),
    ("vec_soft0", 0), ("soft_sum0", 0), ("soft_add0", 0), ("delta_x0", 0), ("vec_soft1", 0),
    ("soft_sum1", 0), ("soft_add1", 0), ("delta_x1", 0), ("first", 0)
]
LEAD = {
    "vec_ln1": (-6, -6, -6), "act_rstd1": (-4, -7, -6), "vec_shift1": (-4, -5, -5), "act_hT": (-2, -4, -2),
    "act_xn1": (-4, -5, -4), "pe_xT": (-3, -3, -2), "act_x0": (1, 1, 2), "pe_x0": (1, 2, 2),
    "act_x1": (1, 1, 2), "vec_c0": (1, 2, 2), "pe_x1": (1, 2, 2), "act_t0": (2, 3, 3), "vec_c1": (1, 3, 2),
    "pe_z0": (2, 4, 3), "act_t1": (2, 4, 3), "act_z0": (3, 4, 4), "vec_x0": (2, 3, 3), "vec_z0": (3, 5, 4),
    "vec_x1": (3, 3, 3), "pe_z1": (5, 5, 4), "vec_z1": (4, 5, 4), "pe_ssm": (5, 5, 5), "act_hi": (5, 5, 5),
    "act_C": (5, 5, 5), "act_z1": (4, 4, 4), "sp_c": (4, 5, 5), "vec_u": (6, 6, 6), "act_mid": (7, 7, 8),
    "vec_parts": (8, 8, 9), "pe_delta": (9, 9, 9), "act_soft0": (7, 9, 9), "vec_soft0": (10, 10, 10),
    "vec_soft1": (10, 10, 10), "act_soft1": (9, 9, 9), "soft_sum0": (10, 10, 10),
    "soft_add0": (10, 10, 10), "soft_sum1": (10, 10, 10), "soft_add1": (10, 10, 10),
    "delta_x0": (11, 11, 11), "delta_x1": (11, 11, 11)
}
LAG = {
    "vec_y0": (1, 0, 0), "gate_z0": (1, 0, 0), "vec_y1": (1, 0, 0), "gate_z1": (1, 0, 0),
    "pe_wout": (4, 3, 2), "vec_x2": (3, 3, 2), "act_rstd2": (5, 4, 2), "vec_shift2": (6, 5, 3),
    "act_xn2": (6, 5, 3), "pe_xT2": (8, 6, 4), "act_h2T": (8, 6, 4), "pe_ra0": (9, 7, 5),
    "sq_ra0": (9, 7, 5), "pe_rb0": (9, 7, 5), "sq_rb0": (9, 7, 5), "pe_ra1": (11, 8, 5),
    "sq_ra1": (11, 8, 5), "sq_rb1": (11, 8, 5), "pe_ra2": (12, 9, 5), "sq_ra2": (12, 9, 5),
    "pe_rb1": (11, 8, 5), "pe_rb2": (11, 9, 5), "sq_rb2": (11, 9, 5), "pe_ra3": (12, 9, 6),
    "sq_ra3": (13, 9, 6), "pe_rb3": (12, 9, 6), "sq_rb3": (13, 9, 6), "pe_o": (19, 15, 8),
    "vec_clamp": (15, 12, 7), "vec_ranka": (15, 10, 7), "act_sqrt": (16, 13, 7), "vec_gate1": (16, 12, 8),
    "vec_rankb": (16, 12, 8), "vec_gate2": (16, 12, 8), "split_w": (17, 12, 8), "pe_wT": (19, 15, 10),
    "act_gexp": (16, 13, 8), "act_wT": (19, 15, 9), "pe_b0": (21, 16, 10), "vec_h0": (21, 16, 9),
    "pe_b1": (21, 16, 10), "vec_h1": (22, 16, 10), "pe_b2": (23, 16, 11), "vec_h2": (23, 17, 11),
    "pe_bias": (23, 18, 11), "pe_b3": (23, 18, 11), "vec_h3": (23, 18, 11), "pe_a0": (22, 18, 11),
    "pe_a1": (24, 18, 11), "pe_b4": (25, 19, 12), "vec_h4": (25, 19, 12), "pe_a2": (26, 20, 15),
    "pe_b5": (26, 20, 12), "vec_h5": (26, 19, 12), "pe_a3": (26, 20, 15), "pe_b6": (26, 21, 12),
    "vec_h6": (26, 21, 13), "pe_a4": (27, 20, 15), "pe_b7": (29, 22, 15), "vec_h7": (28, 22, 15),
    "pe_a5": (28, 21, 15), "pe_a6": (30, 23, 15), "pe_a7": (30, 23, 15), "vec_out": (30, 24, 15),
    "sp_out": (29, 23, 15), "pool_out": (30, 24, 15)
}
SETUP = {
    "pe_gate0": 2, "pe_gate1": 4, "vec_gates": 3, "pool_wog": 6, "pe_V0": 9, "pe_V1": 10, "vec_V": 10
}
SQ_LAST = f"sq_rb{NT - 1}"

ANY = {"vec_gate2": "vec_any", "pe_a2": "pe_any", "vec_h5": "vec_flag"}


def plan():
    steps = [[] for _ in range(NB * NS)]
    for name, n in SETUP.items():
        steps[n].append((name, 0))
    for q in range(NB - 1):
        for name, after in LAG.items():
            steps[NS * (q + 1) + after[q]].append((name, q))
    for q in range(1, NB):
        for name, after in LEAD.items():
            if (name, q) not in HEAD:
                steps[NS * (q - 1) + after[q - 1]].append((name, q))
    order = [("modulate", 0)] + HEAD
    for s, pieces in enumerate(steps):
        order += [("scan", s), *pieces]
    order += [("last", 0)]
    for name in LAG:
        order.append((name, NB - 1))
        if name in ANY:
            order.append((ANY[name], NB - 1))
    pieces = ["vec_top", "pe_wT", "act_wT", "pe_bias"]
    for e in range(NE):
        pieces += [f"pe_b{e}", f"vec_h{e}", f"pe_a{e}"]
    unmasked = [(name, q) for q in range(NB, 2 * NB) for name in pieces + ["vec_out", "pool_out", "sp_out"]]
    return order, unmasked


C_AHEAD = 4
AHEAD = 3
BEHIND = 3
NG = 3
W9_AT = 32


def bank_plan(order, shared_banks):
    uses, turn = {}, []
    for name, q in order:
        if name in shared_banks:
            count, sem, per, first = shared_banks[name]
            for i in range(count):
                k = len(turn)
                before = turn[k - NG] if k >= NG else None
                uses.setdefault((name, q), []).append((k % NG, before))
                turn.append((sem, per * q + first + i))
    return uses


def adaln_mamba_experts(nc, x, W_in, smalls, W_x, W_out, We_Wp, be_bp, VgT, cT, wmod, eye, C_dram, out):
    order, unmasked = plan()
    with ExitStack() as ctx:
        def sb(name, shape, dt=F32):
            return ctx.enter_context(nc.sbuf_tensor(name, shape, dt))

        def ps(name, shape):
            return ctx.enter_context(nc.psum_tensor(name, shape, F32))

        ND, NX, NHB, NPB, NC, NW = 4, 4, 4, 4, 5, 3
        def sem(name):
            return ctx.enter_context(nc.semaphore(name))

        x_in = [sem(f"x{b}_in") for b in range(NB)]
        C_in = [sem(f"C{i}_in") for i in range(NC)]
        bn_ready, stats_ready, lnv_ready, rstd_ready, shift_ready, xn_ready = (
            [sem(f"{name}{i}") for i in range(2)] for name in (
                "bn_ready", "stats_ready", "lnv_ready", "rstd_ready", "shift_ready", "xn_ready"))
        (c_in, wm_in, ident_in, small_in, win_in, wx_in, wo_in, v_in, w9_in, b9_in) = map(sem, (
            "c_in", "wm_in", "ident_in", "small_in", "win_in", "wx_in", "wo_in", "v_in", "w9_in",
            "b9_in"))
        (w41_clear, w41_one, reset_ready, sel_ready, Woh_ready, convbh_ready, taps_ready, Ae_ready,
         A_ready, V_done, M_ready) = map(sem, (
            "w41_clear", "w41_one", "reset_ready", "sel_ready", "Woh_ready", "convbh_ready",
            "taps_ready", "Ae_ready", "A_ready", "V_done", "M_ready"))
        (cth_ready, ch_ready, csig_ready, cs_ready, mod_done, mod_ready, gate_done,
         gates_read, gsgn_twice, gsgn_ready, gabs_ready, gates_ready, Wog_ready) = map(sem, (
            "cth_ready", "ch_ready", "csig_ready", "cs_ready", "mod_done", "mod_ready",
            "gate_done", "gates_read", "gsgn_twice", "gsgn_ready", "gabs_ready", "gates_ready",
            "Wog_ready"))
        (xT_done, hT_ready, x_done, z_done, xin_ready, tap_done, conv_done, xth_ready, xconv_ready,
         zth_ready, zgate_ready) = map(sem, (
            "xT_done", "hT_ready", "x_done", "z_done", "xin_ready", "tap_done", "conv_done",
            "xth_ready", "xconv_ready", "zth_ready", "zgate_ready"))
        (ssm_done, C_rows_ready, C_stored, hi_ready, rest_ready, mid_ready, parts_ready, delta_done,
         dabs_ready, softin_ready, dexp_ready, dw1_ready, dcor_ready, dlog_ready,
         dsum_ready, delta_ready, dx_ready) = map(sem, (
            "ssm_done", "C_rows_ready", "C_stored", "hi_ready", "rest_ready", "mid_ready",
            "parts_ready", "delta_done", "dabs_ready", "softin_ready", "dexp_ready",
            "dw1_ready", "dcor_ready", "dlog_ready", "dsum_ready", "delta_ready", "dx_ready"))
        (Bps_ready, dA_half, dA_ready, dBx_ready, scan_done, prod_ready, nsum_done) = map(sem, (
            "Bps_ready", "dA_half", "dA_ready", "dBx_ready", "scan_done", "prod_ready",
            "nsum_done"))
        (y_ready, yg_ready, wout_done, x2_ready, xT2_done, h2T_ready) = map(sem, (
            "y_ready", "yg_ready", "wout_done", "x2_ready", "xT2_done", "h2T_ready"))
        (ra_done, rb_done, sqa_some, sqa_done, sqb_some, sqb_done, clamp_ready, lr_ready, res_ready, rmin_ready, gd_ready, ge_ready,
         lt_ready, eq_ready, eql_ready, cnt_ready, rank_ready, gs_ready, gr_ready, rw_ready, msk_ready,
         keep_ready, fw_ready, sw_ready, swz_ready, rsw_ready, w_ready, w_hi_ready, w_part0,
         w_rest_ready, w_mid_ready, w_part1, w_parts_ready, wT_done, wTp_ready, wT_ready) = map(sem, (
            "ra_done", "rb_done", "sqa_some", "sqa_done", "sqb_some", "sqb_done", "clamp_ready", "lr_ready", "res_ready", "rmin_ready",
            "gd_ready", "ge_ready", "lt_ready", "eq_ready", "eql_ready", "cnt_ready", "rank_ready",
            "gs_ready", "gr_ready", "rw_ready", "msk_ready", "keep_ready", "fw_ready", "sw_ready",
            "swz_ready", "rsw_ready", "w_ready", "w_hi_ready", "w_part0", "w_rest_ready",
            "w_mid_ready", "w_part1", "w_parts_ready", "wT_done", "wTp_ready", "wT_ready"))
        (bias_done, b_done, wh_ready, a_done, acc_ready, out_ready, stored, passing_ready, any_done,
         flag_ready, resid_copied) = map(sem, (
            "bias_done", "b_done", "wh_ready", "a_done", "acc_ready", "out_ready", "stored", "passing_ready", "any_done",
            "flag_ready", "resid_copied"))
        normT_done = [xT_done, xT2_done]

        shared_banks = {
            "pe_xT": (1, hT_ready, 1, 1), "pe_x0": (1, conv_done, 2, 1), "pe_x1": (1, conv_done, 2, 2),
            "pe_z0": (1, zgate_ready, 2, 1), "pe_z1": (1, zgate_ready, 2, 2), "pe_ssm": (1, rest_ready, 1, 1),
            "pe_delta": (1, softin_ready, 2, 2), "pe_wout": (1, x2_ready, 1, 1), "pe_xT2": (1, h2T_ready, 1, 1),
            "pe_wT": (1, wT_ready, 1, 1), **{f"pe_b{e}": (1, wh_ready, NE, e + 1) for e in range(NE)},
            "pe_gate0": (1, gates_read, 2, 1), "pe_gate1": (1, gates_read, 2, 2),
            "pe_V0": (1, M_ready, 2, 1), "pe_V1": (1, M_ready, 2, 2),
            **{f"pe_ra{j}": (1, sqa_done, NT, j + 1) for j in range(NT)},
            **{f"pe_rb{j}": (1, sqb_done, NT, j + 1) for j in range(NT)},
        }
        banks = bank_plan(order + unmasked, shared_banks)

        Win = sb("Win", [P, 2 * DI])
        small = sb("small", [P, sum(SMALL.values())])
        part_of, at = {}, 0
        for name, width in SMALL.items():
            part_of[name] = small[:, at:at + width]
            at += width
        convb, dtw, dtb, Dsk = (part_of[k] for k in ("conv_b", "dt_w", "dt_b", "D"))
        Al = part_of["A_log"].rearrange("p (h n) -> p h n", h=NH)
        low, selc = part_of["low"], part_of["sel"]
        tri = part_of["tri"].rearrange("p (e f) -> p e f", e=NE)
        conv_w = part_of["conv_w"].rearrange("p (h k) -> p h k", h=NH)
        convbh = sb("convbh", [P, NH])
        taps = sb("taps", [P, NH, KC])
        Wx = sb("Wx", [P, NH, C_AT + NS])
        Ae = sb("Ae", [P, NH, NS])
        A = sb("A", [P, NH, NS])
        Wo = sb("Wo", [P, NH, P])
        Wog = sb("Wog", [P, NB, NH, P])
        W9 = sb("W9", [P, (NE + 1) * P])
        b9 = sb("b9", [W9_AT + NE + 1, P])
        M = sb("M", [P, NE, P])
        c_sb = sb("c_sb", [P, NB])
        c_th = sb("c_th", [P, NB])
        c_h = sb("c_h", [P, NB])
        c_s = sb("c_s", [P, NB])
        wm = sb("wm", [P, 6, P])
        mod = sb("mod", [P, 4, NB])
        mod1 = sb("mod1", [P, 4, NB])
        gate = sb("gate", [P, NB, 2, P])
        ident = sb("ident", [P, P])
        sel = sb("sel", [P, NS + 1], BF16)
        selE = sb("selE", [P, NE], BF16)
        x_sb = sb("x_sb", [P, NB, NT, P])
        stats = sb("stats", [P, 2, NT, 6])
        mv = sb("mv", [P, 2, NT, 2])
        lnv = sb("lnv", [P, 2, NT])
        rstd = sb("rstd", [P, 2, NT])
        shift = sb("shift", [P, 2, NT])
        xn = sb("xn", [P, 2, NT, P])
        hT = sb("hT", [P, 2, T])
        h2T = sb("h2T", [P, NB, T])
        xch = sb("xch", [P, NH, T])
        th = sb("th", [P, NH, T])
        xconv = sb("xconv", [P, 2, NH, T])
        zz = sb("zz", [P, 2, NH, T])
        hi = sb("hi", [P, T], BF16)
        mid = sb("mid", [P, T], BF16)
        parts = sb("parts", [P, 2, T], BF16)
        dexp = sb("dexp", [P, NH, T])
        drel = sb("drel", [P, NH, T])
        dlog = sb("dlog", [P, NH, T])
        dw1 = sb("dw1", [P, NH, T])
        delta = sb("delta", [P, 2, NH, T])
        dx = sb("dx", [P, 2, NH, T])
        dA = sb("dA", [P, ND, NH, T])
        dBx = sb("dBx", [P, NX, NH, T])
        hs = sb("hs", [P, NHB, NH, T])
        prod = sb("prod", [P, NPB, NH, T])
        rest_C = sb("rest_C", [C_AT + NS, T])
        rest = rest_C[0:NPART, :]
        C_rows = rest_C[C_AT:, :]
        C_sb = sb("C_sb", [P, NC, T])
        y2 = sb("y2", [P, NH, T])
        r2 = sb("r2", [P, NB, NT, NE])
        r2c = sb("r2c", [P, NT, NE])
        lr = sb("lr", [P, NT, NE])
        res = sb("res", [P, NT, NE])
        rmin = sb("rmin", [P, NT])
        gd = sb("gd", [P, NT, NE])
        ge = sb("ge", [P, NT, NE])
        gs = sb("gs", [P, NT])
        gr = sb("gr", [P, NT])
        rw = sb("rw", [P, NT, NE])
        msk = sb("msk", [P, NB, NT, NE])
        passing = sb("passing", [P, 1])
        flag = sb("flag", [1, 1], mybir.dt.int32)
        lt = sb("lt", [P, NT, NE, NE])
        eq = sb("eq", [P, NT, NE, NE])
        rank = sb("rank", [P, NB, NT, NE])
        keep = sb("keep", [P, NT, NE])
        fw = sb("fw", [P, NT, NE])
        sw = sb("sw", [P, NT])
        swz = sb("swz", [P, NT])
        rsw = sb("rsw", [P, NT])
        w_hi = sb("w_hi", [P, NT, NE], BF16)
        w_rest = sb("w_rest", [P, NT, NE])
        w_mid = sb("w_mid", [P, NT, NE], BF16)
        w41 = sb("w41", [P, NT, W9_AT + NE + 1])
        wTp = sb("wTp", [NP3 * NE, T], BF16)
        wT9_all = sb("wT9_all", [P, T])
        wT9 = wT9_all[0:W9_AT + NE + 1, :]
        wh = sb("wh", [P, NW, T])
        V = wh[0:RV, 0:NE * P // T].rearrange("r w (e i) -> r (w e) i", i=P)
        graw = wT9_all
        acc = sb("acc", [P, NT, P])
        gsgn = acc[:, :, :].rearrange("p j o -> p (j o)")

        Bps = [ps(f"Bps{i}", [P, T]) for i in range(2)]
        Yps = ps("Yps", [P, NH, T])
        Ops = ps("Ops", [P, T])
        G = [ps(f"G{i}", [P, T]) for i in range(NG)]
        block = ctx.enter_context(nc.Block())

        last_s = NB * NS - 1

        loads = [
            (x_sb[:, 0], x[0].rearrange("(j p) i -> p j i", p=P), x_in[0]), (c_sb[:, :], cT, c_in),
            (wm[:, :, :], wmod.rearrange("k (m n) -> k m n", m=6), wm_in), (ident[:, :], eye, ident_in),
            (small[:, :], smalls, small_in), (Win[:, :], W_in, win_in), (Wx[:, :, :], W_x, wx_in),
            (x_sb[:, 1], x[1].rearrange("(j p) i -> p j i", p=P), x_in[1]),
            (Wo[:, :, :], W_out, wo_in), (V[:, :, :], VgT, v_in),
            (W9[:, :], We_Wp, w9_in), (b9[W9_AT:, :], be_bp, b9_in),
            (x_sb[:, 2], x[2].rearrange("(j p) i -> p j i", p=P), x_in[2]),
            (x_sb[:, 3], x[3].rearrange("(j p) i -> p j i", p=P), x_in[3]),
        ]
        @block.sync
        def _(sp):
            for dst, src, landed in loads:
                sp.dma_start(dst, src).then_inc(landed, 16)
            def load_C(s):
                sp.wait_ge(C_stored, 16 * (s // NS + 1))
                if s >= NC:
                    sp.wait_ge(prod_ready, s - NC + 1)
                sp.dma_start(C_sb[:, s % NC], C_dram[s // NS, s % NS].partition_broadcast(P)
                             ).then_inc(C_in[s % NC], 16)

            def piece(name, q):
                if name == "sp_c":
                    sp.wait_ge(C_rows_ready, q + 1)
                    sp.dma_start(C_dram[q], C_rows).then_inc(C_stored, 16)
                elif name == "first":
                    for s in range(C_AHEAD):
                        load_C(s)
                elif name == "scan":
                    if q + C_AHEAD <= last_s:
                        load_C(q + C_AHEAD)
                elif name == "sp_out":
                    sp.wait_ge(out_ready, q + 1)
                    sp.dma_start(out[q % NB].rearrange("(j p) i -> p j i", p=P), x_sb[:, q % NB]).then_inc(stored, 16)

            for name, q in order:
                piece(name, q)
            sp.wait_ge(stored, 16 * NB)
            sp.wait_ge(flag_ready, 1)
            with sp.If(sp.value_load(flag[:, :]) == 0):
                for name, q in unmasked:
                    piece(name, q)
                sp.wait_ge(stored, 2 * 16 * NB)

        def soft_sum(eng, q, h):
            k = NH * q + h
            eng.wait_ge(dcor_ready, k + 1)
            eng.wait_ge(dlog_ready, k + 1)
            eng.tensor_tensor(dlog[:, h], dlog[:, h], dw1[:, h], ALU.subtract).then_inc(dsum_ready, 1)

        def soft_add(eng, q, h):
            k = NH * q + h
            eng.wait_ge(dsum_ready, k + 1)
            eng.wait_ge(softin_ready, k + 1)
            if q >= 2:
                eng.wait_ge(dA_ready, NS * (q - 1))
            eng.tensor_tensor(delta[:, q % 2, h], dlog[:, h], drel[:, h], ALU.add).then_inc(delta_ready, 1)

        def gate_z(eng, q, h):
            k = NH * q + h
            eng.wait_ge(y_ready, k + 1)
            eng.wait_ge(zgate_ready, k + 1)
            if q > 0:
                eng.wait_ge(wout_done, q)
            eng.tensor_tensor(y2[:, h], y2[:, h], zz[:, q % 2, h], ALU.mult).then_inc(yg_ready, 1)

        def split_w(eng, q):
            w = w41[:, :, W9_AT:W9_AT + NE]
            eng.wait_ge(w_ready, q + 1)
            eng.tensor_copy(w_hi[:, :, :], w).then_inc(w_hi_ready, 1)
            eng.wait_ge(w_hi_ready, q + 1)
            eng.tensor_copy(w41[:, :, 0:NE], w_hi[:, :, :]).then_inc(w_part0, 1)
            eng.tensor_tensor(w_rest[:, :, :], w, w_hi[:, :, :], ALU.subtract).then_inc(w_rest_ready, 1)
            eng.wait_ge(w_rest_ready, q + 1)
            eng.tensor_copy(w_mid[:, :, :], w_rest[:, :, :]).then_inc(w_mid_ready, 1)
            eng.wait_ge(w_mid_ready, q + 1)
            eng.tensor_copy(w41[:, :, NE:2 * NE], w_mid[:, :, :]).then_inc(w_part1, 1)
            eng.tensor_tensor(w41[:, :, 2 * NE:3 * NE], w_rest[:, :, :], w_mid[:, :, :], ALU.subtract
                              ).then_inc(w_parts_ready, 1)

        def delta_x(eng, q, h):
            k = NH * q + h
            eng.wait_ge(delta_ready, k + 1)
            eng.wait_ge(xconv_ready, k + 1)
            if q >= 2:
                eng.wait_ge(dBx_ready, NS * (q - 1))
            eng.tensor_tensor(dx[:, q % 2, h], delta[:, q % 2, h], xconv[:, q % 2, h], ALU.mult).then_inc(dx_ready, 1)

        @block.gpsimd
        def _(pool):
            pool.memset(w41[:, :, :], 0.0).then_inc(w41_clear, 1)
            pool.wait_ge(w41_clear, 1)
            pool.memset(w41[:, :, W9_AT + NE:], 1.0).then_inc(w41_one, 1)
            for i in range(ND):
                pool.memset(dA[:, i, :, 0:1], 0.0).then_inc(reset_ready, 1)
            pool.wait_ge(small_in, 16)
            pool.tensor_copy(sel[:, :], selc).then_inc(sel_ready, 1)
            pool.tensor_copy(selE[:, :], part_of["selE"]).then_inc(sel_ready, 1)
            pool.wait_ge(wo_in, 16)
            pool.tensor_scalar(Wo[:, :, :], Wo[:, :, :], 0.5, 1.0, ALU.mult, ALU.mult).then_inc(Woh_ready, 1)

            def piece(name, q):
                if name == "scan":
                    s = q
                    pool.wait_ge(scan_done, s + 1)
                    pool.wait_ge(C_in[s % NC], 16 * (s // NC + 1))
                    if s >= NPB:
                        pool.wait_ge(nsum_done, s - NPB + 1)
                    pool.tensor_tensor(prod[:, s % NPB], hs[:, s % NHB],
                                       C_sb[:, s % NC].unsqueeze(1).to_broadcast([P, NH, T]),
                                       ALU.mult).then_inc(prod_ready, 1)
                elif name == "pool_wog":
                    pool.wait_ge(gates_ready, 2)
                    pool.wait_ge(Woh_ready, 1)
                    for b in range(NB):
                        pool.tensor_tensor(Wog[:, b], Wo[:, :, :],
                                           gate[:, b, 0].unsqueeze(1).to_broadcast([P, NH, P]),
                                           ALU.mult).then_inc(Wog_ready, 1)
                elif name[:-1] == "soft_sum" and q > 0:
                    soft_sum(pool, q, int(name[-1]))
                elif name[:-1] == "soft_add" and q > 0:
                    soft_add(pool, q, int(name[-1]))
                elif name[:-1] == "delta_x" and q > 0:
                    delta_x(pool, q, int(name[-1]))
                elif name in ("gate_z0", "gate_z1") and q < NB - 1:
                    gate_z(pool, q, int(name[-1]))
                elif name == "split_w" and q < NB - 1:
                    split_w(pool, q)
                elif name == "pool_out":
                    pool.wait_ge(acc_ready, q + 1)
                    if q >= NB:
                        pool.wait_ge(stored, 16 * q)
                    pool.tensor_tensor(x_sb[:, q % NB], acc[:, :, :], x_sb[:, q % NB], ALU.add).then_inc(out_ready, 1)

            for name, q in order:
                piece(name, q)
            pool.wait_ge(flag_ready, 1)
            with pool.If(pool.value_load(flag[:, :]) == 0):
                for name, q in unmasked:
                    piece(name, q)

        @block.scalar
        def _(act):
            act.preload_act_table_set("natural_log_exp_and_others")
            act.wait_ge(c_in, 16)
            act.activation(c_th[:, :], c_sb[:, :], ACT.Exp, scale=-1.0).then_inc(cth_ready, 1)
            act.wait_ge(small_in, 16)
            act.activation(convbh[:, :], convb[:, :], ACT.Copy, scale=0.5).then_inc(convbh_ready, 1)
            act.activation(Ae[:, :, :], Al[:, :, :], ACT.Exp).then_inc(Ae_ready, 1)

            def exps(s):
                q, n = divmod(s, NS)
                act.wait_ge(A_ready, 1)
                act.wait_ge(reset_ready, ND)
                if s >= ND:
                    act.wait_ge(scan_done, s - ND + 1)
                for h in range(NH):
                    act.wait_ge(delta_ready, NH * q + h + 1)
                    act.activation(dA[:, s % ND, h, 1:T], delta[:, q % 2, h, 1:T], ACT.Exp,
                                   scale=A[:, h, n:n + 1]).then_inc(dA_half if h == 0 else dA_ready, 1)

            def norm_of(which, q):
                act.wait_ge(shift_ready[which], q + 1)
                if q > 0:
                    act.wait_ge(normT_done[which], q)
                for j in range(NT):
                    act.activation(xn[:, which, j], x_sb[:, q, j], ACT.Identity, scale=rstd[:, which, j:j + 1],
                                   bias=shift[:, which, j:j + 1]).then_inc(xn_ready[which], 1)

            def rstd_of(which, q):
                act.wait_ge(stats_ready[which], NT * (q + 1))
                if q > 0:
                    act.wait_ge(rstd_ready[which], q)
                act.activation(lnv[:, which], mv[:, which, :, 1], ACT.Ln, bias=low[:, 2:3]).then_inc(lnv_ready[which], 1)
                act.wait_ge(lnv_ready[which], q + 1)
                if q > 0:
                    act.wait_ge(xn_ready[which], NT * q)
                act.activation(rstd[:, which], lnv[:, which], ACT.Exp, scale=-0.5).then_inc(rstd_ready[which], 1)

            def piece(name, q):
                g = banks.get(("pe_" + name[4:], q)) if name.startswith("act_") else None
                if name == "first":
                    for s in range(AHEAD):
                        exps(s)
                elif name == "scan":
                    if q + AHEAD <= last_s:
                        exps(q + AHEAD)
                elif name == "modulate":
                    act.wait_ge(mod_done, 1)
                    act.copy(mod[:, :, :], Yps[:, 0, 0:16].rearrange("p (k b) -> p k b", k=4)).then_inc(mod_ready, 1)
                    act.activation(mod1[:, :, :], Yps[:, 0, 0:16].rearrange("p (k b) -> p k b", k=4), ACT.Identity,
                                   bias=1.0).then_inc(mod_ready, 1)
                elif name == "act_xn1":
                    norm_of(0, q)
                elif name == "act_xn2":
                    norm_of(1, q)
                elif name == "act_rstd1":
                    rstd_of(0, q)
                elif name == "act_rstd2":
                    rstd_of(1, q)
                elif name == "act_hT":
                    g = banks[("pe_xT", q)]
                    act.wait_ge(xT_done, q + 1)
                    act.wait_ge(mod_ready, 2)
                    if q >= 2:
                        act.wait_ge(x_done, 2 * (q - 1))
                        act.wait_ge(z_done, 2 * (q - 1))
                    act.activation(hT[:, q % 2], G[g[0][0]][:, :], ACT.Identity, scale=mod1[:, 1, q:q + 1],
                                   bias=mod[:, 0, q:q + 1]).then_inc(hT_ready, 1)
                elif name == "act_h2T":
                    g = banks[("pe_xT2", q)]
                    act.wait_ge(xT2_done, q + 1)
                    act.activation(h2T[:, q], G[g[0][0]][:, :], ACT.Identity, scale=mod1[:, 3, q:q + 1],
                                   bias=mod[:, 2, q:q + 1]).then_inc(h2T_ready, 1)
                elif name in ("act_x0", "act_x1"):
                    h = int(name[-1])
                    k = 2 * q + h
                    act.wait_ge(x_done, k + 1)
                    act.wait_ge(taps_ready, 1)
                    act.wait_ge(convbh_ready, 1)
                    if k >= 2:
                        act.wait_ge(xconv_ready, k - 1)
                    act.activation(xch[:, h], G[g[0][0]][:, :], ACT.Identity, scale=taps[:, h, KC - 1:KC],
                                   bias=convbh[:, h:h + 1]).then_inc(xin_ready, 1)
                elif name in ("act_t0", "act_t1"):
                    h = int(name[-1])
                    k = 2 * q + h
                    act.wait_ge(conv_done, k + 1)
                    if k >= 2:
                        act.wait_ge(zgate_ready, k - 1)
                    act.activation(th[:, h], xch[:, h], ACT.Tanh).then_inc(xth_ready, 1)
                elif name in ("act_z0", "act_z1"):
                    h = int(name[-1])
                    k = 2 * q + h
                    act.wait_ge(z_done, k + 1)
                    act.wait_ge(xconv_ready, k + 1)
                    act.activation(th[:, h], G[g[0][0]][:, :], ACT.Tanh, scale=0.5).then_inc(zth_ready, 1)
                    if h == NH - 1:
                        act.preload_act_table_set("natural_log_exp_and_others")
                elif name == "act_hi":
                    g = banks[("pe_ssm", q)]
                    act.wait_ge(ssm_done, q + 1)
                    if q > 0:
                        act.wait_ge(rest_ready, q)
                    act.copy(hi[0:NPART, :], G[g[0][0]][0:NPART, :]).then_inc(hi_ready, 1)
                elif name == "act_C":
                    if q > 0:
                        act.wait_ge(C_stored, 16 * q)
                    act.wait_ge(ssm_done, q + 1)
                    act.copy(C_rows, G[banks[("pe_ssm", q)][0][0]][C_AT:C_AT + NS, :]).then_inc(C_rows_ready, 1)
                elif name == "act_mid":
                    act.wait_ge(rest_ready, q + 1)
                    if q > 0:
                        act.wait_ge(parts_ready, q)
                    act.copy(mid[0:NPART, :], rest).then_inc(mid_ready, 1)
                elif name in ("act_soft0", "act_soft1"):
                    h = int(name[-1])
                    k = NH * q + h
                    g = G[banks[("pe_delta", q)][0][0]]
                    act.wait_ge(delta_done, q + 1)
                    if q > 0:
                        act.wait_ge(dcor_ready, k + 1 - NH)
                    act.activation(dexp[:, h], g[:, :], ACT.Abs, scale=dtw[:, h:h + 1],
                                   bias=dtb[:, h:h + 1]).then_inc(dabs_ready, 1)
                    act.wait_ge(dabs_ready, k + 1)
                    act.activation(dexp[:, h], dexp[:, h], ACT.Exp, scale=-1.0).then_inc(dexp_ready, 1)
                    if q > 0:
                        act.wait_ge(delta_ready, k + 1 - NH)
                    act.wait_ge(dexp_ready, k + 1)
                    if q > 0:
                        act.wait_ge(dsum_ready, k + 1 - NH)
                        act.activation(dw1[:, h], dexp[:, h], ACT.Identity, bias=1.0).then_inc(dw1_ready, 1)
                    act.activation(dlog[:, h], dexp[:, h], ACT.Ln, bias=1.0).then_inc(dlog_ready, 1)
                    act.activation(drel[:, h], g[:, :], ACT.Relu, scale=dtw[:, h:h + 1], bias=dtb[:, h:h + 1]
                                   ).then_inc(softin_ready, 1)
                elif name[:5] == "sq_ra":
                    j = int(name[-1])
                    k = NT * q + j
                    g = G[banks[(f"pe_ra{j}", q)][0][0]]
                    act.wait_ge(ra_done, k + 1)
                    for e in range(NE // 2):
                        act.activation(g[:, e * P:(e + 1) * P], g[:, e * P:(e + 1) * P], ACT.Square,
                                       accum_out=r2[:, q, j, e:e + 1]
                                       ).then_inc(sqa_some if e < NE // 2 - 1 else sqa_done, 1)
                elif name[:5] == "sq_rb" and (q < NB - 1 or name == SQ_LAST):
                    j = int(name[-1])
                    k = NT * q + j
                    g = G[banks[(f"pe_rb{j}", q)][0][0]]
                    act.wait_ge(rb_done, k + 1)
                    for e in range(NE // 2):
                        act.activation(g[:, e * P:(e + 1) * P], g[:, e * P:(e + 1) * P], ACT.Square,
                                       accum_out=r2[:, q, j, NE // 2 + e:NE // 2 + e + 1]
                                       ).then_inc(sqb_some if e < NE // 2 - 1 else sqb_done, 1)
                elif name == "act_sqrt":
                    act.wait_ge(clamp_ready, q + 1)
                    if q > 0:
                        act.wait_ge(res_ready, q)
                    act.activation(lr[:, :, :], r2c[:, :, :], ACT.Ln).then_inc(lr_ready, 1)
                    act.wait_ge(lr_ready, q + 1)
                    if q > 0:
                        act.wait_ge(gd_ready, q)
                    act.activation(res[:, :, :], lr[:, :, :], ACT.Exp, scale=0.5).then_inc(res_ready, 1)
                elif name == "act_gexp":
                    act.wait_ge(gd_ready, q + 1)
                    if q > 0:
                        act.wait_ge(rw_ready, q)
                    act.activation(ge[:, :, :], gd[:, :, :], ACT.Exp).then_inc(ge_ready, 1)
                elif name == "act_wT":
                    g = G[g[0][0]]
                    act.wait_ge(wT_done, q + 1)
                    if q > 0:
                        act.wait_ge(b_done, NE * q)
                        act.wait_ge(bias_done, q)
                    act.copy(wTp[:, :], g[0:NP3 * NE, :]).then_inc(wTp_ready, 1)
                    act.copy(wT9[W9_AT:, :], g[W9_AT:W9_AT + NE + 1, :]).then_inc(wT_ready, 1)

            for name, q in order:
                piece(name, q)
            act.wait_ge(flag_ready, 1)
            with act.If(act.value_load(flag[:, :]) == 0):
                for name, q in unmasked:
                    piece(name, q)

        @block.vector
        def _(vec):
            vec.wait_ge(c_in, 16)
            vec.wait_ge(cth_ready, 1)
            vec.tensor_scalar(c_h[:, :], c_th[:, :], 1.0, None, ALU.add).then_inc(ch_ready, 1)
            vec.wait_ge(ch_ready, 1)
            vec.reciprocal(c_th[:, :], c_h[:, :]).then_inc(csig_ready, 1)
            vec.wait_ge(csig_ready, 1)
            vec.tensor_tensor(c_s[:, :], c_th[:, :], c_sb[:, :], ALU.mult).then_inc(cs_ready, 1)
            vec.wait_ge(small_in, 16)
            vec.tensor_scalar(taps[:, :, :], conv_w, 0.5, None, ALU.mult).then_inc(taps_ready, 1)
            vec.wait_ge(Ae_ready, 1)
            vec.tensor_scalar(A[:, :, :], Ae[:, :, :], -1.0, None, ALU.mult).then_inc(A_ready, 1)

            def dbx(s):
                q = s // NS
                vec.wait_ge(Bps_ready, s + 1)
                vec.wait_ge(dx_ready, NH * (q + 1))
                if s >= NX:
                    vec.wait_ge(scan_done, s - NX + 1)
                vec.tensor_tensor(dBx[:, s % NX], dx[:, q % 2], Bps[s % 2][:, :].unsqueeze(1).to_broadcast([P, NH, T]),
                                  ALU.mult).then_inc(dBx_ready, 1)

            def stats_of(which, q, src):
                if q > 0:
                    vec.wait_ge(bn_ready[which], NT * q)
                    vec.wait_ge(stats_ready[which], NT * q)
                for j in range(NT):
                    vec.bn_stats(stats[:, which, j], src[:, q, j]).then_inc(bn_ready[which], 1)
                if q > 0:
                    vec.wait_ge(rstd_ready[which], q)
                    vec.wait_ge(xn_ready[which], NT * q)
                for j in range(NT):
                    vec.wait_ge(bn_ready[which], NT * q + j + 1)
                    vec.bn_aggr(mv[:, which, j], stats[:, which, j]).then_inc(stats_ready[which], 1)

            def shift_of(which, q):
                vec.wait_ge(rstd_ready[which], q + 1)
                vec.wait_ge(stats_ready[which], NT * (q + 1))
                if q > 0:
                    vec.wait_ge(xn_ready[which], NT * q)
                vec.scalar_tensor_tensor(shift[:, which], mv[:, which, :, 0], -1.0, rstd[:, which], ALU.mult, ALU.mult
                                         ).then_inc(shift_ready[which], 1)

            def piece(name, q):
                if name == "first":
                    for s in range(AHEAD):
                        dbx(s)
                elif name == "scan":
                    s = q
                    if s + AHEAD <= last_s:
                        dbx(s + AHEAD)
                    vec.wait_ge(dA_ready, s + 1)
                    vec.wait_ge(dBx_ready, s + 1)
                    if s >= NHB:
                        vec.wait_ge(prod_ready, s - NHB + 1)
                    vec.tensor_tensor_scan(hs[:, s % NHB].rearrange("p h t -> p (h t)"),
                                           dA[:, s % ND].rearrange("p h t -> p (h t)"),
                                           dBx[:, s % NX].rearrange("p h t -> p (h t)"), 0.0,
                                           ALU.mult, ALU.add).then_inc(scan_done, 1)
                elif name == "vec_ln1":
                    vec.wait_ge(x_in[q], 16)
                    stats_of(0, q, x_sb)
                elif name == "vec_shift1":
                    shift_of(0, q)
                elif name == "vec_shift2":
                    shift_of(1, q)
                elif name in ("vec_c0", "vec_c1"):
                    h = int(name[-1])
                    k = 2 * q + h
                    g = G[banks[("pe_x%d" % h, q)][0][0]]
                    vec.wait_ge(xin_ready, k + 1)
                    for i in range(1, KC):
                        if k > 0 or i > 1:
                            vec.wait_ge(tap_done, 2 * k + i - 1)
                        vec.scalar_tensor_tensor(xch[:, h, i:], g[:, :T - i], taps[:, h, KC - 1 - i:KC - i],
                                                 xch[:, h, i:], ALU.mult, ALU.add
                                                 ).then_inc(tap_done if i < KC - 1 else conv_done, 1)
                elif name in ("vec_x0", "vec_x1"):
                    h = int(name[-1])
                    k = 2 * q + h
                    vec.wait_ge(xth_ready, k + 1)
                    if q >= 2:
                        vec.wait_ge(y_ready, 2 * (q - 1))
                        vec.wait_ge(dx_ready, NH * (q - 1))
                    vec.scalar_tensor_tensor(xconv[:, q % 2, h], th[:, h], 1.0, xch[:, h], ALU.add,
                                             ALU.mult).then_inc(xconv_ready, 1)
                elif name in ("vec_z0", "vec_z1"):
                    h = int(name[-1])
                    k = 2 * q + h
                    g = banks[("pe_" + name[4:], q)]
                    vec.wait_ge(zth_ready, k + 1)
                    if q >= 2:
                        vec.wait_ge(yg_ready, NH * (q - 1))
                    vec.scalar_tensor_tensor(zz[:, q % 2, h], th[:, h], 1.0, G[g[0][0]][:, :], ALU.add,
                                             ALU.mult).then_inc(zgate_ready, 1)
                elif name == "vec_u":
                    g = banks[("pe_ssm", q)]
                    vec.wait_ge(hi_ready, q + 1)
                    vec.wait_ge(C_rows_ready, q + 1)
                    if q > 0:
                        vec.wait_ge(mid_ready, q)
                        vec.wait_ge(parts_ready, q)
                    vec.scalar_tensor_tensor(rest, hi[0:NPART, :], low[0:NPART, 0:1],
                                             G[g[0][0]][0:NPART, :], ALU.mult, ALU.add).then_inc(rest_ready, 1)
                elif name == "vec_parts":
                    vec.wait_ge(mid_ready, q + 1)
                    if q >= 2:
                        vec.wait_ge(Bps_ready, NS * (q - 1))
                        vec.wait_ge(delta_done, q - 1)
                    vec.scalar_tensor_tensor(parts[0:NPART, q % 2], mid[0:NPART, :], low[0:NPART, 1:2],
                                             rest, ALU.mult, ALU.add).then_inc(parts_ready, 1)
                elif name in ("vec_soft0", "vec_soft1"):
                    h = int(name[-1])
                    k = NH * q + h
                    if q == 0:
                        vec.wait_ge(dexp_ready, k + 1)
                        vec.tensor_scalar(dw1[:, h], dexp[:, h], 1.0, None, ALU.add).then_inc(dw1_ready, 1)
                    vec.wait_ge(dw1_ready, k + 1)
                    vec.scalar_tensor_tensor(dw1[:, h], dw1[:, h], -1.0, dexp[:, h], ALU.add, ALU.subtract
                                             ).then_inc(dcor_ready, 1)
                elif name[:-1] == "soft_sum" and q == 0:
                    soft_sum(vec, q, int(name[-1]))
                elif name[:-1] == "soft_add" and q == 0:
                    soft_add(vec, q, int(name[-1]))
                elif name[:-1] == "delta_x" and q == 0:
                    delta_x(vec, q, int(name[-1]))
                elif name == "vec_gates":
                    for i in range(2):
                        b = banks[(f"pe_gate{i}", 0)][0][0]
                        vec.wait_ge(gate_done, i + 1)
                        if i > 0:
                            vec.wait_ge(gates_ready, i)
                        vec.tensor_copy(graw[:, :], G[b][:, :]).then_inc(gates_read, 1)
                        vec.wait_ge(gates_read, i + 1)
                        vec.tensor_scalar(gsgn, graw[:, :], 0.0, 2.0, ALU.is_ge, ALU.mult).then_inc(gsgn_twice, 1)
                        vec.wait_ge(gsgn_twice, i + 1)
                        vec.tensor_scalar(gsgn, gsgn, -1.0, None, ALU.add).then_inc(gsgn_ready, 1)
                        vec.wait_ge(gsgn_ready, i + 1)
                        vec.tensor_tensor(graw[:, :], gsgn, graw[:, :], ALU.mult).then_inc(gabs_ready, 1)
                        vec.wait_ge(gabs_ready, i + 1)
                        vec.scalar_tensor_tensor(gate[:, 2 * i:2 * i + 2].rearrange("p b k o -> p (b k o)"), graw[:, :], 0.25,
                                                 gsgn, ALU.max, ALU.mult).then_inc(gates_ready, 1)
                elif name == "vec_V":
                    for i in range(2):
                        b = banks[(f"pe_V{i}", 0)][0][0]
                        vec.wait_ge(V_done, i + 1)
                        vec.tensor_tensor(M[:, 4 * i:4 * i + 4], ident[:, :].unsqueeze(1).to_broadcast([P, 4, P]),
                                          G[b][:, :].rearrange("p (e i) -> p e i", e=4), ALU.subtract
                                          ).then_inc(M_ready, 1)
                elif name in ("vec_y0", "vec_y1"):
                    h = int(name[-1])
                    vec.wait_ge(nsum_done, NS * (q + 1))
                    if q > 0:
                        vec.wait_ge(wout_done, q)
                    vec.scalar_tensor_tensor(y2[:, h], xconv[:, q % 2, h], Dsk[:, h:h + 1], Yps[:, h], ALU.mult,
                                             ALU.add).then_inc(y_ready, 1)
                elif name in ("gate_z0", "gate_z1") and q == NB - 1:
                    gate_z(vec, q, int(name[-1]))
                elif name == "vec_x2":
                    g = banks[("pe_wout", q)]
                    vec.wait_ge(wout_done, q + 1)
                    vec.tensor_tensor(x_sb[:, q], G[g[0][0]][:, :].rearrange("p (j o) -> p j o", j=NT), x_sb[:, q],
                                      ALU.add).then_inc(x2_ready, 1)
                    vec.wait_ge(x2_ready, q + 1)
                    stats_of(1, q, x_sb)
                elif name[:5] == "sq_rb" and q == NB - 1 and name != SQ_LAST:
                    j = int(name[-1])
                    k = NT * q + j
                    g = G[banks[(f"pe_rb{j}", q)][0][0]]
                    vec.wait_ge(rb_done, k + 1)
                    vec.wait_ge(wout_done, NB)
                    if j >= 2:
                        vec.wait_ge(sqb_done, k - 1)
                    vec.tensor_copy(y2[:, j % 2], g[:, :]).then_inc(resid_copied, 1)
                    vec.wait_ge(resid_copied, j + 1)
                    for e in range(NE // 2):
                        vec.scalar_tensor_tensor(g[:, e * P:(e + 1) * P], y2[:, j % 2, e * P:(e + 1) * P], 1.0,
                                                 g[:, e * P:(e + 1) * P], ALU.mult, ALU.mult,
                                                 accum_out=r2[:, q, j, NE // 2 + e:NE // 2 + e + 1]
                                                 ).then_inc(sqb_some if e < NE // 2 - 1 else sqb_done, 1)
                elif name == "vec_clamp":
                    vec.wait_ge(sqa_done, NT * (q + 1))
                    vec.wait_ge(sqb_done, NT * (q + 1))
                    if q > 0:
                        vec.wait_ge(lr_ready, q)
                    vec.tensor_scalar(r2c[:, :, :], r2[:, q], 1e-18, None, ALU.max).then_inc(clamp_ready, 1)
                elif name == "vec_gate1":
                    vec.wait_ge(res_ready, q + 1)
                    if q > 0:
                        vec.wait_ge(gd_ready, q)
                    vec.tensor_reduce(rmin[:, :], res[:, :, :], AX, ALU.min).then_inc(rmin_ready, 1)
                    vec.wait_ge(rmin_ready, q + 1)
                    if q > 0:
                        vec.wait_ge(ge_ready, q)
                    vec.tensor_tensor(gd[:, :, :], rmin[:, :].unsqueeze(2).to_broadcast([P, NT, NE]), res[:, :, :],
                                      ALU.subtract).then_inc(gd_ready, 1)
                elif name == "vec_ranka":
                    ve = r2[:, q].unsqueeze(3).to_broadcast([P, NT, NE, NE])
                    vf = r2[:, q].unsqueeze(2).to_broadcast([P, NT, NE, NE])
                    vec.wait_ge(sqa_done, NT * (q + 1))
                    vec.wait_ge(sqb_done, NT * (q + 1))
                    if q > 0:
                        vec.wait_ge(rank_ready, q)
                        vec.wait_ge(cnt_ready, q)
                    vec.tensor_tensor(lt[:, :, :, :], vf, ve, ALU.is_lt).then_inc(lt_ready, 1)
                    vec.tensor_tensor(eq[:, :, :, :], vf, ve, ALU.is_equal).then_inc(eq_ready, 1)
                    vec.wait_ge(eq_ready, q + 1)
                    vec.tensor_tensor(eq[:, :, :, :].rearrange("p j e f -> p j (e f)"),
                                       eq[:, :, :, :].rearrange("p j e f -> p j (e f)"),
                                       tri[:, :, :].rearrange("p e f -> p (e f)").unsqueeze(1).to_broadcast([P, NT, NE * NE]),
                                       ALU.mult).then_inc(eql_ready, 1)
                elif name == "vec_rankb":
                    vec.wait_ge(eql_ready, q + 1)
                    vec.wait_ge(lt_ready, q + 1)
                    vec.tensor_tensor(lt[:, :, :, :], lt[:, :, :, :], eq[:, :, :, :], ALU.add).then_inc(cnt_ready, 1)
                    vec.wait_ge(cnt_ready, q + 1)
                    if q > 0:
                        vec.wait_ge(keep_ready, q)
                    vec.tensor_reduce(rank[:, q], lt[:, :, :, :], AX, ALU.add).then_inc(rank_ready, 1)
                elif name == "vec_gate2":
                    vec.wait_ge(ge_ready, q + 1)
                    if q > 0:
                        vec.wait_ge(w_ready, q)
                    vec.tensor_reduce(gs[:, :], ge[:, :, :], AX, ALU.add).then_inc(gs_ready, 1)
                    vec.wait_ge(gs_ready, q + 1)
                    vec.reciprocal(gr[:, :], gs[:, :]).then_inc(gr_ready, 1)
                    vec.wait_ge(gr_ready, q + 1)
                    vec.tensor_tensor(rw[:, :, :], ge[:, :, :], gr[:, :].unsqueeze(2).to_broadcast([P, NT, NE]),
                                      ALU.mult).then_inc(rw_ready, 1)
                    vec.wait_ge(rw_ready, q + 1)
                    vec.tensor_scalar(msk[:, q], rw[:, :, :], 1.0 / NE, None, ALU.is_gt).then_inc(msk_ready, 1)
                    vec.wait_ge(msk_ready, q + 1)
                    vec.wait_ge(rank_ready, q + 1)
                    vec.scalar_tensor_tensor(keep[:, :, :], rank[:, q], 2.0, msk[:, q], ALU.is_lt,
                                             ALU.mult).then_inc(keep_ready, 1)
                    vec.wait_ge(keep_ready, q + 1)
                    vec.tensor_tensor(fw[:, :, :], rw[:, :, :], keep[:, :, :], ALU.mult).then_inc(fw_ready, 1)
                    vec.wait_ge(fw_ready, q + 1)
                    vec.tensor_reduce(sw[:, :], fw[:, :, :], AX, ALU.add).then_inc(sw_ready, 1)
                    vec.wait_ge(sw_ready, q + 1)
                    vec.scalar_tensor_tensor(swz[:, :], sw[:, :], 0.0, sw[:, :], ALU.is_equal, ALU.add).then_inc(swz_ready, 1)
                    vec.wait_ge(swz_ready, q + 1)
                    vec.reciprocal(rsw[:, :], swz[:, :]).then_inc(rsw_ready, 1)
                    vec.wait_ge(rsw_ready, q + 1)
                    vec.wait_ge(w41_one, 1)
                    if q > 0:
                        vec.wait_ge(wT_done, q)
                    w = w41[:, :, W9_AT:W9_AT + NE]
                    vec.tensor_tensor(w, fw[:, :, :], rsw[:, :].unsqueeze(2).to_broadcast([P, NT, NE]),
                                      ALU.mult).then_inc(w_ready, 1)
                elif name == "split_w" and q == NB - 1:
                    split_w(vec, q)
                elif name == "vec_any":
                    vec.wait_ge(msk_ready, NB)
                    vec.tensor_reduce(passing[:, :], msk[:, :, :, :].rearrange("p b j e -> p (b j e)"), AX, ALU.max
                                      ).then_inc(passing_ready, 1)
                elif name == "vec_flag":
                    vec.wait_ge(any_done, 1)
                    vec.tensor_copy(flag[:, :], Yps[0:1, 0, 0:1]).then_inc(flag_ready, 1)
                elif name == "vec_top":
                    vec.wait_ge(wT_done, q)
                    vec.wait_ge(rank_ready, NB)
                    vec.tensor_scalar(w41[:, :, 0:NE], rank[:, q % NB], 1.0, None, ALU.is_lt).then_inc(w_part0, 1)
                    vec.memset(w41[:, :, NE:NP3 * NE], 0.0).then_inc(w_part1, 1)
                    vec.tensor_scalar(w41[:, :, W9_AT:W9_AT + NE], rank[:, q % NB], 1.0, None, ALU.is_lt
                                      ).then_inc(w_parts_ready, 1)
                elif name[:5] == "vec_h":
                    e = int(name[-1])
                    k = NE * q + e
                    bank = banks[(f"pe_b{e}", q)][0][0]
                    vec.wait_ge(b_done, k + 1)
                    if k >= NW:
                        vec.wait_ge(a_done, k - NW + 1)
                    vec.tensor_tensor(wh[:, (NE * q + e) % NW], h2T[:, q % NB], G[bank][:, :], ALU.mult).then_inc(wh_ready, 1)
                elif name == "vec_out":
                    vec.wait_ge(a_done, NE * (q + 1))
                    if q > 0:
                        vec.wait_ge(out_ready, q)
                    else:
                        vec.wait_ge(gates_ready, 2)
                    vec.tensor_tensor(acc[:, :, :], Ops[:, :].rearrange("p (j o) -> p j o", j=NT),
                                      gate[:, q % NB, 1].unsqueeze(1).to_broadcast([P, NT, P]), ALU.mult
                                      ).then_inc(acc_ready, 1)

            for name, q in order:
                piece(name, q)
            vec.wait_ge(flag_ready, 1)
            with vec.If(vec.value_load(flag[:, :]) == 0):
                for name, q in unmasked:
                    piece(name, q)

        @block.tensor
        def _(pe):
            def shared(name, q, i=0):
                bank, before = banks[(name, q)][i]
                if before is not None:
                    pe.wait_ge(*before)
                return G[bank]

            def bcast_B(s):
                q, n = divmod(s, NS)
                pe.wait_ge(parts_ready, q + 1)
                pe.wait_ge(sel_ready, 2)
                if s >= 2:
                    pe.wait_ge(dBx_ready, s - 1)
                pe.matmul(Bps[s % 2][:, :], sel[0:NPART, n:n + 1].to_broadcast([NPART, P]), parts[0:NPART, q % 2], start=True, stop=True
                          ).then_inc(Bps_ready, 1)

            def nsum(s):
                q, n = divmod(s, NS)
                pe.wait_ge(prod_ready, s + 1)
                if n == 0:
                    pe.wait_ge(mod_ready, 2)
                    if q > 0:
                        pe.wait_ge(y_ready, 2 * q)
                for h in range(NH):
                    mm = pe.matmul(Yps[:, h], ident[:, :], prod[:, s % NPB, h], start=(n == 0), stop=(n == NS - 1))
                mm.then_inc(nsum_done, 1)

            pe.wait_ge(wm_in, 16)
            pe.wait_ge(cs_ready, 1)
            for i, k in enumerate((0, 1, 3, 4)):
                mm = pe.matmul(Yps[:, 0, NB * i:NB * i + NB], wm[:, k], c_s[:, :], start=True, stop=True)
            mm.then_inc(mod_done, 1)
            pe.wait_ge(ident_in, 16)

            def piece(name, q):
                if name == "first":
                    for s in range(AHEAD):
                        bcast_B(s)
                elif name == "scan":
                    if q + AHEAD <= last_s:
                        bcast_B(q + AHEAD)
                    if q >= BEHIND:
                        nsum(q - BEHIND)
                elif name == "last":
                    for s in range(last_s - BEHIND + 1, last_s + 1):
                        nsum(s)
                elif name == "pe_xT":
                    g = shared(name, q)
                    for j in range(NT):
                        pe.wait_ge(xn_ready[0], NT * q + j + 1)
                        mm = pe.transpose(g[:, j * P:(j + 1) * P], xn[:, 0, j], ident[:, :])
                    mm.then_inc(xT_done, 1)
                elif name == "pe_xT2":
                    g = shared(name, q)
                    for j in range(NT):
                        pe.wait_ge(xn_ready[1], NT * q + j + 1)
                        mm = pe.transpose(g[:, j * P:(j + 1) * P], xn[:, 1, j], ident[:, :])
                    mm.then_inc(xT2_done, 1)
                elif name in ("pe_x0", "pe_x1"):
                    h = int(name[-1])
                    g = shared(name, q)
                    pe.wait_ge(hT_ready, q + 1)
                    pe.wait_ge(win_in, 16)
                    pe.matmul(g[:, :], Win[:, h * P:(h + 1) * P], hT[:, q % 2], start=True, stop=True).then_inc(x_done, 1)
                elif name in ("pe_z0", "pe_z1"):
                    h = int(name[-1])
                    g = shared(name, q)
                    pe.matmul(g[:, :], Win[:, DI + h * P:DI + (h + 1) * P], hT[:, q % 2], start=True, stop=True
                              ).then_inc(z_done, 1)
                elif name == "pe_ssm":
                    g = shared(name, q)
                    pe.wait_ge(wx_in, 16)
                    pe.wait_ge(xconv_ready, 2 * (q + 1))
                    for h in range(NH):
                        mm = pe.matmul(g[0:C_AT + NS, :], Wx[:, h], xconv[:, q % 2, h], start=(h == 0), stop=(h == NH - 1))
                    mm.then_inc(ssm_done, 1)
                elif name == "pe_delta":
                    g = shared(name, q)
                    pe.wait_ge(parts_ready, q + 1)
                    pe.wait_ge(sel_ready, 2)
                    pe.matmul(g[:, :], sel[0:NPART, NS:NS + 1].to_broadcast([NPART, P]), parts[0:NPART, q % 2], start=True, stop=True
                              ).then_inc(delta_done, 1)
                elif name in ("pe_gate0", "pe_gate1"):
                    i = int(name[-1])
                    g = shared(name, q)
                    for b in range(2):
                        for k in range(2):
                            at = (2 * b + k) * P
                            mm = pe.matmul(g[:, at:at + P], c_s[:, 2 * i + b:2 * i + b + 1].to_broadcast([P, P]), wm[:, 2 + 3 * k], start=True, stop=True)
                    mm.then_inc(gate_done, 1)
                elif name in ("pe_V0", "pe_V1"):
                    i = int(name[-1])
                    g = shared(name, q)
                    pe.wait_ge(v_in, 16)
                    for e in range(4):
                        mm = pe.matmul(g[:, e * P:(e + 1) * P], V[:, 4 * i + e], V[:, 4 * i + e], start=True, stop=True)
                    mm.then_inc(V_done, 1)
                elif name == "pe_wout":
                    g = shared(name, q)
                    pe.wait_ge(yg_ready, NH * (q + 1))
                    pe.wait_ge(Wog_ready, NB)
                    for j in range(NT):
                        for h in range(NH):
                            mm = pe.matmul(g[:, j * P:(j + 1) * P], y2[:, h, j * P:(j + 1) * P], Wog[:, q, h],
                                           start=(h == 0), stop=(h == NH - 1))
                    mm.then_inc(wout_done, 1)
                elif name[:5] in ("pe_ra", "pe_rb"):
                    j = int(name[-1])
                    i = "ab".index(name[4])
                    g = shared(name, q)
                    if j == 0:
                        pe.wait_ge(h2T_ready, q + 1)
                        pe.wait_ge(M_ready, 2)
                    pe.matmul(g[:, :], h2T[:, q, j * P:(j + 1) * P], M[:, 4 * i:4 * i + 4].rearrange("p e i -> p (e i)"),
                              start=True, stop=True).then_inc(ra_done if i == 0 else rb_done, 1)
                elif name == "pe_wT":
                    g = shared(name, q)
                    pe.wait_ge(w_parts_ready, q + 1)
                    pe.wait_ge(w_part0, q + 1)
                    pe.wait_ge(w_part1, q + 1)
                    for j in range(NT):
                        mm = pe.transpose(g[0:W9_AT + NE + 1, j * P:(j + 1) * P], w41[:, j], ident[:, :])
                    mm.then_inc(wT_done, 1)
                elif name == "pe_o":
                    pe.wait_ge(w9_in, 16)
                    pe.wait_ge(h2T_ready, q + 1)
                    if q > 0:
                        pe.wait_ge(acc_ready, q)
                    for j in range(NT):
                        pe.matmul(Ops[:, j * P:(j + 1) * P], h2T[:, q, j * P:(j + 1) * P], W9[:, NE * P:],
                                  start=(j == 0), stop=False, skip_group_check=True)
                elif name == "pe_bias":
                    pe.wait_ge(b9_in, 16)
                    pe.wait_ge(wT_ready, q + 1)
                    if q >= NB:
                        pe.wait_ge(acc_ready, q)
                    rows = slice(W9_AT, W9_AT + NE + (q < NB))
                    for j in range(NT):
                        mm = pe.matmul(Ops[:, j * P:(j + 1) * P], wT9[rows, j * P:(j + 1) * P], b9[rows, :],
                                       start=(q >= NB and j == 0), stop=False, skip_group_check=True)
                    mm.then_inc(bias_done, 1)
                elif name == "pe_any":
                    pe.wait_ge(passing_ready, 1)
                    pe.wait_ge(w41_one, 1)
                    pe.wait_ge(y_ready, NH * NB)
                    pe.matmul(Yps[0:1, 0, 0:1], passing[:, :], w41[:, 0, W9_AT + NE:], start=True, stop=True
                              ).then_inc(any_done, 1)
                elif name[:4] == "pe_b":
                    e = int(name[-1])
                    g = shared(name, q)
                    pe.wait_ge(wTp_ready, q + 1)
                    pe.matmul(g[:, :], selE[0:NP3 * NE, e:e + 1].to_broadcast([NP3 * NE, P]), wTp[:, :], start=True,
                              stop=True).then_inc(b_done, 1)
                elif name[:4] == "pe_a":
                    e = int(name[-1])
                    pe.wait_ge(wh_ready, NE * q + e + 1)
                    for j in range(NT):
                        mm = pe.matmul(Ops[:, j * P:(j + 1) * P], wh[:, (NE * q + e) % NW, j * P:(j + 1) * P], W9[:, e * P:(e + 1) * P],
                                       start=False, stop=(e == NE - 1), skip_group_check=True)
                    mm.then_inc(a_done, 1)

            for name, q in order:
                piece(name, q)
            pe.wait_ge(flag_ready, 1)
            with pe.If(pe.value_load(flag[:, :]) == 0):
                for name, q in unmasked:
                    piece(name, q)


def kernel(L0_attn_x, L0_attn_W_in, L0_attn_conv_w, L0_attn_conv_b, L0_attn_W_x, L0_attn_dt_w, L0_attn_dt_b,
           L0_attn_A_log, L0_attn_D, L0_attn_W_out, L0_ffn_Wp, L0_ffn_bp, L0_ffn_We, L0_ffn_be, L0_ffn_Vg, L0_c, L0_wmod):
    import concourse.bacc as _bacc
    from concourse.bass_utils import run_bass_kernel_spmd as _run

    def halves(a):
        return a.reshape(NH, P).T

    part = np.full(P, -1)
    which = np.full(P, -1)
    for i in range(NP3):
        part[NS * i:NS * (i + 1)], which[NS * i:NS * (i + 1)] = i, np.arange(NS)
        part[NS * NP3 + i], which[NS * NP3 + i] = i, NS
    sel = np.zeros((P, NS + 1), np.float32)
    for p in range(NPART):
        sel[p, which[p]] = 1.0
    selE = np.zeros((P, NE), np.float32)
    for p in range(NP3 * NE):
        selE[p, p % NE] = 1.0
    low = np.zeros((P, 8), np.float32)
    low[:, 0] = -(part >= 1).astype(np.float32)
    low[:, 1] = -(part >= 2).astype(np.float32)
    low[:, 2] = EPS
    tri = np.broadcast_to(np.tril(np.ones((NE, NE), np.float32), -1), (P, NE, NE))
    small = {
        "conv_b": halves(np.asarray(L0_attn_conv_b)), "dt_w": halves(np.asarray(L0_attn_dt_w)),
        "dt_b": halves(np.asarray(L0_attn_dt_b)), "D": halves(np.asarray(L0_attn_D)),
        "A_log": np.asarray(L0_attn_A_log).reshape(NH, P, NS).transpose(1, 0, 2).reshape(P, NH * NS),
        "conv_w": np.asarray(L0_attn_conv_w).reshape(NH, P, KC).transpose(1, 0, 2).reshape(P, NH * KC),
        "selE": selE, "low": low, "sel": sel, "tri": tri.reshape(P, NE * NE),
    }
    W_x = np.asarray(L0_attn_W_x).reshape(NH, P, 2 * NS + 1).transpose(1, 0, 2)
    W_o = np.asarray(L0_attn_W_out).reshape(NH, P, P).transpose(1, 0, 2)
    W9 = np.concatenate([np.asarray(L0_ffn_We), np.asarray(L0_ffn_Wp)[None]]).transpose(2, 0, 1).reshape(P, (NE + 1) * P)
    b9 = np.concatenate([np.asarray(L0_ffn_be), np.asarray(L0_ffn_bp)[None]])
    arrays = {
        "x": L0_attn_x, "W_in": L0_attn_W_in, 
        "small": np.concatenate([small[k] for k in SMALL], axis=1),
        "W_x": np.concatenate([W_x[:, :, 1:1 + NS]] * NP3 + [W_x[:, :, :1]] * NP3
                              + [np.zeros((P, NH, C_AT - NPART), np.float32), W_x[:, :, 1 + NS:]], axis=2),
        "W_out": W_o,
        "W9": W9, "b9": b9, "VgT": np.asarray(L0_ffn_Vg).transpose(2, 0, 1),
        "cT": np.asarray(L0_c).T, "wmod": L0_wmod, "ident": np.eye(P, dtype=np.float32),
    }
    nc = _bacc.Bacc("TRN2", target_bir_lowering=False, num_devices=1)
    ins, args = {}, []
    for name, a in arrays.items():
        a = np.ascontiguousarray(a)
        ins["in_" + name] = a
        args.append(nc.dram_tensor("in_" + name, a.shape, mybir.dt.from_np(a.dtype), kind="ExternalInput").ap())
    out = nc.dram_tensor("out", (NB, T, P), F32, kind="ExternalOutput").ap()
    C_dram = nc.dram_tensor("C_dram", (NB, NS, T), F32, kind="Internal").ap()
    adaln_mamba_experts(nc, *args, C_dram, out)
    return _run(nc, [ins], core_ids=[0]).results[0]["out"]
```

```python
from contextlib import ExitStack

import numpy as np

import concourse.bass as bass
from concourse import mybir

ALU = mybir.AluOpType
ACT = mybir.ActivationFunctionType
AX = mybir.AxisListType.X
F32 = mybir.dt.float32
BF16 = mybir.dt.bfloat16

P = 128
NB = 4
T = 512
NT = T // P
DI = 256
NH = DI // P
NS = 16
KC = 4
NE = 8
RV = 64
NP3 = 3
NR = 2 * NS + 1
EPS = 1e-5

SMALL = {"selE": NE, "conv_b": NH, "dt_w": NH, "dt_b": NH, "D": NH, "A_log": NH * NS, "conv_w": NH * KC, "eps": 1, "tri": NE * NE}

HEAD = [
    ("vec_ln1", 0), ("act_rstd1", 0), ("pe_xT", 0), ("vec_shift1", 0), ("norm1", 0), ("act_hT", 0),
    ("vec_ln1", 1), ("pe_x0", 0), ("pe_x1", 0), ("pe_z0", 0), ("act_rstd1", 1), ("vec_shift1", 1),
    ("act_x0", 0), ("act_x1", 0), ("vec_c0", 0), ("pe_z1", 0), ("vec_c1", 0), ("act_t0", 0), ("vec_x0", 0),
    ("act_t1", 0), ("vec_x1", 0), ("act_z0", 0), ("pe_ssm", 0), ("vec_z0", 0), ("act_z1", 0),
    ("vec_z1", 0), ("act_rows", 0), ("norm1", 1), ("pe_xT", 1), ("sp_rows", 0), ("act_hT", 1),
    ("vec_soft0", 0), ("act_soft0", 0), ("act_soft1", 0), ("soft_sum0", 0), ("soft_add0", 0),
    ("delta_x0", 0), ("vec_soft1", 0), ("soft_sum1", 0), ("soft_add1", 0), ("delta_x1", 0), ("first", 0)
]
LEAD = {
    "vec_ln1": (-6, -6, -6), "act_rstd1": (-4, -7, -6), "vec_shift1": (-4, -5, -4), "act_hT": (-2, -4, -2),
    "norm1": (-2, -5, -4), "pe_xT": (-3, -2, -2), "act_x0": (1, 1, 2), "pe_x0": (1, 2, 1),
    "pe_x1": (1, 2, 2), "act_x1": (1, 1, 2), "vec_c0": (1, 2, 2), "act_t0": (2, 3, 3), "vec_c1": (2, 3, 2),
    "pe_z0": (2, 4, 3), "vec_x0": (2, 3, 3), "act_t1": (2, 4, 3), "act_z0": (3, 4, 4), "vec_x1": (3, 3, 3),
    "pe_z1": (5, 5, 4), "vec_z0": (4, 5, 4), "act_z1": (4, 4, 4), "pe_ssm": (6, 4, 4),
    "act_rows": (5, 5, 5), "sp_rows": (4, 5, 5), "vec_z1": (4, 5, 4), "vec_soft0": (10, 10, 10),
    "vec_soft1": (10, 10, 10), "act_soft0": (7, 9, 9), "act_soft1": (9, 9, 9), "soft_sum0": (10, 10, 10),
    "soft_add0": (10, 10, 10), "soft_sum1": (10, 10, 10), "soft_add1": (10, 10, 10),
    "delta_x0": (11, 11, 11), "delta_x1": (11, 11, 11)
}
LAG = {
    "vec_y0": (2, 0, 1), "vec_y1": (2, 0, 1), "gate_z0": (1, 0, 0), "gate_z1": (2, 0, 0),
    "pe_wout": (4, 3, 3), "vec_x2": (4, 3, 2), "act_rstd2": (5, 4, 3), "vec_shift2": (6, 5, 3),
    "norm2": (6, 5, 3), "pe_xT2": (8, 6, 5), "act_h2T": (8, 6, 4), "pe_ra0": (10, 7, 6),
    "sq_ra0": (10, 7, 5), "pe_rb0": (10, 7, 6), "sq_rb0": (10, 7, 5), "pe_ra1": (11, 8, 6),
    "sq_ra1": (11, 8, 5), "sq_rb1": (11, 8, 5), "pe_ra2": (12, 9, 6), "sq_ra2": (12, 9, 5),
    "pe_rb1": (11, 8, 6), "pe_rb2": (11, 8, 6), "sq_rb2": (11, 8, 5), "pe_ra3": (12, 9, 6),
    "sq_ra3": (13, 9, 6), "pe_rb3": (12, 9, 6), "sq_rb3": (13, 9, 6), "pe_o": (19, 15, 9),
    "vec_clamp": (15, 11, 7), "vec_ranka": (15, 10, 7), "act_sqrt": (16, 13, 7), "vec_gate1": (16, 12, 8),
    "vec_rankb": (16, 12, 8), "vec_gate2": (16, 12, 8), "split_w": (17, 12, 8), "pe_wT": (19, 15, 10),
    "act_gexp": (16, 13, 8), "act_wT": (19, 15, 9), "vec_h0": (21, 16, 9), "pe_b0": (21, 16, 10),
    "pe_b1": (21, 16, 10), "vec_h1": (22, 16, 10), "pe_b2": (23, 16, 11), "vec_h2": (23, 17, 11),
    "vec_h3": (23, 18, 11), "pe_bias": (23, 18, 11), "pe_b3": (23, 18, 11), "pe_a0": (22, 18, 11),
    "pe_a1": (24, 18, 12), "vec_h4": (25, 19, 13), "pe_b4": (25, 19, 12), "pe_a2": (26, 20, 15),
    "pe_b5": (26, 20, 12), "vec_h5": (26, 19, 14), "vec_h6": (26, 21, 14), "pe_a3": (26, 20, 15),
    "pe_b6": (26, 21, 12), "pe_b7": (29, 22, 15), "pe_a4": (27, 20, 15), "vec_h7": (28, 22, 15),
    "pe_a5": (27, 21, 15), "pe_a6": (30, 23, 15), "pe_a7": (30, 23, 15), "vec_out": (29, 24, 15),
    "sp_out": (29, 23, 15), "add_out": (30, 24, 15)
}
SETUP = {
    "pe_gate0": 2, "pe_gate1": 4, "vec_gates": 3, "pool_wog": 7, "pe_V0": 7, "pe_V1": 10, "vec_V": 11
}
SQ_LAST = f"sq_rb{NT - 1}"

ANY = {"vec_gate2": "vec_any", "pe_a2": "pe_any", "vec_h5": "vec_flag"}

BUSY = {"pe_wout": 10, "pe_xT2": 12, "pe_wT": 20}


def plan():
    steps = [[] for _ in range(NB * NS)]
    for name, n in SETUP.items():
        steps[n].append((name, 0))
    for q in range(NB - 1):
        for name, after in LAG.items():
            steps[NS * (q + 1) + after[q]].append((name, q))
    for q in range(1, NB):
        for name, after in LEAD.items():
            if (name, q) not in HEAD:
                steps[NS * (q - 1) + after[q - 1]].append((name, q))
    order = [("modulate", 0)] + HEAD
    for s, pieces in enumerate(steps):
        order += [("scan", s), *pieces]
    order += [("last", 0)]
    for name in LAG:
        if name in BUSY:
            order.append(("pe_busy", BUSY[name]))
        order.append((name, NB - 1))
        if name in ANY:
            order.append((ANY[name], NB - 1))
    pieces = ["vec_top", "pe_wT", "act_wT", "pe_bias"]
    for e in range(NE):
        pieces += [f"pe_b{e}", f"vec_h{e}", f"pe_a{e}"]
    unmasked = [(name, q) for q in range(NB, 2 * NB) for name in pieces + ["vec_out", "add_out", "sp_out"]]
    return order, unmasked


C_AHEAD = 4
AHEAD = 3
IN_AHEAD = 1
SHARED_FROM = NB * NS - 2
BEHIND = 3
NG = 4
W9_AT = 32


def bank_plan(order, shared_banks):
    uses, turn = {}, []
    for name, q in order:
        if name in shared_banks:
            count, sem, per, first = shared_banks[name]
            for i in range(count):
                k = len(turn)
                before = turn[k - NG] if k >= NG else None
                uses.setdefault((name, q), []).append((k % NG, before))
                turn.append((sem, per * q + first + i))
    return uses


def adaln_mamba_experts(nc, x, W_in, smalls, W_x, W_out, We_Wp, be_bp, VgT, cT, wmod, eye, rows_dram, out):
    order, unmasked = plan()
    with ExitStack() as ctx:
        def sb(name, shape, dt=F32):
            return ctx.enter_context(nc.sbuf_tensor(name, shape, dt))

        def ps(name, shape):
            return ctx.enter_context(nc.psum_tensor(name, shape, F32))

        ND, NX, NHB, NPB, NBR, NC, NW = 4, 2, 4, 4, 4, 5, 3
        def sem(name):
            return ctx.enter_context(nc.semaphore(name))

        x_in = [sem(f"x{b}_in") for b in range(NB)]
        B_in = [sem(f"B{i}_in") for i in range(NBR)]
        C_in = [sem(f"C{i}_in") for i in range(NC)]
        bn_ready, stats_ready, lnv_ready, rstd_ready, shift_ready, xn_ready = (
            [sem(f"{name}{i}") for i in range(2)] for name in (
                "bn_ready", "stats_ready", "lnv_ready", "rstd_ready", "shift_ready", "xn_ready"))
        (c_in, wm_in, ident_in, small_in, win_in, wx_in, wo_in, v_in, w9_in, b9_in) = map(sem, (
            "c_in", "wm_in", "ident_in", "small_in", "win_in", "wx_in", "wo_in", "v_in", "w9_in",
            "b9_in"))
        (blank_ready, w41_clear, w41_one, reset_ready, sel_ready, Woh_ready, convbh_ready, taps_ready, Ae_ready,
         A_ready, V_done, M_ready) = map(sem, (
            "blank_ready", "w41_clear", "w41_one", "reset_ready", "sel_ready", "Woh_ready", "convbh_ready",
            "taps_ready", "Ae_ready", "A_ready", "V_done", "M_ready"))
        (cth_ready, ch_ready, csig_ready, cs_ready, mod_done, mod_ready, gate_done,
         gates_read, gsgn_twice, gsgn_ready, gabs_ready, gates_ready, Wog_ready) = map(sem, (
            "cth_ready", "ch_ready", "csig_ready", "cs_ready", "mod_done", "mod_ready",
            "gate_done", "gates_read", "gsgn_twice", "gsgn_ready", "gabs_ready", "gates_ready",
            "Wog_ready"))
        (xT_done, hT_ready, x_done, z_done, xin_ready, tap_done, conv_done, xth_ready, xconv_ready,
         zth_ready, zgate_ready) = map(sem, (
            "xT_done", "hT_ready", "x_done", "z_done", "xin_ready", "tap_done", "conv_done",
            "xth_ready", "xconv_ready", "zth_ready", "zgate_ready"))
        (ssm_done, rows_ready, rows_stored, raw_in, dabs_ready, softin_ready, dexp_ready, dw1_ready,
         dcor_ready, dlog_ready, dsum_ready, delta_ready, dx_ready) = map(sem, (
            "ssm_done", "rows_ready", "rows_stored", "raw_in", "dabs_ready", "softin_ready", "dexp_ready",
            "dw1_ready", "dcor_ready", "dlog_ready", "dsum_ready", "delta_ready", "dx_ready"))
        (dA_half, dA_ready, dBx_ready, scan_done, prod_ready, prod_rest_ready, nsum_done) = map(sem, (
            "dA_half", "dA_ready", "dBx_ready", "scan_done", "prod_ready", "prod_rest_ready",
            "nsum_done"))
        (y_ready, yg_ready, wout_done, x2_ready, xT2_done, h2T_ready) = map(sem, (
            "y_ready", "yg_ready", "wout_done", "x2_ready", "xT2_done", "h2T_ready"))
        (ra_done, rb_done, sqa_some, sqa_done, sqb_some, sqb_done, clamp_ready, lr_ready, res_ready, rmin_ready, gd_ready, ge_ready,
         lt_ready, eq_ready, eql_ready, cnt_ready, rank_ready, gs_ready, gr_ready, rw_ready, msk_ready,
         keep_ready, fw_ready, sw_ready, swz_ready, rsw_ready, w_ready, w_hi_ready, w_part0,
         w_rest_ready, w_mid_ready, w_part1, w_parts_ready, wT_done, wTp_ready, wT_ready) = map(sem, (
            "ra_done", "rb_done", "sqa_some", "sqa_done", "sqb_some", "sqb_done", "clamp_ready", "lr_ready", "res_ready", "rmin_ready",
            "gd_ready", "ge_ready", "lt_ready", "eq_ready", "eql_ready", "cnt_ready", "rank_ready",
            "gs_ready", "gr_ready", "rw_ready", "msk_ready", "keep_ready", "fw_ready", "sw_ready",
            "swz_ready", "rsw_ready", "w_ready", "w_hi_ready", "w_part0", "w_rest_ready",
            "w_mid_ready", "w_part1", "w_parts_ready", "wT_done", "wTp_ready", "wT_ready"))
        (bias_done, b_done, wh_ready, a_done, acc_ready, out_ready, stored, passing_ready, any_done,
         flag_ready, resid_copied) = map(sem, (
            "bias_done", "b_done", "wh_ready", "a_done", "acc_ready", "out_ready", "stored", "passing_ready", "any_done",
            "flag_ready", "resid_copied"))
        normT_done = [xT_done, xT2_done]

        shared_banks = {
            "pe_xT": (1, hT_ready, 1, 1), "pe_x0": (1, conv_done, 2, 1), "pe_x1": (1, conv_done, 2, 2),
            "pe_z0": (1, zgate_ready, 2, 1), "pe_z1": (1, zgate_ready, 2, 2), "pe_ssm": (1, rows_ready, 1, 1), "pe_wout": (1, x2_ready, 1, 1), "pe_xT2": (1, h2T_ready, 1, 1),
            "pe_wT": (1, wT_ready, 1, 1), **{f"pe_b{e}": (1, wh_ready, NE, e + 1) for e in range(NE)},
            "pe_gate0": (1, gates_read, 2, 1), "pe_gate1": (1, gates_read, 2, 2),
            "pe_V0": (1, M_ready, 2, 1), "pe_V1": (1, M_ready, 2, 2),
            **{f"pe_ra{j}": (1, sqa_done, NT, j + 1) for j in range(NT)},
            **{f"pe_rb{j}": (1, sqb_done, NT, j + 1) for j in range(NT)},
        }
        banks = bank_plan(order + unmasked, shared_banks)

        Win = sb("Win", [P, 2 * DI])
        small = sb("small", [P, sum(SMALL.values())])
        part_of, at = {}, 0
        for name, width in SMALL.items():
            part_of[name] = small[:, at:at + width]
            at += width
        convb, dtw, dtb, Dsk = (part_of[k] for k in ("conv_b", "dt_w", "dt_b", "D"))
        Al = part_of["A_log"].rearrange("p (h n) -> p h n", h=NH)
        eps = part_of["eps"]
        tri = part_of["tri"].rearrange("p (e f) -> p e f", e=NE)
        conv_w = part_of["conv_w"].rearrange("p (h k) -> p h k", h=NH)
        convbh = sb("convbh", [P, NH])
        taps = sb("taps", [P, NH, KC])
        Wx = sb("Wx", [P, NH, NR])
        Ae = sb("Ae", [P, NH, NS])
        A = sb("A", [P, NH, NS])
        Wo = sb("Wo", [P, NH, P])
        Wog = sb("Wog", [P, NB, NH, P])
        W9 = sb("W9", [P, (NE + 1) * P])
        b9 = sb("b9", [W9_AT + NE + 1, P])
        M = sb("M", [P, NE, P])
        c_sb = sb("c_sb", [P, NB])
        c_th = sb("c_th", [P, NB])
        c_h = sb("c_h", [P, NB])
        c_s = sb("c_s", [P, NB])
        wm = sb("wm", [P, 6, P])
        mod = sb("mod", [P, 4, NB])
        mod1 = sb("mod1", [P, 4, NB])
        gate = sb("gate", [P, NB, 2, P])
        ident = sb("ident", [P, P])
        selE = sb("selE", [P, NE], BF16)
        blank = sb("blank", [P, T], BF16)
        x_sb = sb("x_sb", [P, NB, NT, P])
        stats = sb("stats", [P, 2, NT, 6])
        mv = sb("mv", [P, 2, NT, 2])
        lnv = sb("lnv", [P, 2, NT])
        rstd = sb("rstd", [P, 2, NT])
        shift = sb("shift", [P, 2, NT])
        xn = sb("xn", [P, 2, NT, P])
        hT = sb("hT", [P, 2, T])
        h2T = sb("h2T", [P, NB, T])
        xch = sb("xch", [P, NH, T])
        th = sb("th", [P, NH, T])
        xconv = sb("xconv", [P, 2, NH, T])
        zz = sb("zz", [P, 2, NH, T])
        dexp = sb("dexp", [P, NH, T])
        drel = sb("drel", [P, NH, T])
        dlog = sb("dlog", [P, NH, T])
        dw1 = sb("dw1", [P, NH, T])
        delta = sb("delta", [P, 2, NH, T])
        dx = sb("dx", [P, 2, NH, T])
        dA = sb("dA", [P, ND, NH, T])
        dBx = sb("dBx", [P, NX, NH, T])
        hs = sb("hs", [P, NHB, NH, T])
        prod = sb("prod", [P, NPB, NH, T])
        rows = sb("rows", [NR, T])
        raw = sb("raw", [P, T])
        B_sb = sb("B_sb", [P, NBR, T])
        C_sb = sb("C_sb", [P, NC, T])
        y2 = sb("y2", [P, NH, T])
        r2 = sb("r2", [P, NB, NT, NE])
        r2c = sb("r2c", [P, NT, NE])
        lr = sb("lr", [P, NT, NE])
        res = sb("res", [P, NT, NE])
        rmin = sb("rmin", [P, NT])
        gd = sb("gd", [P, NT, NE])
        ge = sb("ge", [P, NT, NE])
        gs = sb("gs", [P, NT])
        gr = sb("gr", [P, NT])
        rw = sb("rw", [P, NT, NE])
        msk = sb("msk", [P, NB, NT, NE])
        passing = sb("passing", [P, 1])
        flag = sb("flag", [1, 1], mybir.dt.int32)
        lt = sb("lt", [P, NT, NE, NE])
        eq = sb("eq", [P, NT, NE, NE])
        rank = sb("rank", [P, NB, NT, NE])
        keep = sb("keep", [P, NT, NE])
        fw = sb("fw", [P, NT, NE])
        sw = sb("sw", [P, NT])
        swz = sb("swz", [P, NT])
        rsw = sb("rsw", [P, NT])
        w_hi = sb("w_hi", [P, NT, NE], BF16)
        w_rest = sb("w_rest", [P, NT, NE])
        w_mid = sb("w_mid", [P, NT, NE], BF16)
        w41 = sb("w41", [P, NT, W9_AT + NE + 1])
        wTp = sb("wTp", [NP3 * NE, T], BF16)
        wT9_all = sb("wT9_all", [P, T])
        wT9 = wT9_all[0:W9_AT + NE + 1, :]
        wh = sb("wh", [P, NW, T])
        V = wh[0:RV, 0:NE * P // T].rearrange("r w (e i) -> r (w e) i", i=P)
        graw = wT9_all
        acc = sb("acc", [P, NT, P])
        gsgn = acc[:, :, :].rearrange("p j o -> p (j o)")

        spare = ps("spare", [P, T])
        Yps = ps("Yps", [P, NH, T])
        Ops = ps("Ops", [P, T])
        G = [ps(f"G{i}", [P, T]) for i in range(NG)]
        block = ctx.enter_context(nc.Block())

        last_s = NB * NS - 1

        loads = [
            (x_sb[:, 0], x[0].rearrange("(j p) i -> p j i", p=P), x_in[0]), (c_sb[:, :], cT, c_in),
            (wm[:, :, :], wmod.rearrange("k (m n) -> k m n", m=6), wm_in), (ident[:, :], eye, ident_in),
            (small[:, :], smalls, small_in), (Win[:, :], W_in, win_in), (Wx[:, :, :], W_x, wx_in),
            (x_sb[:, 1], x[1].rearrange("(j p) i -> p j i", p=P), x_in[1]),
            (Wo[:, :, :], W_out, wo_in), (V[:, :, :], VgT, v_in),
            (W9[:, :], We_Wp, w9_in), (b9[W9_AT:, :], be_bp, b9_in),
            (x_sb[:, 2], x[2].rearrange("(j p) i -> p j i", p=P), x_in[2]),
            (x_sb[:, 3], x[3].rearrange("(j p) i -> p j i", p=P), x_in[3]),
        ]
        @block.sync
        def _(sp):
            for dst, src, landed in loads:
                sp.dma_start(dst, src).then_inc(landed, 16)

            def load_row(row, q, dst, landed):
                sp.wait_ge(rows_stored, 16 * (q + 1))
                sp.dma_start(dst, rows_dram[q, row].partition_broadcast(P)).then_inc(landed, 16)

            def load_B(s):
                if s >= NBR:
                    sp.wait_ge(dBx_ready, s - NBR + 1)
                load_row(1 + s % NS, s // NS, B_sb[:, s % NBR], B_in[s % NBR])

            def load_C(s):
                if s >= NC:
                    sp.wait_ge(prod_ready, s - NC + 1)
                load_row(1 + NS + s % NS, s // NS, C_sb[:, s % NC], C_in[s % NC])

            def piece(name, q):
                if name == "sp_rows":
                    sp.wait_ge(rows_ready, q + 1)
                    sp.dma_start(rows_dram[q], rows[:, :]).then_inc(rows_stored, 16)
                    if q > 0:
                        sp.wait_ge(dabs_ready, NH * q)
                        sp.wait_ge(softin_ready, NH * q)
                    load_row(0, q, raw[:, :], raw_in)
                elif name == "first":
                    for s in range(C_AHEAD):
                        load_B(s)
                        load_C(s)
                elif name == "scan":
                    if q + C_AHEAD <= last_s:
                        load_B(q + C_AHEAD)
                        load_C(q + C_AHEAD)
                elif name == "sp_out":
                    sp.wait_ge(out_ready, q + 1)
                    sp.dma_start(out[q % NB].rearrange("(j p) i -> p j i", p=P), x_sb[:, q % NB]).then_inc(stored, 16)

            for name, q in order:
                piece(name, q)
            sp.wait_ge(stored, 16 * NB)
            sp.wait_ge(flag_ready, 1)
            with sp.If(sp.value_load(flag[:, :]) == 0):
                for name, q in unmasked:
                    piece(name, q)
                sp.wait_ge(stored, 2 * 16 * NB)

        def soft_sum(eng, q, h):
            k = NH * q + h
            eng.wait_ge(dcor_ready, k + 1)
            eng.wait_ge(dlog_ready, k + 1)
            eng.tensor_tensor(dlog[:, h], dlog[:, h], dw1[:, h], ALU.subtract).then_inc(dsum_ready, 1)

        def soft_add(eng, q, h):
            k = NH * q + h
            eng.wait_ge(dsum_ready, k + 1)
            eng.wait_ge(softin_ready, k + 1)
            if q >= 2:
                eng.wait_ge(dA_ready, NS * (q - 1))
            eng.tensor_tensor(delta[:, q % 2, h], dlog[:, h], drel[:, h], ALU.add).then_inc(delta_ready, 1)

        def gate_z(eng, q, h):
            k = NH * q + h
            eng.wait_ge(y_ready, k + 1)
            eng.wait_ge(zgate_ready, k + 1)
            if q > 0:
                eng.wait_ge(wout_done, q)
            eng.tensor_tensor(y2[:, h], y2[:, h], zz[:, q % 2, h], ALU.mult).then_inc(yg_ready, 1)

        def split_w(eng, q):
            w = w41[:, :, W9_AT:W9_AT + NE]
            eng.wait_ge(w_ready, q + 1)
            eng.tensor_copy(w_hi[:, :, :], w).then_inc(w_hi_ready, 1)
            eng.wait_ge(w_hi_ready, q + 1)
            eng.tensor_copy(w41[:, :, 0:NE], w_hi[:, :, :]).then_inc(w_part0, 1)
            eng.tensor_tensor(w_rest[:, :, :], w, w_hi[:, :, :], ALU.subtract).then_inc(w_rest_ready, 1)
            eng.wait_ge(w_rest_ready, q + 1)
            eng.tensor_copy(w_mid[:, :, :], w_rest[:, :, :]).then_inc(w_mid_ready, 1)
            eng.wait_ge(w_mid_ready, q + 1)
            eng.tensor_copy(w41[:, :, NE:2 * NE], w_mid[:, :, :]).then_inc(w_part1, 1)
            eng.tensor_tensor(w41[:, :, 2 * NE:3 * NE], w_rest[:, :, :], w_mid[:, :, :], ALU.subtract
                              ).then_inc(w_parts_ready, 1)

        def delta_x(eng, q, h):
            k = NH * q + h
            eng.wait_ge(delta_ready, k + 1)
            eng.wait_ge(xconv_ready, k + 1)
            if q >= 2:
                eng.wait_ge(dBx_ready, NS * (q - 1))
            eng.tensor_tensor(dx[:, q % 2, h], delta[:, q % 2, h], xconv[:, q % 2, h], ALU.mult).then_inc(dx_ready, 1)

        @block.gpsimd
        def _(pool):
            pool.memset(blank[:, :], 0.0).then_inc(blank_ready, 1)
            pool.memset(w41[:, :, :], 0.0).then_inc(w41_clear, 1)
            pool.wait_ge(w41_clear, 1)
            pool.memset(w41[:, :, W9_AT + NE:], 1.0).then_inc(w41_one, 1)
            for i in range(ND):
                pool.memset(dA[:, i, :, 0:1], 0.0).then_inc(reset_ready, 1)
            pool.wait_ge(small_in, 16)
            pool.tensor_copy(selE[:, :], part_of["selE"]).then_inc(sel_ready, 1)
            pool.wait_ge(wo_in, 16)
            pool.tensor_scalar(Wo[:, :, :], Wo[:, :, :], 0.5, 1.0, ALU.mult, ALU.mult).then_inc(Woh_ready, 1)

            def piece(name, q):
                if name == "scan":
                    s = q
                    pool.wait_ge(scan_done, s + 1)
                    pool.wait_ge(C_in[s % NC], 16 * (s // NC + 1))
                    if s >= NPB:
                        pool.wait_ge(nsum_done, s - NPB + 1)
                    halves = NH if s < SHARED_FROM else 1
                    pool.tensor_tensor(prod[:, s % NPB, 0:halves], hs[:, s % NHB, 0:halves],
                                       C_sb[:, s % NC].unsqueeze(1).to_broadcast([P, halves, T]),
                                       ALU.mult).then_inc(prod_ready, 1)
                elif name == "pool_wog":
                    pool.wait_ge(gates_ready, 2)
                    pool.wait_ge(Woh_ready, 1)
                    for b in range(NB):
                        pool.tensor_tensor(Wog[:, b], Wo[:, :, :],
                                           gate[:, b, 0].unsqueeze(1).to_broadcast([P, NH, P]),
                                           ALU.mult).then_inc(Wog_ready, 1)
                elif name[:-1] == "soft_sum" and q > 0:
                    soft_sum(pool, q, int(name[-1]))
                elif name[:-1] == "soft_add" and q > 0:
                    soft_add(pool, q, int(name[-1]))
                elif name[:-1] == "delta_x" and q > 0:
                    delta_x(pool, q, int(name[-1]))
                elif name in ("gate_z0", "gate_z1") and q < NB - 1:
                    gate_z(pool, q, int(name[-1]))
                elif name == "split_w" and q < NB - 1:
                    split_w(pool, q)
                elif name == "add_out" and q != NB - 1:
                    pool.wait_ge(acc_ready, q + 1)
                    if q >= NB:
                        pool.wait_ge(stored, 16 * q)
                    pool.tensor_tensor(x_sb[:, q % NB], acc[:, :, :], x_sb[:, q % NB], ALU.add).then_inc(out_ready, 1)

            for name, q in order:
                piece(name, q)
            pool.wait_ge(flag_ready, 1)
            with pool.If(pool.value_load(flag[:, :]) == 0):
                for name, q in unmasked:
                    piece(name, q)

        @block.scalar
        def _(act):
            act.preload_act_table_set("natural_log_exp_and_others")
            act.wait_ge(c_in, 16)
            act.activation(c_th[:, :], c_sb[:, :], ACT.Exp, scale=-1.0).then_inc(cth_ready, 1)
            act.wait_ge(small_in, 16)
            act.activation(convbh[:, :], convb[:, :], ACT.Copy, scale=0.5).then_inc(convbh_ready, 1)
            act.activation(Ae[:, :, :], Al[:, :, :], ACT.Exp).then_inc(Ae_ready, 1)

            def exps(s):
                q, n = divmod(s, NS)
                act.wait_ge(A_ready, 1)
                act.wait_ge(reset_ready, ND)
                if s >= ND:
                    act.wait_ge(scan_done, s - ND + 1)
                for h in range(NH):
                    act.wait_ge(delta_ready, NH * q + h + 1)
                    act.activation(dA[:, s % ND, h, 1:T], delta[:, q % 2, h, 1:T], ACT.Exp,
                                   scale=A[:, h, n:n + 1]).then_inc(dA_half if h == 0 else dA_ready, 1)

            def norm_of(which, q):
                act.wait_ge(shift_ready[which], q + 1)
                if q > 0:
                    act.wait_ge(normT_done[which], q)
                for j in range(NT):
                    act.activation(xn[:, which, j], x_sb[:, q, j], ACT.Identity, scale=rstd[:, which, j:j + 1],
                                   bias=shift[:, which, j:j + 1]).then_inc(xn_ready[which], 1)

            def rstd_of(which, q):
                act.wait_ge(stats_ready[which], NT * (q + 1))
                if q > 0:
                    act.wait_ge(rstd_ready[which], q)
                act.activation(lnv[:, which], mv[:, which, :, 1], ACT.Ln, bias=eps).then_inc(lnv_ready[which], 1)
                act.wait_ge(lnv_ready[which], q + 1)
                if q > 0:
                    act.wait_ge(xn_ready[which], NT * q)
                act.activation(rstd[:, which], lnv[:, which], ACT.Exp, scale=-0.5).then_inc(rstd_ready[which], 1)

            def piece(name, q):
                g = banks.get(("pe_" + name[4:], q)) if name.startswith("act_") else None
                if name == "first":
                    for s in range(AHEAD):
                        exps(s)
                elif name == "scan":
                    if q + AHEAD <= last_s:
                        exps(q + AHEAD)
                elif name == "modulate":
                    act.wait_ge(mod_done, 1)
                    act.copy(mod[:, :, :], Yps[:, 0, 0:16].rearrange("p (k b) -> p k b", k=4)).then_inc(mod_ready, 1)
                    act.activation(mod1[:, :, :], Yps[:, 0, 0:16].rearrange("p (k b) -> p k b", k=4), ACT.Identity,
                                   bias=1.0).then_inc(mod_ready, 1)
                elif name == "norm1":
                    norm_of(0, q)
                elif name == "norm2" and q < NB - 1:
                    norm_of(1, q)
                elif name == "act_rstd1":
                    rstd_of(0, q)
                elif name == "act_rstd2":
                    rstd_of(1, q)
                elif name == "act_hT":
                    g = banks[("pe_xT", q)]
                    act.wait_ge(xT_done, q + 1)
                    act.wait_ge(mod_ready, 2)
                    if q >= 2:
                        act.wait_ge(x_done, 2 * (q - 1))
                        act.wait_ge(z_done, 2 * (q - 1))
                    act.activation(hT[:, q % 2], G[g[0][0]][:, :], ACT.Identity, scale=mod1[:, 1, q:q + 1],
                                   bias=mod[:, 0, q:q + 1]).then_inc(hT_ready, 1)
                elif name == "act_h2T":
                    g = banks[("pe_xT2", q)]
                    act.wait_ge(xT2_done, q + 1)
                    act.activation(h2T[:, q], G[g[0][0]][:, :], ACT.Identity, scale=mod1[:, 3, q:q + 1],
                                   bias=mod[:, 2, q:q + 1]).then_inc(h2T_ready, 1)
                elif name in ("act_x0", "act_x1"):
                    h = int(name[-1])
                    k = 2 * q + h
                    act.wait_ge(x_done, k + 1)
                    act.wait_ge(taps_ready, 1)
                    act.wait_ge(convbh_ready, 1)
                    if k >= 2:
                        act.wait_ge(xconv_ready, k - 1)
                    act.activation(xch[:, h], G[g[0][0]][:, :], ACT.Identity, scale=taps[:, h, KC - 1:KC],
                                   bias=convbh[:, h:h + 1]).then_inc(xin_ready, 1)
                elif name in ("act_t0", "act_t1"):
                    h = int(name[-1])
                    k = 2 * q + h
                    act.wait_ge(conv_done, k + 1)
                    if k >= 2:
                        act.wait_ge(zgate_ready, k - 1)
                    act.activation(th[:, h], xch[:, h], ACT.Tanh).then_inc(xth_ready, 1)
                elif name in ("act_z0", "act_z1"):
                    h = int(name[-1])
                    k = 2 * q + h
                    act.wait_ge(z_done, k + 1)
                    act.wait_ge(xconv_ready, k + 1)
                    act.activation(th[:, h], G[g[0][0]][:, :], ACT.Tanh, scale=0.5).then_inc(zth_ready, 1)
                    if h == NH - 1:
                        act.preload_act_table_set("natural_log_exp_and_others")
                elif name == "act_rows":
                    act.wait_ge(ssm_done, q + 1)
                    if q > 0:
                        act.wait_ge(rows_stored, 16 * q)
                    act.copy(rows[:, :], G[banks[("pe_ssm", q)][0][0]][0:NR, :]).then_inc(rows_ready, 1)
                elif name in ("act_soft0", "act_soft1"):
                    h = int(name[-1])
                    k = NH * q + h
                    act.wait_ge(raw_in, 16 * (q + 1))
                    if q > 0:
                        act.wait_ge(dcor_ready, k + 1 - NH)
                    act.activation(dexp[:, h], raw[:, :], ACT.Abs, scale=dtw[:, h:h + 1],
                                   bias=dtb[:, h:h + 1]).then_inc(dabs_ready, 1)
                    act.wait_ge(dabs_ready, k + 1)
                    act.activation(dexp[:, h], dexp[:, h], ACT.Exp, scale=-1.0).then_inc(dexp_ready, 1)
                    if q > 0:
                        act.wait_ge(delta_ready, k + 1 - NH)
                    act.wait_ge(dexp_ready, k + 1)
                    if q > 0:
                        act.wait_ge(dsum_ready, k + 1 - NH)
                        act.activation(dw1[:, h], dexp[:, h], ACT.Identity, bias=1.0).then_inc(dw1_ready, 1)
                    act.activation(dlog[:, h], dexp[:, h], ACT.Ln, bias=1.0).then_inc(dlog_ready, 1)
                    act.activation(drel[:, h], raw[:, :], ACT.Relu, scale=dtw[:, h:h + 1], bias=dtb[:, h:h + 1]
                                   ).then_inc(softin_ready, 1)
                elif name[:5] == "sq_ra":
                    j = int(name[-1])
                    k = NT * q + j
                    g = G[banks[(f"pe_ra{j}", q)][0][0]]
                    act.wait_ge(ra_done, k + 1)
                    for e in range(NE // 2):
                        act.activation(g[:, e * P:(e + 1) * P], g[:, e * P:(e + 1) * P], ACT.Square,
                                       accum_out=r2[:, q, j, e:e + 1]
                                       ).then_inc(sqa_some if e < NE // 2 - 1 else sqa_done, 1)
                elif name[:5] == "sq_rb" and (q < NB - 1 or name == SQ_LAST):
                    j = int(name[-1])
                    k = NT * q + j
                    g = G[banks[(f"pe_rb{j}", q)][0][0]]
                    act.wait_ge(rb_done, k + 1)
                    for e in range(NE // 2):
                        act.activation(g[:, e * P:(e + 1) * P], g[:, e * P:(e + 1) * P], ACT.Square,
                                       accum_out=r2[:, q, j, NE // 2 + e:NE // 2 + e + 1]
                                       ).then_inc(sqb_some if e < NE // 2 - 1 else sqb_done, 1)
                elif name == "act_sqrt":
                    act.wait_ge(clamp_ready, q + 1)
                    if q > 0:
                        act.wait_ge(res_ready, q)
                    act.activation(lr[:, :, :], r2c[:, :, :], ACT.Ln).then_inc(lr_ready, 1)
                    act.wait_ge(lr_ready, q + 1)
                    if q > 0:
                        act.wait_ge(gd_ready, q)
                    act.activation(res[:, :, :], lr[:, :, :], ACT.Exp, scale=0.5).then_inc(res_ready, 1)
                elif name == "act_gexp":
                    act.wait_ge(gd_ready, q + 1)
                    if q > 0:
                        act.wait_ge(rw_ready, q)
                    act.activation(ge[:, :, :], gd[:, :, :], ACT.Exp).then_inc(ge_ready, 1)
                elif name == "act_wT":
                    g = G[g[0][0]]
                    act.wait_ge(wT_done, q + 1)
                    if q > 0:
                        act.wait_ge(b_done, NE * q)
                        act.wait_ge(bias_done, q)
                    act.copy(wTp[:, :], g[0:NP3 * NE, :]).then_inc(wTp_ready, 1)
                    act.copy(wT9[W9_AT:, :], g[W9_AT:W9_AT + NE + 1, :]).then_inc(wT_ready, 1)

            for name, q in order:
                piece(name, q)
            act.wait_ge(flag_ready, 1)
            with act.If(act.value_load(flag[:, :]) == 0):
                for name, q in unmasked:
                    piece(name, q)

        @block.vector
        def _(vec):
            vec.wait_ge(c_in, 16)
            vec.wait_ge(cth_ready, 1)
            vec.tensor_scalar(c_h[:, :], c_th[:, :], 1.0, None, ALU.add).then_inc(ch_ready, 1)
            vec.wait_ge(ch_ready, 1)
            vec.reciprocal(c_th[:, :], c_h[:, :]).then_inc(csig_ready, 1)
            vec.wait_ge(csig_ready, 1)
            vec.tensor_tensor(c_s[:, :], c_th[:, :], c_sb[:, :], ALU.mult).then_inc(cs_ready, 1)
            vec.wait_ge(small_in, 16)
            vec.tensor_scalar(taps[:, :, :], conv_w, 0.5, None, ALU.mult).then_inc(taps_ready, 1)
            vec.wait_ge(Ae_ready, 1)
            vec.tensor_scalar(A[:, :, :], Ae[:, :, :], -1.0, None, ALU.mult).then_inc(A_ready, 1)

            def dbx(s):
                q = s // NS
                vec.wait_ge(B_in[s % NBR], 16 * (s // NBR + 1))
                vec.wait_ge(dx_ready, NH * (q + 1))
                if s >= NX:
                    vec.wait_ge(scan_done, s - NX + 1)
                vec.tensor_tensor(dBx[:, s % NX], dx[:, q % 2], B_sb[:, s % NBR].unsqueeze(1).to_broadcast([P, NH, T]),
                                  ALU.mult).then_inc(dBx_ready, 1)

            def stats_of(which, q, src):
                if q > 0:
                    vec.wait_ge(bn_ready[which], NT * q)
                    vec.wait_ge(stats_ready[which], NT * q)
                for j in range(NT):
                    vec.bn_stats(stats[:, which, j], src[:, q, j]).then_inc(bn_ready[which], 1)
                if q > 0:
                    vec.wait_ge(rstd_ready[which], q)
                    vec.wait_ge(xn_ready[which], NT * q)
                for j in range(NT):
                    vec.wait_ge(bn_ready[which], NT * q + j + 1)
                    vec.bn_aggr(mv[:, which, j], stats[:, which, j]).then_inc(stats_ready[which], 1)

            def shift_of(which, q):
                vec.wait_ge(rstd_ready[which], q + 1)
                vec.wait_ge(stats_ready[which], NT * (q + 1))
                if q > 0:
                    vec.wait_ge(xn_ready[which], NT * q)
                vec.scalar_tensor_tensor(shift[:, which], mv[:, which, :, 0], -1.0, rstd[:, which], ALU.mult, ALU.mult
                                         ).then_inc(shift_ready[which], 1)

            def piece(name, q):
                if name == "first":
                    for s in range(IN_AHEAD):
                        dbx(s)
                elif name == "scan":
                    s = q
                    if s + IN_AHEAD <= last_s:
                        dbx(s + IN_AHEAD)
                    vec.wait_ge(dA_ready, s + 1)
                    vec.wait_ge(dBx_ready, s + 1)
                    if s >= NHB:
                        vec.wait_ge(prod_ready, s - NHB + 1)
                    vec.tensor_tensor_scan(hs[:, s % NHB].rearrange("p h t -> p (h t)"),
                                           dA[:, s % ND].rearrange("p h t -> p (h t)"),
                                           dBx[:, s % NX].rearrange("p h t -> p (h t)"), 0.0,
                                           ALU.mult, ALU.add).then_inc(scan_done, 1)
                    if s >= SHARED_FROM:
                        vec.wait_ge(scan_done, s + 1)
                        vec.wait_ge(C_in[s % NC], 16 * (s // NC + 1))
                        vec.wait_ge(nsum_done, s - NPB + 1)
                        vec.tensor_tensor(prod[:, s % NPB, 1], hs[:, s % NHB, 1], C_sb[:, s % NC],
                                          ALU.mult).then_inc(prod_rest_ready, 1)
                elif name == "vec_ln1":
                    vec.wait_ge(x_in[q], 16)
                    stats_of(0, q, x_sb)
                elif name == "vec_shift1":
                    shift_of(0, q)
                elif name == "vec_shift2" and q < NB - 1:
                    shift_of(1, q)
                elif name == "norm2" and q == NB - 1:
                    vec.wait_ge(rstd_ready[1], q + 1)
                    vec.wait_ge(stats_ready[1], NT * (q + 1))
                    vec.wait_ge(xT2_done, q)
                    for j in range(NT):
                        vec.tensor_scalar(xn[:, 1, j], x_sb[:, q, j], mv[:, 1, j, 0:1], rstd[:, 1, j:j + 1],
                                          ALU.subtract, ALU.mult).then_inc(xn_ready[1], 1)
                elif name in ("vec_c0", "vec_c1"):
                    h = int(name[-1])
                    k = 2 * q + h
                    g = G[banks[("pe_x%d" % h, q)][0][0]]
                    vec.wait_ge(xin_ready, k + 1)
                    for i in range(1, KC):
                        if k > 0 or i > 1:
                            vec.wait_ge(tap_done, 2 * k + i - 1)
                        vec.scalar_tensor_tensor(xch[:, h, i:], g[:, :T - i], taps[:, h, KC - 1 - i:KC - i],
                                                 xch[:, h, i:], ALU.mult, ALU.add
                                                 ).then_inc(tap_done if i < KC - 1 else conv_done, 1)
                elif name in ("vec_x0", "vec_x1"):
                    h = int(name[-1])
                    k = 2 * q + h
                    vec.wait_ge(xth_ready, k + 1)
                    if q >= 2:
                        vec.wait_ge(y_ready, 2 * (q - 1))
                        vec.wait_ge(dx_ready, NH * (q - 1))
                    vec.scalar_tensor_tensor(xconv[:, q % 2, h], th[:, h], 1.0, xch[:, h], ALU.add,
                                             ALU.mult).then_inc(xconv_ready, 1)
                elif name in ("vec_z0", "vec_z1"):
                    h = int(name[-1])
                    k = 2 * q + h
                    g = banks[("pe_" + name[4:], q)]
                    vec.wait_ge(zth_ready, k + 1)
                    if q >= 2:
                        vec.wait_ge(yg_ready, NH * (q - 1))
                    vec.scalar_tensor_tensor(zz[:, q % 2, h], th[:, h], 1.0, G[g[0][0]][:, :], ALU.add,
                                             ALU.mult).then_inc(zgate_ready, 1)
                elif name in ("vec_soft0", "vec_soft1"):
                    h = int(name[-1])
                    k = NH * q + h
                    if q == 0:
                        vec.wait_ge(dexp_ready, k + 1)
                        vec.tensor_scalar(dw1[:, h], dexp[:, h], 1.0, None, ALU.add).then_inc(dw1_ready, 1)
                    vec.wait_ge(dw1_ready, k + 1)
                    vec.scalar_tensor_tensor(dw1[:, h], dw1[:, h], -1.0, dexp[:, h], ALU.add, ALU.subtract
                                             ).then_inc(dcor_ready, 1)
                elif name[:-1] == "soft_sum" and q == 0:
                    soft_sum(vec, q, int(name[-1]))
                elif name[:-1] == "soft_add" and q == 0:
                    soft_add(vec, q, int(name[-1]))
                elif name[:-1] == "delta_x" and q == 0:
                    delta_x(vec, q, int(name[-1]))
                elif name == "vec_gates":
                    for i in range(2):
                        b = banks[(f"pe_gate{i}", 0)][0][0]
                        vec.wait_ge(gate_done, i + 1)
                        if i > 0:
                            vec.wait_ge(gates_ready, i)
                        vec.tensor_copy(graw[:, :], G[b][:, :]).then_inc(gates_read, 1)
                        vec.wait_ge(gates_read, i + 1)
                        vec.tensor_scalar(gsgn, graw[:, :], 0.0, 2.0, ALU.is_ge, ALU.mult).then_inc(gsgn_twice, 1)
                        vec.wait_ge(gsgn_twice, i + 1)
                        vec.tensor_scalar(gsgn, gsgn, -1.0, None, ALU.add).then_inc(gsgn_ready, 1)
                        vec.wait_ge(gsgn_ready, i + 1)
                        vec.tensor_tensor(graw[:, :], gsgn, graw[:, :], ALU.mult).then_inc(gabs_ready, 1)
                        vec.wait_ge(gabs_ready, i + 1)
                        vec.scalar_tensor_tensor(gate[:, 2 * i:2 * i + 2].rearrange("p b k o -> p (b k o)"), graw[:, :], 0.25,
                                                 gsgn, ALU.max, ALU.mult).then_inc(gates_ready, 1)
                elif name == "vec_V":
                    for i in range(2):
                        b = banks[(f"pe_V{i}", 0)][0][0]
                        vec.wait_ge(V_done, i + 1)
                        vec.tensor_tensor(M[:, 4 * i:4 * i + 4], ident[:, :].unsqueeze(1).to_broadcast([P, 4, P]),
                                          G[b][:, :].rearrange("p (e i) -> p e i", e=4), ALU.subtract
                                          ).then_inc(M_ready, 1)
                elif name in ("vec_y0", "vec_y1"):
                    h = int(name[-1])
                    vec.wait_ge(nsum_done, NS * (q + 1))
                    if q > 0:
                        vec.wait_ge(wout_done, q)
                    vec.scalar_tensor_tensor(y2[:, h], xconv[:, q % 2, h], Dsk[:, h:h + 1], Yps[:, h], ALU.mult,
                                             ALU.add).then_inc(y_ready, 1)
                elif name in ("gate_z0", "gate_z1") and q == NB - 1:
                    gate_z(vec, q, int(name[-1]))
                elif name == "vec_x2":
                    g = banks[("pe_wout", q)]
                    vec.wait_ge(wout_done, q + 1)
                    vec.tensor_tensor(x_sb[:, q], G[g[0][0]][:, :].rearrange("p (j o) -> p j o", j=NT), x_sb[:, q],
                                      ALU.add).then_inc(x2_ready, 1)
                    vec.wait_ge(x2_ready, q + 1)
                    stats_of(1, q, x_sb)
                elif name[:5] == "sq_rb" and q == NB - 1 and name != SQ_LAST:
                    j = int(name[-1])
                    k = NT * q + j
                    g = G[banks[(f"pe_rb{j}", q)][0][0]]
                    vec.wait_ge(rb_done, k + 1)
                    vec.wait_ge(wout_done, NB)
                    if j >= 2:
                        vec.wait_ge(sqb_done, k - 1)
                    vec.tensor_copy(y2[:, j % 2], g[:, :]).then_inc(resid_copied, 1)
                    vec.wait_ge(resid_copied, j + 1)
                    for e in range(NE // 2):
                        vec.scalar_tensor_tensor(g[:, e * P:(e + 1) * P], y2[:, j % 2, e * P:(e + 1) * P], 1.0,
                                                 g[:, e * P:(e + 1) * P], ALU.mult, ALU.mult,
                                                 accum_out=r2[:, q, j, NE // 2 + e:NE // 2 + e + 1]
                                                 ).then_inc(sqb_some if e < NE // 2 - 1 else sqb_done, 1)
                elif name == "vec_clamp":
                    vec.wait_ge(sqa_done, NT * (q + 1))
                    vec.wait_ge(sqb_done, NT * (q + 1))
                    if q > 0:
                        vec.wait_ge(lr_ready, q)
                    vec.tensor_scalar(r2c[:, :, :], r2[:, q], 1e-18, None, ALU.max).then_inc(clamp_ready, 1)
                elif name == "vec_gate1":
                    vec.wait_ge(res_ready, q + 1)
                    if q > 0:
                        vec.wait_ge(gd_ready, q)
                    vec.tensor_reduce(rmin[:, :], res[:, :, :], AX, ALU.min).then_inc(rmin_ready, 1)
                    vec.wait_ge(rmin_ready, q + 1)
                    if q > 0:
                        vec.wait_ge(ge_ready, q)
                    vec.tensor_tensor(gd[:, :, :], rmin[:, :].unsqueeze(2).to_broadcast([P, NT, NE]), res[:, :, :],
                                      ALU.subtract).then_inc(gd_ready, 1)
                elif name == "vec_ranka":
                    ve = r2[:, q].unsqueeze(3).to_broadcast([P, NT, NE, NE])
                    vf = r2[:, q].unsqueeze(2).to_broadcast([P, NT, NE, NE])
                    vec.wait_ge(sqa_done, NT * (q + 1))
                    vec.wait_ge(sqb_done, NT * (q + 1))
                    if q > 0:
                        vec.wait_ge(rank_ready, q)
                        vec.wait_ge(cnt_ready, q)
                    vec.tensor_tensor(lt[:, :, :, :], vf, ve, ALU.is_lt).then_inc(lt_ready, 1)
                    vec.tensor_tensor(eq[:, :, :, :], vf, ve, ALU.is_equal).then_inc(eq_ready, 1)
                    vec.wait_ge(eq_ready, q + 1)
                    vec.tensor_tensor(eq[:, :, :, :].rearrange("p j e f -> p j (e f)"),
                                       eq[:, :, :, :].rearrange("p j e f -> p j (e f)"),
                                       tri[:, :, :].rearrange("p e f -> p (e f)").unsqueeze(1).to_broadcast([P, NT, NE * NE]),
                                       ALU.mult).then_inc(eql_ready, 1)
                elif name == "vec_rankb":
                    vec.wait_ge(eql_ready, q + 1)
                    vec.wait_ge(lt_ready, q + 1)
                    vec.tensor_tensor(lt[:, :, :, :], lt[:, :, :, :], eq[:, :, :, :], ALU.add).then_inc(cnt_ready, 1)
                    vec.wait_ge(cnt_ready, q + 1)
                    if q > 0:
                        vec.wait_ge(keep_ready, q)
                    vec.tensor_reduce(rank[:, q], lt[:, :, :, :], AX, ALU.add).then_inc(rank_ready, 1)
                elif name == "vec_gate2":
                    vec.wait_ge(ge_ready, q + 1)
                    if q > 0:
                        vec.wait_ge(w_ready, q)
                    vec.tensor_reduce(gs[:, :], ge[:, :, :], AX, ALU.add).then_inc(gs_ready, 1)
                    vec.wait_ge(gs_ready, q + 1)
                    vec.reciprocal(gr[:, :], gs[:, :]).then_inc(gr_ready, 1)
                    vec.wait_ge(gr_ready, q + 1)
                    vec.tensor_tensor(rw[:, :, :], ge[:, :, :], gr[:, :].unsqueeze(2).to_broadcast([P, NT, NE]),
                                      ALU.mult).then_inc(rw_ready, 1)
                    vec.wait_ge(rw_ready, q + 1)
                    vec.tensor_scalar(msk[:, q], rw[:, :, :], 1.0 / NE, None, ALU.is_gt).then_inc(msk_ready, 1)
                    vec.wait_ge(msk_ready, q + 1)
                    vec.wait_ge(rank_ready, q + 1)
                    vec.scalar_tensor_tensor(keep[:, :, :], rank[:, q], 2.0, msk[:, q], ALU.is_lt,
                                             ALU.mult).then_inc(keep_ready, 1)
                    vec.wait_ge(keep_ready, q + 1)
                    vec.tensor_tensor(fw[:, :, :], rw[:, :, :], keep[:, :, :], ALU.mult).then_inc(fw_ready, 1)
                    vec.wait_ge(fw_ready, q + 1)
                    vec.tensor_reduce(sw[:, :], fw[:, :, :], AX, ALU.add).then_inc(sw_ready, 1)
                    vec.wait_ge(sw_ready, q + 1)
                    vec.scalar_tensor_tensor(swz[:, :], sw[:, :], 0.0, sw[:, :], ALU.is_equal, ALU.add).then_inc(swz_ready, 1)
                    vec.wait_ge(swz_ready, q + 1)
                    vec.reciprocal(rsw[:, :], swz[:, :]).then_inc(rsw_ready, 1)
                    vec.wait_ge(rsw_ready, q + 1)
                    vec.wait_ge(w41_one, 1)
                    if q > 0:
                        vec.wait_ge(wT_done, q)
                    w = w41[:, :, W9_AT:W9_AT + NE]
                    vec.tensor_tensor(w, fw[:, :, :], rsw[:, :].unsqueeze(2).to_broadcast([P, NT, NE]),
                                      ALU.mult).then_inc(w_ready, 1)
                elif name == "split_w" and q == NB - 1:
                    split_w(vec, q)
                elif name == "vec_any":
                    vec.wait_ge(msk_ready, NB)
                    vec.tensor_reduce(passing[:, :], msk[:, :, :, :].rearrange("p b j e -> p (b j e)"), AX, ALU.max
                                      ).then_inc(passing_ready, 1)
                elif name == "vec_flag":
                    vec.wait_ge(any_done, 1)
                    vec.tensor_copy(flag[:, :], Yps[0:1, 0, 0:1]).then_inc(flag_ready, 1)
                elif name == "vec_top":
                    vec.wait_ge(wT_done, q)
                    vec.wait_ge(rank_ready, NB)
                    vec.tensor_scalar(w41[:, :, 0:NE], rank[:, q % NB], 1.0, None, ALU.is_lt).then_inc(w_part0, 1)
                    vec.memset(w41[:, :, NE:NP3 * NE], 0.0).then_inc(w_part1, 1)
                    vec.tensor_scalar(w41[:, :, W9_AT:W9_AT + NE], rank[:, q % NB], 1.0, None, ALU.is_lt
                                      ).then_inc(w_parts_ready, 1)
                elif name[:5] == "vec_h":
                    e = int(name[-1])
                    k = NE * q + e
                    bank = banks[(f"pe_b{e}", q)][0][0]
                    vec.wait_ge(b_done, k + 1)
                    if k >= NW:
                        vec.wait_ge(a_done, k - NW + 1)
                    vec.tensor_tensor(wh[:, (NE * q + e) % NW], h2T[:, q % NB], G[bank][:, :], ALU.mult).then_inc(wh_ready, 1)
                elif name == "add_out" and q == NB - 1:
                    vec.wait_ge(acc_ready, q + 1)
                    vec.tensor_tensor(x_sb[:, q], acc[:, :, :], x_sb[:, q], ALU.add).then_inc(out_ready, 1)
                elif name == "vec_out":
                    vec.wait_ge(a_done, NE * (q + 1))
                    if q > 0:
                        vec.wait_ge(out_ready, q)
                    else:
                        vec.wait_ge(gates_ready, 2)
                    vec.tensor_tensor(acc[:, :, :], Ops[:, :].rearrange("p (j o) -> p j o", j=NT),
                                      gate[:, q % NB, 1].unsqueeze(1).to_broadcast([P, NT, P]), ALU.mult
                                      ).then_inc(acc_ready, 1)

            for name, q in order:
                piece(name, q)
            vec.wait_ge(flag_ready, 1)
            with vec.If(vec.value_load(flag[:, :]) == 0):
                for name, q in unmasked:
                    piece(name, q)

        @block.tensor
        def _(pe):
            def shared(name, q, i=0):
                bank, before = banks[(name, q)][i]
                if before is not None:
                    pe.wait_ge(*before)
                return G[bank]

            def nsum(s):
                q, n = divmod(s, NS)
                pe.wait_ge(prod_ready, s + 1)
                if s >= SHARED_FROM:
                    pe.wait_ge(prod_rest_ready, s - SHARED_FROM + 1)
                if n == 0:
                    pe.wait_ge(mod_ready, 2)
                    if q > 0:
                        pe.wait_ge(y_ready, 2 * q)
                for h in range(NH):
                    mm = pe.matmul(Yps[:, h], ident[:, :], prod[:, s % NPB, h], start=(n == 0), stop=(n == NS - 1))
                mm.then_inc(nsum_done, 1)

            def stay_busy(count):
                for _ in range(count):
                    pe.matmul(spare[:, :], blank[:, 0:P], blank[:, :], start=True, stop=True)

            pe.wait_ge(wm_in, 16)
            pe.wait_ge(cs_ready, 1)
            for i, k in enumerate((0, 1, 3, 4)):
                mm = pe.matmul(Yps[:, 0, NB * i:NB * i + NB], wm[:, k], c_s[:, :], start=True, stop=True)
            mm.then_inc(mod_done, 1)
            pe.wait_ge(ident_in, 16)

            def piece(name, q):
                if name == "scan":
                    if q >= BEHIND:
                        nsum(q - BEHIND)
                elif name == "last":
                    pe.wait_ge(blank_ready, 1)
                    for s in range(last_s - BEHIND + 1, last_s + 1):
                        nsum(s)
                elif name == "pe_busy":
                    stay_busy(q)
                elif name == "pe_xT":
                    g = shared(name, q)
                    for j in range(NT):
                        pe.wait_ge(xn_ready[0], NT * q + j + 1)
                        mm = pe.transpose(g[:, j * P:(j + 1) * P], xn[:, 0, j], ident[:, :])
                    mm.then_inc(xT_done, 1)
                elif name == "pe_xT2":
                    g = shared(name, q)
                    for j in range(NT):
                        pe.wait_ge(xn_ready[1], NT * q + j + 1)
                        mm = pe.transpose(g[:, j * P:(j + 1) * P], xn[:, 1, j], ident[:, :])
                    mm.then_inc(xT2_done, 1)
                elif name in ("pe_x0", "pe_x1"):
                    h = int(name[-1])
                    g = shared(name, q)
                    pe.wait_ge(hT_ready, q + 1)
                    pe.wait_ge(win_in, 16)
                    pe.matmul(g[:, :], Win[:, h * P:(h + 1) * P], hT[:, q % 2], start=True, stop=True).then_inc(x_done, 1)
                elif name in ("pe_z0", "pe_z1"):
                    h = int(name[-1])
                    g = shared(name, q)
                    pe.matmul(g[:, :], Win[:, DI + h * P:DI + (h + 1) * P], hT[:, q % 2], start=True, stop=True
                              ).then_inc(z_done, 1)
                elif name == "pe_ssm":
                    g = shared(name, q)
                    pe.wait_ge(wx_in, 16)
                    pe.wait_ge(xconv_ready, 2 * (q + 1))
                    for h in range(NH):
                        mm = pe.matmul(g[0:NR, :], Wx[:, h], xconv[:, q % 2, h], start=(h == 0), stop=(h == NH - 1))
                    mm.then_inc(ssm_done, 1)
                elif name in ("pe_gate0", "pe_gate1"):
                    i = int(name[-1])
                    g = shared(name, q)
                    for b in range(2):
                        for k in range(2):
                            at = (2 * b + k) * P
                            mm = pe.matmul(g[:, at:at + P], c_s[:, 2 * i + b:2 * i + b + 1].to_broadcast([P, P]), wm[:, 2 + 3 * k], start=True, stop=True)
                    mm.then_inc(gate_done, 1)
                elif name in ("pe_V0", "pe_V1"):
                    i = int(name[-1])
                    g = shared(name, q)
                    pe.wait_ge(v_in, 16)
                    for e in range(4):
                        mm = pe.matmul(g[:, e * P:(e + 1) * P], V[:, 4 * i + e], V[:, 4 * i + e], start=True, stop=True)
                    mm.then_inc(V_done, 1)
                elif name == "pe_wout":
                    g = shared(name, q)
                    pe.wait_ge(yg_ready, NH * (q + 1))
                    pe.wait_ge(Wog_ready, NB)
                    for j in range(NT):
                        for h in range(NH):
                            mm = pe.matmul(g[:, j * P:(j + 1) * P], y2[:, h, j * P:(j + 1) * P], Wog[:, q, h],
                                           start=(h == 0), stop=(h == NH - 1))
                    mm.then_inc(wout_done, 1)
                elif name[:5] in ("pe_ra", "pe_rb"):
                    j = int(name[-1])
                    i = "ab".index(name[4])
                    g = shared(name, q)
                    if j == 0:
                        pe.wait_ge(h2T_ready, q + 1)
                        pe.wait_ge(M_ready, 2)
                    pe.matmul(g[:, :], h2T[:, q, j * P:(j + 1) * P], M[:, 4 * i:4 * i + 4].rearrange("p e i -> p (e i)"),
                              start=True, stop=True).then_inc(ra_done if i == 0 else rb_done, 1)
                elif name == "pe_wT":
                    g = shared(name, q)
                    pe.wait_ge(w_parts_ready, q + 1)
                    pe.wait_ge(w_part0, q + 1)
                    pe.wait_ge(w_part1, q + 1)
                    for j in range(NT):
                        mm = pe.transpose(g[0:W9_AT + NE + 1, j * P:(j + 1) * P], w41[:, j], ident[:, :])
                    mm.then_inc(wT_done, 1)
                elif name == "pe_o":
                    pe.wait_ge(w9_in, 16)
                    pe.wait_ge(h2T_ready, q + 1)
                    if q > 0:
                        pe.wait_ge(acc_ready, q)
                    for j in range(NT):
                        pe.matmul(Ops[:, j * P:(j + 1) * P], h2T[:, q, j * P:(j + 1) * P], W9[:, NE * P:],
                                  start=(j == 0), stop=False, skip_group_check=True)
                elif name == "pe_bias":
                    pe.wait_ge(b9_in, 16)
                    pe.wait_ge(wT_ready, q + 1)
                    if q >= NB:
                        pe.wait_ge(acc_ready, q)
                    rows = slice(W9_AT, W9_AT + NE + (q < NB))
                    for j in range(NT):
                        mm = pe.matmul(Ops[:, j * P:(j + 1) * P], wT9[rows, j * P:(j + 1) * P], b9[rows, :],
                                       start=(q >= NB and j == 0), stop=False, skip_group_check=True)
                    mm.then_inc(bias_done, 1)
                elif name == "pe_any":
                    pe.wait_ge(passing_ready, 1)
                    pe.wait_ge(w41_one, 1)
                    pe.wait_ge(y_ready, NH * NB)
                    pe.matmul(Yps[0:1, 0, 0:1], passing[:, :], w41[:, 0, W9_AT + NE:], start=True, stop=True
                              ).then_inc(any_done, 1)
                elif name[:4] == "pe_b":
                    e = int(name[-1])
                    g = shared(name, q)
                    pe.wait_ge(wTp_ready, q + 1)
                    pe.wait_ge(sel_ready, 1)
                    pe.matmul(g[:, :], selE[0:NP3 * NE, e:e + 1].to_broadcast([NP3 * NE, P]), wTp[:, :], start=True,
                              stop=True).then_inc(b_done, 1)
                elif name[:4] == "pe_a":
                    e = int(name[-1])
                    pe.wait_ge(wh_ready, NE * q + e + 1)
                    for j in range(NT):
                        mm = pe.matmul(Ops[:, j * P:(j + 1) * P], wh[:, (NE * q + e) % NW, j * P:(j + 1) * P], W9[:, e * P:(e + 1) * P],
                                       start=False, stop=(e == NE - 1), skip_group_check=True)
                    mm.then_inc(a_done, 1)

            for name, q in order:
                piece(name, q)
            pe.wait_ge(flag_ready, 1)
            with pe.If(pe.value_load(flag[:, :]) == 0):
                for name, q in unmasked:
                    piece(name, q)


def kernel(L0_attn_x, L0_attn_W_in, L0_attn_conv_w, L0_attn_conv_b, L0_attn_W_x, L0_attn_dt_w, L0_attn_dt_b,
           L0_attn_A_log, L0_attn_D, L0_attn_W_out, L0_ffn_Wp, L0_ffn_bp, L0_ffn_We, L0_ffn_be, L0_ffn_Vg, L0_c, L0_wmod):
    import concourse.bacc as _bacc
    from concourse.bass_utils import run_bass_kernel_spmd as _run

    def halves(a):
        return a.reshape(NH, P).T

    selE = np.zeros((P, NE), np.float32)
    for p in range(NP3 * NE):
        selE[p, p % NE] = 1.0
    tri = np.broadcast_to(np.tril(np.ones((NE, NE), np.float32), -1), (P, NE, NE))
    small = {
        "conv_b": halves(np.asarray(L0_attn_conv_b)), "dt_w": halves(np.asarray(L0_attn_dt_w)),
        "dt_b": halves(np.asarray(L0_attn_dt_b)), "D": halves(np.asarray(L0_attn_D)),
        "A_log": np.asarray(L0_attn_A_log).reshape(NH, P, NS).transpose(1, 0, 2).reshape(P, NH * NS),
        "conv_w": np.asarray(L0_attn_conv_w).reshape(NH, P, KC).transpose(1, 0, 2).reshape(P, NH * KC),
        "selE": selE, "eps": np.full((P, 1), EPS, np.float32), "tri": tri.reshape(P, NE * NE),
    }
    W_o = np.asarray(L0_attn_W_out).reshape(NH, P, P).transpose(1, 0, 2)
    W9 = np.concatenate([np.asarray(L0_ffn_We), np.asarray(L0_ffn_Wp)[None]]).transpose(2, 0, 1).reshape(P, (NE + 1) * P)
    b9 = np.concatenate([np.asarray(L0_ffn_be), np.asarray(L0_ffn_bp)[None]])
    arrays = {
        "x": L0_attn_x, "W_in": L0_attn_W_in,
        "small": np.concatenate([small[k] for k in SMALL], axis=1),
        "W_x": np.asarray(L0_attn_W_x).reshape(NH, P, NR).transpose(1, 0, 2),
        "W_out": W_o,
        "W9": W9, "b9": b9, "VgT": np.asarray(L0_ffn_Vg).transpose(2, 0, 1),
        "cT": np.asarray(L0_c).T, "wmod": L0_wmod, "ident": np.eye(P, dtype=np.float32),
    }
    nc = _bacc.Bacc("TRN2", target_bir_lowering=False, num_devices=1)
    ins, args = {}, []
    for name, a in arrays.items():
        a = np.ascontiguousarray(a)
        ins["in_" + name] = a
        args.append(nc.dram_tensor("in_" + name, a.shape, mybir.dt.from_np(a.dtype), kind="ExternalInput").ap())
    out = nc.dram_tensor("out", (NB, T, P), F32, kind="ExternalOutput").ap()
    rows_dram = nc.dram_tensor("rows_dram", (NB, NR, T), F32, kind="Internal").ap()
    adaln_mamba_experts(nc, *args, rows_dram, out)
    return _run(nc, [ins], core_ids=[0]).results[0]["out"]
```
